# Optimizing a Trainium2 kernel written in Bass

```python
import numpy as np
import jax
import jax.numpy as jnp

def _softmax(x, axis=-1):
    return jax.nn.softmax(x, axis=axis)

def _gelu(x):
    return jax.nn.gelu(x, approximate=True)

def _silu(x):
    return jax.nn.silu(x)

def _sigmoid(x):
    return jax.nn.sigmoid(x)

def _layernorm(x, axis=-1, eps=1e-05):
    m = jnp.mean(x, axis=axis, keepdims=True)
    v = jnp.var(x, axis=axis, keepdims=True)
    return (x - m) / jnp.sqrt(v + eps)

def _scatter_add(tgt, idx, src, axis=0):
    return tgt.at[idx].add(src)

def _segment_sum(src, seg, n):
    return jax.ops.segment_sum(src, seg, n)
kernel_name = 'mk_lm_tower_d1_tok_ids768_r4_e16afc'

def setup_inputs(seed: int=0):
    np.random.seed(seed)
    _w = jnp.asarray

    def _rec_inputs():
        import jax
        import jax.numpy as jnp
        _rk = jax.random.key(seed)
        x = jax.random.randint(jax.random.fold_in(_rk, 1), (8, 256), 0, 40470, jnp.int32)
        pos_S = jnp.broadcast_to(jnp.arange(256, dtype=jnp.int32), (256,))
        mask_BS_f1_0 = jnp.where(jnp.ones((8, 256), dtype=bool), 1.0, 0.0).astype(jnp.float32)
        return (x, pos_S, mask_BS_f1_0)
    x, pos_S, mask_BS_f1_0 = _rec_inputs()

    def _L0_tok_setup():
        import jax, jax.numpy as jnp
        import numpy as np
        N_LAYER, D, H, V, S_MAX = (5, 192, 12, 40478, 256)
        HD = D // H
        GELU_C = float(np.sqrt(2.0 / np.pi))

        def gelu(x):
            return 0.5 * x * (1.0 + jnp.tanh(GELU_C * (x + 0.044715 * x ** 3)))

        def layernorm(x, w, b, eps=1e-05):
            mu = jnp.mean(x, axis=-1, keepdims=True)
            var = jnp.mean((x - mu) ** 2, axis=-1, keepdims=True)
            return (x - mu) * jax.lax.rsqrt(var + eps) * w + b

        def forward(input_ids, position_ids, attention_mask, tok_emb, pos_emb, c_attn_w, c_attn_b, c_proj_w, c_proj_b, ln1_w, ln1_b, c_fc_w, c_fc_b, mlp_proj_w, mlp_proj_b, ln2_w, ln2_b):
            B, S = input_ids.shape
            h = tok_emb[input_ids] + pos_emb[position_ids][None]
            ext_mask = (1.0 - attention_mask)[:, None, None, :] * jnp.finfo(h.dtype).min
            causal = jnp.tril(jnp.ones((S, S), dtype=h.dtype))
            scale = 1.0 / jnp.sqrt(jnp.asarray(HD, h.dtype))
            for i in range(N_LAYER):
                qkv = h @ c_attn_w[i] + c_attn_b[i]
                q, k, v = jnp.split(qkv, 3, axis=-1)
                q = q.reshape(B, S, H, HD).transpose(0, 2, 1, 3)
                k = k.reshape(B, S, H, HD).transpose(0, 2, 1, 3)
                v = v.reshape(B, S, H, HD).transpose(0, 2, 1, 3)
                w = jnp.einsum('bhqd,bhkd->bhqk', q, k) * scale
                w = w * causal + -10000.0 * (1.0 - causal)
                w = w + ext_mask
                p = jax.nn.softmax(w, axis=-1)
                a = jnp.einsum('bhqk,bhkd->bhqd', p, v)
                a = a.transpose(0, 2, 1, 3).reshape(B, S, D)
                a = a @ c_proj_w[i] + c_proj_b[i]
                n = layernorm(h + a, ln1_w[i], ln1_b[i])
                m = gelu(n @ c_fc_w[i] + c_fc_b[i]) @ mlp_proj_w[i] + mlp_proj_b[i]
                h = layernorm(n + m, ln2_w[i], ln2_b[i])
            return h
        key = jax.random.key(seed)
        ks = jax.random.split(key, 8)
        B, S = (4, 256)
        w = 0.02
        return {'input_ids': jax.random.randint(ks[0], (B, S), 0, V), 'position_ids': jnp.arange(S, dtype=jnp.int64), 'attention_mask': jnp.ones((B, S), dtype=jnp.float32), 'tok_emb': jax.random.normal(ks[1], (V, D), jnp.float32) * w, 'pos_emb': jax.random.normal(ks[2], (S_MAX, D), jnp.float32) * w, 'c_attn_w': jax.random.normal(ks[3], (N_LAYER, D, 3 * D), jnp.float32) * w, 'c_attn_b': jnp.zeros((N_LAYER, 3 * D), jnp.float32), 'c_proj_w': jax.random.normal(ks[4], (N_LAYER, D, D), jnp.float32) * w, 'c_proj_b': jnp.zeros((N_LAYER, D), jnp.float32), 'ln1_w': jnp.ones((N_LAYER, D), jnp.float32), 'ln1_b': jnp.zeros((N_LAYER, D), jnp.float32), 'c_fc_w': jax.random.normal(ks[5], (N_LAYER, D, 4 * D), jnp.float32) * w, 'c_fc_b': jnp.zeros((N_LAYER, 4 * D), jnp.float32), 'mlp_proj_w': jax.random.normal(ks[6], (N_LAYER, 4 * D, D), jnp.float32) * w, 'mlp_proj_b': jnp.zeros((N_LAYER, D), jnp.float32), 'ln2_w': jnp.ones((N_LAYER, D), jnp.float32), 'ln2_b': jnp.zeros((N_LAYER, D), jnp.float32)}
    _L0_tok_all = _L0_tok_setup()
    _L0_tok_in = {k: v for k, v in _L0_tok_all.items() if k in ('tok_emb', 'pos_emb', 'c_attn_w', 'c_attn_b', 'c_proj_w', 'c_proj_b', 'ln1_w', 'ln1_b', 'c_fc_w', 'c_fc_b', 'mlp_proj_w', 'mlp_proj_b', 'ln2_w', 'ln2_b')}
    del _L0_tok_all

    def _L0_attn_setup():
        import jax, jax.numpy as jnp
        import numpy as np
        import math
        D_MODEL, D_INNER, D_STATE, D_CONV, DT_RANK = (192, 384, 16, 4, 48)
        BATCH, SEQLEN = (2, 256)
        DT_MIN, DT_MAX = (0.0001, 1.0)

        def _forward(x, ln_w, ln_b, W_in, W_dt, conv_w, conv_b, A_log, Dskip, dt_bias, norm_w, W_res, W_out):
            B, L, _ = x.shape
            D, N = A_log.shape
            K = conv_w.shape[1]
            R = W_dt.shape[1]
            mu = x.mean(-1, keepdims=True)
            var = ((x - mu) ** 2).mean(-1, keepdims=True)
            xn = (x - mu) * jax.lax.rsqrt(var + 1e-05) * ln_w + ln_b
            p = jnp.einsum('bld,od->blo', xn, W_in)
            z = p[..., :D]
            u = p[..., D:2 * D]
            dth = p[..., 2 * D:2 * D + R]
            Bpar = p[..., 2 * D + R:2 * D + R + D * N].reshape(B, L, D, N)
            Cpar = p[..., 2 * D + R + D * N:].reshape(B, L, D, N)
            uc = jax.lax.conv_general_dilated(u.transpose(0, 2, 1), conv_w[:, None, :], (1,), [(K - 1, 0)], feature_group_count=D, dimension_numbers=('NCH', 'OIH', 'NCH'))
            u = (uc + conv_b[None, :, None]).transpose(0, 2, 1)
            dt = jnp.clip(jax.nn.softplus(jnp.einsum('blr,dr->bld', dth, W_dt) + dt_bias), DT_MIN, DT_MAX)
            A = -jnp.exp(A_log)
            dA = jnp.exp(dt[..., None] * A)
            dBu = (dt * u)[..., None] * Bpar

            def step(h, inp):
                dA_t, dBu_t, C_t = inp
                h = dA_t * h + dBu_t
                return (h, (C_t * h).sum(-1))
            h0 = jnp.zeros((B, D, N), x.dtype)
            _, ys = jax.lax.scan(step, h0, (dA.transpose(1, 0, 2, 3), dBu.transpose(1, 0, 2, 3), Cpar.transpose(1, 0, 2, 3)))
            y = ys.transpose(1, 0, 2) + u * Dskip
            res = jnp.einsum('blm,dm->bld', x, W_res)
            g = y * jax.nn.silu(z)
            g = g * jax.lax.rsqrt((g * g).mean(-1, keepdims=True) + 1e-06) * norm_w + res
            return jnp.einsum('bld,md->blm', g, W_out)
        key = jax.random.key(seed)
        ks = jax.random.split(key, 10)
        D, N, R, K = (D_INNER, D_STATE, DT_RANK, D_CONV)
        total_out = 2 * D + R + 2 * D * N

        def xavier(k, shape):
            fan_in, fan_out = (shape[1], shape[0])
            a = math.sqrt(6.0 / (fan_in + fan_out))
            return jax.random.uniform(k, shape, jnp.float32, -a, a)
        x = jax.random.normal(ks[0], (BATCH, SEQLEN, D_MODEL), jnp.float32)
        W_in = xavier(ks[1], (total_out, D_MODEL))
        W_dt = xavier(ks[2], (D, R))
        W_out = xavier(ks[3], (D_MODEL, D))
        W_res = xavier(ks[4], (D, D_MODEL))
        conv_w = jax.random.normal(ks[5], (D, K), jnp.float32) * (1.0 / math.sqrt(K))
        conv_b = jnp.zeros((D,), jnp.float32)
        A_log = jnp.broadcast_to(jnp.log(jnp.arange(1, N + 1, dtype=jnp.float32)), (D, N))
        Dskip = jnp.ones((D,), jnp.float32)
        dt = jnp.exp(jax.random.uniform(ks[6], (D,), jnp.float32) * (math.log(DT_MAX) - math.log(DT_MIN)) + math.log(DT_MIN))
        dt_bias = dt + jnp.log(-jnp.expm1(-dt))
        norm_w = jnp.ones((D,), jnp.float32)
        ln_w = jnp.ones((D_MODEL,), jnp.float32)
        ln_b = jnp.zeros((D_MODEL,), jnp.float32)
        return {'x': x, 'ln_w': ln_w, 'ln_b': ln_b, 'W_in': W_in, 'W_dt': W_dt, 'conv_w': conv_w, 'conv_b': conv_b, 'A_log': A_log, 'Dskip': Dskip, 'dt_bias': dt_bias, 'norm_w': norm_w, 'W_res': W_res, 'W_out': W_out}
    _L0_attn_all = _L0_attn_setup()
    _L0_attn_in = {k: v for k, v in _L0_attn_all.items() if k in ('ln_w', 'ln_b', 'W_in', 'W_dt', 'conv_w', 'conv_b', 'A_log', 'Dskip', 'dt_bias', 'norm_w', 'W_res', 'W_out')}
    del _L0_attn_all

    def _L0_ffn_setup():
        import jax, jax.numpy as jnp
        import numpy as np
        N_EXPERTS = 8
        TOP_K = 2
        key = jax.random.key(seed)
        ks = jax.random.split(key, 4)
        B, T, C = (8, 128, 192)
        H = 4 * C
        E = N_EXPERTS
        scale = 0.02
        x = jax.random.normal(ks[0], (B, T, C), dtype=jnp.float32)
        gate_w = jax.random.normal(ks[1], (E, C), dtype=jnp.float32) * scale
        gate_b = jnp.zeros((E,), dtype=jnp.float32)
        w1 = jax.random.normal(ks[2], (E, H, C), dtype=jnp.float32) * scale
        b1 = jnp.zeros((E, H), dtype=jnp.float32)
        w2 = jax.random.normal(ks[3], (E, C, H), dtype=jnp.float32) * scale
        b2 = jnp.zeros((E, C), dtype=jnp.float32)
        return {'x': x, 'gate_w': gate_w, 'gate_b': gate_b, 'w1': w1, 'b1': b1, 'w2': w2, 'b2': b2}
    _L0_ffn_all = _L0_ffn_setup()
    _L0_ffn_in = {k: v for k, v in _L0_ffn_all.items() if k in ('gate_w', 'gate_b', 'w1', 'b1', 'w2', 'b2')}
    del _L0_ffn_all
    return {'x': x, 'pos_S': pos_S, 'mask_BS_f1_0': mask_BS_f1_0, 'L0_tok_tok_emb': _L0_tok_in['tok_emb'], 'L0_tok_pos_emb': _L0_tok_in['pos_emb'], 'L0_tok_c_attn_w': _L0_tok_in['c_attn_w'], 'L0_tok_c_attn_b': _L0_tok_in['c_attn_b'], 'L0_tok_c_proj_w': _L0_tok_in['c_proj_w'], 'L0_tok_c_proj_b': _L0_tok_in['c_proj_b'], 'L0_tok_ln1_w': _L0_tok_in['ln1_w'], 'L0_tok_ln1_b': _L0_tok_in['ln1_b'], 'L0_tok_c_fc_w': _L0_tok_in['c_fc_w'], 'L0_tok_c_fc_b': _L0_tok_in['c_fc_b'], 'L0_tok_mlp_proj_w': _L0_tok_in['mlp_proj_w'], 'L0_tok_mlp_proj_b': _L0_tok_in['mlp_proj_b'], 'L0_tok_ln2_w': _L0_tok_in['ln2_w'], 'L0_tok_ln2_b': _L0_tok_in['ln2_b'], 'L0_attn_ln_w': _L0_attn_in['ln_w'], 'L0_attn_ln_b': _L0_attn_in['ln_b'], 'L0_attn_W_in': _L0_attn_in['W_in'], 'L0_attn_W_dt': _L0_attn_in['W_dt'], 'L0_attn_conv_w': _L0_attn_in['conv_w'], 'L0_attn_conv_b': _L0_attn_in['conv_b'], 'L0_attn_A_log': _L0_attn_in['A_log'], 'L0_attn_Dskip': _L0_attn_in['Dskip'], 'L0_attn_dt_bias': _L0_attn_in['dt_bias'], 'L0_attn_norm_w': _L0_attn_in['norm_w'], 'L0_attn_W_res': _L0_attn_in['W_res'], 'L0_attn_W_out': _L0_attn_in['W_out'], 'L0_ffn_gate_w': _L0_ffn_in['gate_w'], 'L0_ffn_gate_b': _L0_ffn_in['gate_b'], 'L0_ffn_w1': _L0_ffn_in['w1'], 'L0_ffn_b1': _L0_ffn_in['b1'], 'L0_ffn_w2': _L0_ffn_in['w2'], 'L0_ffn_b2': _L0_ffn_in['b2']}

def reference(x, pos_S, mask_BS_f1_0, L0_tok_tok_emb, L0_tok_pos_emb, L0_tok_c_attn_w, L0_tok_c_attn_b, L0_tok_c_proj_w, L0_tok_c_proj_b, L0_tok_ln1_w, L0_tok_ln1_b, L0_tok_c_fc_w, L0_tok_c_fc_b, L0_tok_mlp_proj_w, L0_tok_mlp_proj_b, L0_tok_ln2_w, L0_tok_ln2_b, L0_attn_ln_w, L0_attn_ln_b, L0_attn_W_in, L0_attn_W_dt, L0_attn_conv_w, L0_attn_conv_b, L0_attn_A_log, L0_attn_Dskip, L0_attn_dt_bias, L0_attn_norm_w, L0_attn_W_res, L0_attn_W_out, L0_ffn_gate_w, L0_ffn_gate_b, L0_ffn_w1, L0_ffn_b1, L0_ffn_w2, L0_ffn_b2):
    import jax
    import jax.numpy as jnp

    def _L0_tok_ref(input_ids, position_ids, attention_mask, tok_emb, pos_emb, c_attn_w, c_attn_b, c_proj_w, c_proj_b, ln1_w, ln1_b, c_fc_w, c_fc_b, mlp_proj_w, mlp_proj_b, ln2_w, ln2_b):
        import jax, jax.numpy as jnp
        import numpy as np
        N_LAYER, D, H, V, S_MAX = (5, 192, 12, 40478, 256)
        HD = D // H
        GELU_C = float(np.sqrt(2.0 / np.pi))

        def gelu(x):
            return 0.5 * x * (1.0 + jnp.tanh(GELU_C * (x + 0.044715 * x ** 3)))

        def layernorm(x, w, b, eps=1e-05):
            mu = jnp.mean(x, axis=-1, keepdims=True)
            var = jnp.mean((x - mu) ** 2, axis=-1, keepdims=True)
            return (x - mu) * jax.lax.rsqrt(var + eps) * w + b

        def forward(input_ids, position_ids, attention_mask, tok_emb, pos_emb, c_attn_w, c_attn_b, c_proj_w, c_proj_b, ln1_w, ln1_b, c_fc_w, c_fc_b, mlp_proj_w, mlp_proj_b, ln2_w, ln2_b):
            B, S = input_ids.shape
            h = tok_emb[input_ids] + pos_emb[position_ids][None]
            ext_mask = (1.0 - attention_mask)[:, None, None, :] * jnp.finfo(h.dtype).min
            causal = jnp.tril(jnp.ones((S, S), dtype=h.dtype))
            scale = 1.0 / jnp.sqrt(jnp.asarray(HD, h.dtype))
            for i in range(N_LAYER):
                qkv = h @ c_attn_w[i] + c_attn_b[i]
                q, k, v = jnp.split(qkv, 3, axis=-1)
                q = q.reshape(B, S, H, HD).transpose(0, 2, 1, 3)
                k = k.reshape(B, S, H, HD).transpose(0, 2, 1, 3)
                v = v.reshape(B, S, H, HD).transpose(0, 2, 1, 3)
                w = jnp.einsum('bhqd,bhkd->bhqk', q, k) * scale
                w = w * causal + -10000.0 * (1.0 - causal)
                w = w + ext_mask
                p = jax.nn.softmax(w, axis=-1)
                a = jnp.einsum('bhqk,bhkd->bhqd', p, v)
                a = a.transpose(0, 2, 1, 3).reshape(B, S, D)
                a = a @ c_proj_w[i] + c_proj_b[i]
                n = layernorm(h + a, ln1_w[i], ln1_b[i])
                m = gelu(n @ c_fc_w[i] + c_fc_b[i]) @ mlp_proj_w[i] + mlp_proj_b[i]
                h = layernorm(n + m, ln2_w[i], ln2_b[i])
            return h
        return forward(input_ids, position_ids, attention_mask, tok_emb, pos_emb, c_attn_w, c_attn_b, c_proj_w, c_proj_b, ln1_w, ln1_b, c_fc_w, c_fc_b, mlp_proj_w, mlp_proj_b, ln2_w, ln2_b)

    def _L0_attn_ref(x, ln_w, ln_b, W_in, W_dt, conv_w, conv_b, A_log, Dskip, dt_bias, norm_w, W_res, W_out):
        import jax, jax.numpy as jnp
        import numpy as np
        import math
        D_MODEL, D_INNER, D_STATE, D_CONV, DT_RANK = (192, 384, 16, 4, 48)
        BATCH, SEQLEN = (2, 256)
        DT_MIN, DT_MAX = (0.0001, 1.0)

        def _forward(x, ln_w, ln_b, W_in, W_dt, conv_w, conv_b, A_log, Dskip, dt_bias, norm_w, W_res, W_out):
            B, L, _ = x.shape
            D, N = A_log.shape
            K = conv_w.shape[1]
            R = W_dt.shape[1]
            mu = x.mean(-1, keepdims=True)
            var = ((x - mu) ** 2).mean(-1, keepdims=True)
            xn = (x - mu) * jax.lax.rsqrt(var + 1e-05) * ln_w + ln_b
            p = jnp.einsum('bld,od->blo', xn, W_in)
            z = p[..., :D]
            u = p[..., D:2 * D]
            dth = p[..., 2 * D:2 * D + R]
            Bpar = p[..., 2 * D + R:2 * D + R + D * N].reshape(B, L, D, N)
            Cpar = p[..., 2 * D + R + D * N:].reshape(B, L, D, N)
            uc = jax.lax.conv_general_dilated(u.transpose(0, 2, 1), conv_w[:, None, :], (1,), [(K - 1, 0)], feature_group_count=D, dimension_numbers=('NCH', 'OIH', 'NCH'))
            u = (uc + conv_b[None, :, None]).transpose(0, 2, 1)
            dt = jnp.clip(jax.nn.softplus(jnp.einsum('blr,dr->bld', dth, W_dt) + dt_bias), DT_MIN, DT_MAX)
            A = -jnp.exp(A_log)
            dA = jnp.exp(dt[..., None] * A)
            dBu = (dt * u)[..., None] * Bpar

            def step(h, inp):
                dA_t, dBu_t, C_t = inp
                h = dA_t * h + dBu_t
                return (h, (C_t * h).sum(-1))
            h0 = jnp.zeros((B, D, N), x.dtype)
            _, ys = jax.lax.scan(step, h0, (dA.transpose(1, 0, 2, 3), dBu.transpose(1, 0, 2, 3), Cpar.transpose(1, 0, 2, 3)))
            y = ys.transpose(1, 0, 2) + u * Dskip
            res = jnp.einsum('blm,dm->bld', x, W_res)
            g = y * jax.nn.silu(z)
            g = g * jax.lax.rsqrt((g * g).mean(-1, keepdims=True) + 1e-06) * norm_w + res
            return jnp.einsum('bld,md->blm', g, W_out)
        return _forward(x, ln_w, ln_b, W_in, W_dt, conv_w, conv_b, A_log, Dskip, dt_bias, norm_w, W_res, W_out)

    def _L0_ffn_ref(x, gate_w, gate_b, w1, b1, w2, b2):
        import jax, jax.numpy as jnp
        import numpy as np
        N_EXPERTS = 8
        TOP_K = 2
        B, T, C = x.shape
        E = gate_w.shape[0]
        xr = x.reshape(B * T, C)
        N = xr.shape[0]
        logits = xr @ gate_w.T + gate_b
        probs = jax.nn.softmax(logits, axis=-1)
        topv, topi = jax.lax.top_k(probs, TOP_K)
        topv = topv / jnp.sum(topv, axis=-1, keepdims=True)
        tok_w = jnp.zeros((N, E), dtype=xr.dtype).at[jnp.arange(N)[:, None], topi].add(topv)
        out = jnp.zeros((N, C), dtype=xr.dtype)
        for e in range(E):
            h = jax.nn.relu(xr @ w1[e].T + b1[e])
            y = h @ w2[e].T + b2[e]
            out = out + tok_w[:, e:e + 1] * y
        return out.reshape(B, T, C)
    h = _L0_tok_ref(x, pos_S, mask_BS_f1_0, L0_tok_tok_emb, L0_tok_pos_emb, L0_tok_c_attn_w, L0_tok_c_attn_b, L0_tok_c_proj_w, L0_tok_c_proj_b, L0_tok_ln1_w, L0_tok_ln1_b, L0_tok_c_fc_w, L0_tok_c_fc_b, L0_tok_mlp_proj_w, L0_tok_mlp_proj_b, L0_tok_ln2_w, L0_tok_ln2_b)
    h = h + _L0_attn_ref(_layernorm(h, axis=-1), L0_attn_ln_w, L0_attn_ln_b, L0_attn_W_in, L0_attn_W_dt, L0_attn_conv_w, L0_attn_conv_b, L0_attn_A_log, L0_attn_Dskip, L0_attn_dt_bias, L0_attn_norm_w, L0_attn_W_res, L0_attn_W_out)
    h = h + _L0_ffn_ref(_layernorm(h, axis=-1), L0_ffn_gate_w, L0_ffn_gate_b, L0_ffn_w1, L0_ffn_b1, L0_ffn_w2, L0_ffn_b2)
    return h

_drawn_inputs = setup_inputs


def setup_inputs(seed=0):
    import zlib

    import numpy as np

    out = dict(_drawn_inputs(seed))
    spreads = {'L0_tok_c_attn_b': (0.0, 0.1),
     'L0_tok_c_proj_b': (0.0, 0.1),
     'L0_tok_ln1_w': (1.0, 0.2),
     'L0_tok_ln1_b': (0.0, 0.1),
     'L0_tok_c_fc_b': (0.0, 0.1),
     'L0_tok_mlp_proj_b': (0.0, 0.1),
     'L0_tok_ln2_w': (1.0, 0.2),
     'L0_tok_ln2_b': (0.0, 0.1),
     'L0_attn_ln_w': (1.0, 0.2),
     'L0_attn_ln_b': (0.0, 0.1),
     'L0_attn_conv_b': (0.0, 0.1),
     'L0_attn_Dskip': (1.0, 0.2),
     'L0_attn_norm_w': (1.0, 0.2),
     'L0_ffn_gate_b': (0.0, 0.1),
     'L0_ffn_b1': (0.0, 0.594),
     'L0_ffn_b2': (0.0, 0.1)}
    factors = {'L0_attn_W_dt': 8.0, 'L0_attn_A_log': 5.639}
    for name, (base, spread) in spreads.items():
        noise = np.random.default_rng([zlib.crc32(name.encode()), seed]).standard_normal(out[name].shape)
        drawn = base * np.exp(spread * noise) if base else spread * noise
        out[name] = jnp.asarray(drawn.astype(out[name].dtype))
    for name, factor in factors.items():
        out[name] = (out[name] * factor).astype(out[name].dtype)
    return out
```

```python
from contextlib import ExitStack

import numpy as np

import concourse.bass as bass
from concourse import mybir

F32 = mybir.dt.float32
F32R = mybir.dt.float32r
BF16 = mybir.dt.bfloat16
I32 = mybir.dt.int32
ALU = mybir.AluOpType
ACT = mybir.ActivationFunctionType
AX = mybir.AxisListType.X

B, S, D = 8, 256, 192
P = 128
LAYERS, HEADS = 5, 12
HD = D // HEADS
HID = 4 * D
QB = S // P
PAIRS = B // 2
HC = HID // P
DI, NS, RANK, KCONV = 384, 16, 48, 4
DJ = DI // P
EXPERTS = 8
SLOT = 32
HSLOT = P // SLOT
HT = HEADS // HSLOT
KROWS = 6 * HD
CUT = 96
HPC = CUT // HD
NEG = -2.0 ** 100
NEG2 = -2.0 ** 110
EPS = 1e-5
GELU_A = 0.044715
GELU_C = float(np.sqrt(2.0 / np.pi))

WQ, WK, WV, WO, WFC = 0, D, 2 * D, 3 * D, 4 * D
WCOLS = 4 * D + HID
W2COLS = HC * D
PQ, PK, PV_, PL1W, PL1B, PL2W, PL2B, PFC = 0, 2, 4, 6, 8, 10, 12, 14
NPAR = PFC + HC
R_L1W, R_L1B, R_MB, R_L2W, R_L2B, R_PB = range(6)

Q_PARTS = (0, 0, 0, 1, 1, 2)
K_PARTS = (0, 1, 2, 0, 1, 0)


RSQRT_STEPS = 11


def hold(eng, tick):
    eng.sem_inc(tick, 1)


def rsqrt_steps(eng, done, base, var, out, v, t, eps=EPS):
    n = base

    def step(instruction):
        nonlocal n
        instruction.then_inc(done, 1)
        n = n + 1
        eng.wait_ge(done, n)

    step(eng.tensor_scalar(v, var, eps, None, ALU.add))
    step(eng.tensor_scalar(out.bitcast(I32), v.bitcast(I32), -0.5, float(0x5F3759DF), ALU.mult, ALU.add))
    for _ in range(3):
        step(eng.scalar_tensor_tensor(t, out, -0.5, out, ALU.mult, ALU.mult))
        step(eng.tensor_tensor(t, t, v, ALU.mult))
        step(eng.scalar_tensor_tensor(out, t, 1.5, out, ALU.add, ALU.mult))


def setup_phase(nc, io, t, layers):
    with ExitStack() as ctx:
        def sb(name, shape, dt=F32):
            return ctx.enter_context(nc.sbuf_tensor(name, shape, dt))

        def sem(name):
            return nc.alloc_semaphore(name)

        NB = B * QB
        idx, pidx = sb("idx", [P, NB], I32), sb("pidx", [P, QB], I32)
        tok, pos = sb("tok", [P, NB, D]), sb("pos", [P, QB, D])
        htok = sb("htok", [P, NB, 2 * P])
        pb0 = sb("pb0", [P, D])
        lrow = sb("lrow", [LAYERS, 6, D])
        mrow, mcol = sb("mrow", [P, B, S]), sb("mcol", [P, B * QB])
        tri = sb("tri", [P, 3 * P])
        low = sb("low", [P, 3 * P])
        m1 = sb("m1", [P, B, 3 * P])
        fut = sb("fut", [P, B, 3 * P])
        emax, eneg = sb("emax", [P, B * QB]), sb("eneg", [P, B * QB])
        wt = sb("wt", [P, B, 3 * P])
        ps = [ctx.enter_context(nc.psum_tensor(f"set_ps{i}", [P, 512], F32)) for i in range(4)]
        idx_in, pidx_in, pb_in, mask_in = sem("idx_in"), sem("pidx_in"), sem("pb_in"), sem("mask_in")
        tok_in, pos_in = sem("tok_in"), sem("pos_in")
        zeroed, consts = sem("zeroed"), sem("consts")
        added, dup = sem("added"), sem("dup")
        ext, m1_done, fut_done, e_done, en_done = sem("ext"), sem("m1_done"), sem("fut_done"), sem("e_done"), sem("en_done")
        w_done, w_t, wt_done, h_t, h_done = sem("w_done"), sem("w_t"), sem("wt_done"), sem("h_t"), sem("h_done")
        stored, row_in, row_add = sem("stored"), sem("row_in"), sem("row_add")
        block = ctx.enter_context(nc.Block())

        @block.sync
        def _(sp):
            sp.dma_start(idx[:, :], io["ids"]).then_inc(idx_in, 16)
            sp.dma_start(pidx[:, :], io["pos_ids"]).then_inc(pidx_in, 16)
            sp.dma_start(pb0[:, :], io["proj_b0"].partition_broadcast(P)).then_inc(pb_in, 16)
            sp.dma_start(lrow[:, :, :], io["rows"]).then_inc(row_in, 16)
            sp.dma_start(mrow[:, :, :], io["mask_rows"].partition_broadcast(P)).then_inc(mask_in, 16)
            sp.dma_start(mcol[:, :], io["mask_cols"]).then_inc(mask_in, 16)
            sp.wait_ge(m1_done, 2 * B)
            sp.dma_start(t["m1_dram"].rearrange("b p n -> p b n"), m1[:, :, :]).then_inc(stored, 16)
            sp.wait_ge(wt_done, B)
            sp.dma_start(t["wt_dram"].rearrange("b p n -> p b n"), wt[:, :, :]).then_inc(stored, 16)
            sp.wait_ge(row_add, 2)
            for i, r in enumerate((R_L1W, R_L1B, R_L2W, R_L2B)):
                sp.dma_start(t["rows_dram"][:, i, :], lrow[:, r, :]).then_inc(stored, 16)
            sp.wait_ge(stored, 96)

        @block.gpsimd
        def _(pool):
            pool.memset(t["ident"][:, :], 0.0).then_inc(zeroed, 1)
            pool.memset(t["ident_b"][:, :], 0.0).then_inc(zeroed, 1)
            pool.memset(t["trib"][:, :], 0.0).then_inc(zeroed, 1)
            pool.memset(tri[:, :], 0.0).then_inc(zeroed, 1)
            pool.memset(low[:, :], 0.0).then_inc(zeroed, 1)
            pool.wait_ge(zeroed, 5)
            for m in (t["ident"], t["ident_b"]):
                pool.affine_select(out=m[:, :], in_=m[:, :], compare_op=ALU.not_equal, fill=1.0, base=0,
                                   pattern=[[-1, P]], channel_multiplier=1).then_inc(consts, 1)
            pool.affine_select(out=t["trib"][:, :], in_=t["trib"][:, :], compare_op=ALU.is_ge, fill=NEG2,
                               base=0, pattern=[[1, P]], channel_multiplier=-1).then_inc(consts, 1)
            for c in (0, 2):
                m = tri[:, c * P:(c + 1) * P]
                pool.affine_select(out=m, in_=m, compare_op=ALU.is_ge, fill=NEG2, base=0,
                                   pattern=[[-1, P]], channel_multiplier=1).then_inc(consts, 1)
                m = low[:, c * P:(c + 1) * P]
                pool.affine_select(out=m, in_=m, compare_op=ALU.is_gt, fill=NEG2, base=0,
                                   pattern=[[1, P]], channel_multiplier=-1).then_inc(consts, 1)
            pool.wait_ge(pidx_in, 16)
            for i in range(QB):
                pool.indirect_dma_start(pos[:, i, :], None, io["pos_emb"],
                                        bass.IndirectOffsetOnAxis(ap=pidx[:, i:i + 1], axis=0)).then_inc(pos_in, 16)
            pool.wait_ge(idx_in, 16)
            for i in range(NB):
                pool.indirect_dma_start(tok[:, i, :], None, io["tok_emb"],
                                        bass.IndirectOffsetOnAxis(ap=idx[:, i:i + 1], axis=0)).then_inc(tok_in, 16)

        @block.vector
        def _(dve):
            dve.wait_ge(row_in, 16)
            dve.tensor_tensor(lrow[:, R_L1B, :], lrow[:, R_L1B, :], lrow[:, R_MB, :], ALU.add).then_inc(row_add, 1)
            dve.tensor_tensor(lrow[:, R_L2B, :], lrow[:, R_L2B, :], lrow[:, R_PB, :], ALU.add).then_inc(row_add, 1)
            dve.wait_ge(mask_in, 32)
            dve.tensor_scalar(mrow[:, :, :], mrow[:, :, :], -NEG, NEG, ALU.mult, ALU.add).then_inc(ext, 1)
            dve.tensor_scalar(t["ext"][:, :], mcol[:, :], -NEG, NEG, ALU.mult, ALU.add).then_inc(ext, 1)
            dve.wait_ge(ext, 2)
            dve.wait_ge(consts, 7)
            for b in range(B):
                dve.tensor_tensor(m1[:, b, 0:P], mrow[:, b, 0:P], tri[:, 0:P], ALU.add).then_inc(m1_done, 1)
                dve.tensor_tensor(m1[:, b, P:], mrow[:, b, :], tri[:, P:], ALU.add).then_inc(m1_done, 1)
                dve.tensor_tensor(fut[:, b, 0:S], mrow[:, b, :], low[:, 0:S], ALU.add).then_inc(fut_done, 1)
                dve.tensor_tensor(fut[:, b, S:], mrow[:, b, P:], low[:, S:], ALU.add).then_inc(fut_done, 1)
                dve.wait_ge(fut_done, 2 * b + 2)
                dve.tensor_reduce(emax[:, 2 * b:2 * b + 1], fut[:, b, 0:S], AX, ALU.max).then_inc(e_done, 1)
                dve.tensor_reduce(emax[:, 2 * b + 1:2 * b + 2], fut[:, b, S:], AX, ALU.max).then_inc(e_done, 1)
            dve.wait_ge(e_done, 2 * B)
            dve.tensor_scalar(eneg[:, :], emax[:, :], -1.0, None, ALU.mult).then_inc(en_done, 1)
            dve.tensor_scalar(t["e10"][:, :], emax[:, :], -10000.0, None, ALU.add).then_inc(en_done, 1)
            for b in range(B):
                dve.wait_ge(w_t, b + 1)
                dve.tensor_copy(wt[:, b, :], ps[b % 2][:, 0:3 * P]).then_inc(wt_done, 1)
            dve.wait_ge(pos_in, 16 * QB)
            dve.wait_ge(tok_in, 16 * NB)
            dve.wait_ge(pb_in, 16)
            for i in range(NB):
                dve.tensor_tensor(htok[:, i, 0:D], tok[:, i, :], pos[:, i % QB, :], ALU.add).then_inc(added, 1)
                dve.wait_ge(added, i + 1)
                dve.tensor_copy(htok[:, i, D:], htok[:, i, P:D]).then_inc(dup, 1)
                dve.tensor_tensor(t["res"][:, i, :], htok[:, i, 0:D], pb0[:, :], ALU.add).then_inc(dup, 1)
            for b in range(B):
                dve.wait_ge(h_t, b + 1)
                dve.tensor_copy(t["hst"][:, b, :, :], ps[2 + b % 2][:, :].rearrange("p (s n) -> p s n", s=2)).then_inc(h_done, 1)

        @block.scalar
        def _(act):
            act.wait_ge(en_done, 2)
            for b in range(B):
                act.activation(fut[:, b, 0:S], fut[:, b, 0:S], ACT.Exp, bias=eneg[:, 2 * b:2 * b + 1]).then_inc(w_done, 1)
                act.activation(fut[:, b, S:], fut[:, b, S:], ACT.Exp, bias=eneg[:, 2 * b + 1:2 * b + 2]).then_inc(w_done, 1)

        @block.tensor
        def _(pe):
            pe.wait_ge(consts, 7)
            for b in range(B):
                pe.wait_ge(w_done, 2 * b + 2)
                if b >= 2:
                    pe.wait_ge(wt_done, b - 1)
                for c in range(3):
                    last = pe.transpose(ps[b % 2][:, c * P:(c + 1) * P], fut[:, b, c * P:(c + 1) * P], t["ident"][:, :])
                last.then_inc(w_t, 1)
            for b in range(B):
                pe.wait_ge(dup, 4 * b + 4)
                if b >= 2:
                    pe.wait_ge(h_done, b - 1)
                for s in range(2):
                    for q in range(QB):
                        last = pe.transpose(ps[2 + b % 2][:, s * S + q * P:s * S + (q + 1) * P],
                                            htok[:, QB * b + q, s * P:(s + 1) * P], t["ident"][:, :])
                last.then_inc(h_t, 1)


def tower_phase(nc, io, t, layers):
    with ExitStack() as ctx:
        def sb(name, shape, dt=F32):
            return ctx.enter_context(nc.sbuf_tensor(name, shape, dt))

        def both(name, shape, dt=F32):
            return [sb(f"{name}{x}", shape, dt) for x in range(2)]

        def sem(name):
            return nc.alloc_semaphore(name)

        def sems(*names):
            return {n: [sem(f"{n}_{x}") for x in range(2)] for n in names}

        wraw = sb("wraw", [P, 2 * WCOLS + W2COLS])
        whi = sb("whi", [P, 2 * WCOLS + W2COLS], F32R)
        wlo = sb("wlo", [P, 2 * WCOLS + W2COLS], F32R)
        rows = sb("rows", [P, 4, D])
        par = sb("par", [P, LAYERS, NPAR])
        parl = sb("parl", [P, NPAR])
        extp = sb("extp", [P, 2 * QB])

        xh, xl = both("xh", [P, 2, S], F32R), both("xl", [P, S], F32R)
        big, gl, gh = [], [], []
        for x in range(2):
            with nc.sbuf_tensor(f"big{x}", [P, HEADS * 3 * P], F32) as g:
                big.append(g)
            gl.append(sb(f"gl{x}", [P, HC, S], F32R))
            gh.append(sb(f"gh{x}", [P, HC, S], F32R))
            sb(f"big_rest{x}", [P, HEADS * 3 * P - 2 * HC * S])
        stk = both("stk", [P, 2 * HEADS * S], BF16)
        vtok = both("vtok", [P, QB, HEADS, SLOT])
        m1 = both("m1h", [P, 3 * P])
        wt = both("wth", [P, 3 * P])
        mmax = both("mmax", [P, QB, HEADS])
        negm = both("negm", [P, QB, HEADS])
        cpre, cfut = both("cpre", [P, QB, HEADS]), both("cfut", [P, QB, HEADS])
        mres, mtok = both("mres", [P, QB, HEADS]), both("mtok", [P, QB, 3, HEADS], BF16)
        mparts = both("mparts", [3 * HEADS, S], BF16)
        oT = both("oT", [P, HT, S])
        ufut = both("ufut", [P, QB, HEADS, HD + 1])
        otok = both("otok", [P, QB, HEADS, HD + 1])
        rden = both("rden", [P, QB, HEADS])
        xtok = both("xtok", [P, QB, 2 * P])
        xT = both("xT", [P, 2, S])
        ltok = both("ltok", [P, QB, D])
        lst, lmv, lrs = both("lst", [P, QB, 6]), both("lmv", [P, QB, 2]), both("lrs", [P, QB, 1])
        lwk = both("lwk", [P, 2, QB, 1])
        res2 = both("res2", [P, QB, D])
        ps = [[ctx.enter_context(nc.psum_tensor(f"ps{x}{i}", [P, 512], F32)) for i in range(4)] for x in range(2)]

        def w192(tile, slot, col, n):
            return tile[:, slot * WCOLS + col:slot * WCOLS + col + n]

        def w2(tile, c):
            return tile[:, 2 * WCOLS + c * D:2 * WCOLS + (c + 1) * D]

        qk, r1, prt, pt0, pt1, gx, gt, gg = [], [], [], [], [], [], [], []
        qs, ks = [], []
        for x in range(2):
            g = big[x]
            qk.append(g[0:CUT, 0:4 * S].rearrange("p (t n) -> p t n", t=4))
            r1.append(g[0:CUT, 4 * S:8 * S].rearrange("p (t n) -> p t n", t=4))
            prt.append(g[0:CUT, 8 * S:14 * S].bitcast(BF16).rearrange("p (r t n) -> p r t n", t=4, r=3))
            pt0.append(g[:, 0:HEADS * S].rearrange("p (h n) -> p h n", h=HEADS))
            pt1.append(g[:, HEADS * S:].rearrange("p (h n) -> p h n", h=HEADS))
            gx.append(g[:, 0:HC * S].rearrange("p (c n) -> p c n", c=HC))
            gt.append(g[:, HC * S:2 * HC * S].rearrange("p (c n) -> p c n", c=HC))
            gg.append(g[:, 2 * HC * S:3 * HC * S].rearrange("p (c n) -> p c n", c=HC))
            qs.append(stk[x][:, 0:HEADS * S].rearrange("p (h n) -> p h n", h=HEADS))
            ks.append(stk[x][:, HEADS * S:].rearrange("p (h n) -> p h n", h=HEADS))
        HG = HC // 2

        w_in, rows_in, par_in = sem("w_in"), sem("rows_in"), sem("par_in")
        w_hi, w_lo, par_ok, ext_ok = sem("w_hi"), sem("w_lo"), sem("par_ok"), sem("ext_ok")
        init, tick = sem("init"), sem("tick")
        s = sems("h_ready", "x_hi", "x_lo", "qk_mm", "v_mm", "qk32", "v32",
                 "p1", "rs1", "p2", "p3", "stacked", "v1_mm", "v1_rd", "mask_ld", "wt_ld", "mx", "nm", "cp", "cf",
                 "m_t", "mp", "m_ev", "m_st", "u_mm", "u_rd", "v2_mm", "pt", "pv_mm", "o_ev", "o_t", "o_rd", "den", "atok",
                 "a_t", "a_ev", "pj_mm", "ln_add", "ln_st", "ln_ag", "ln_rs", "ln_x", "ln_t", "ln_ev", "ln_res", "r_mul",
                 "fc_mm", "gx", "g_sq", "g_u", "g_th", "g_g", "g_hi", "g_lo", "ml_mm")
        block = ctx.enter_context(nc.Block())

        def product192(pe, out, feature_major, x, col, n, tok0=0, toks=S):
            A, B2, C = xh[x][:, 0, tok0:tok0 + toks], xl[x][:, tok0:tok0 + toks], xh[x][:, 1, tok0:tok0 + toks]
            terms = [(whi, 0, A), (wlo, 0, A), (whi, 0, B2), (whi, 1, C), (wlo, 1, C)]
            for i, (w, slot, act_) in enumerate(terms):
                wa = w192(w, slot, col, n)
                lhs, rhs = (wa, act_) if feature_major else (act_, wa)
                last = pe.matmul(out, lhs, rhs, start=i == 0, stop=i == len(terms) - 1)
            return last

        @block.sync
        def _(sp):
            sp.dma_start(par[:, :, :], io["params"]).then_inc(par_in, 16)
            sp.wait_ge(init, 6)
            with sp.Fori(0, layers) as l:
                sp.wait_ge(w_lo, l * 2)
                sp.wait_ge(w_hi, l * 2)
                hold(sp, tick)
                sp.dma_start(wraw[:, :], io["weights"][l, :, :]).then_inc(w_in, 16)
                for x in range(2):
                    sp.wait_ge(s["ln_res"][x], l * (2 * PAIRS))
                hold(sp, tick)
                sp.dma_start(rows[:, :, :], t["rows_dram"][l, :, :].partition_broadcast(P)).then_inc(rows_in, 16)
                with sp.Fori(0, PAIRS) as p:
                    it = l * PAIRS + p

                    def masks(x):
                        sp.wait_ge(s["v1_rd"][x], it * 9)
                        hold(sp, tick)
                        sp.dma_start(m1[x][:, :], t["m1_dram"][2 * p + x, :, :]).then_inc(s["mask_ld"][x], 16)
                        sp.wait_ge(s["u_mm"][x], it)
                        hold(sp, tick)
                        sp.dma_start(wt[x][:, :], t["wt_dram"][2 * p + x, :, :]).then_inc(s["wt_ld"][x], 16)

                    def stacks(x):
                        sp.wait_ge(s["v2_mm"][x], it * 9)
                        hold(sp, tick)
                        for part, ready in ((0, "p1"), (1, "p2"), (2, "p3")):
                            sp.wait_ge(s[ready][x], it + 1)
                            for role, (dst, parts) in enumerate(((qs[x], Q_PARTS), (ks[x], K_PARTS))):
                                for r in range(6):
                                    if parts[r] != part:
                                        continue
                                    sp.dma_start(
                                        dst[HD * r:HD * (r + 1), :, :], prt[x][:, part, 2 * role:2 * role + 2, :],
                                    ).then_inc(s["stacked"][x], 16)

                    def shifts(x):
                        sp.wait_ge(s["m_ev"][x], it + 1)
                        sp.dma_start(qs[x][KROWS:KROWS + 3, :, :], mparts[x][:, :]).then_inc(s["m_st"][x], 16)

                    for stage in (masks, stacks, shifts):
                        for x in range(2):
                            stage(x)

        @block.gpsimd
        def _(pool):
            n = 0
            for x in range(2):
                for m, value in ((ks[x][KROWS:KROWS + 3, :, :], 1.0), (vtok[x][:, :, :, HD + 1:], 0.0),
                                 (vtok[x][:, :, :, HD:HD + 1], 1.0)):
                    if n:
                        pool.wait_ge(init, n)
                    pool.memset(m, value).then_inc(init, 1)
                    n += 1
            with pool.Fori(0, layers) as l:
                def split_input(x, p):
                    it = l * PAIRS + p
                    pool.wait_ge(s["x_hi"][x], it * 3 + 1)
                    hold(pool, tick)
                    h0 = t["hst"][:, bass.ds(2 * p + x, 1), 0, :].rearrange("p b n -> p (b n)")
                    h1 = t["hst"][P // 2:, bass.ds(2 * p + x, 1), 1, :].rearrange("p b n -> p (b n)")
                    pool.tensor_tensor(xl[x][:, :], h0, xh[x][:, 0, :], ALU.subtract).then_inc(s["x_lo"][x], 1)
                    pool.wait_ge(s["x_lo"][x], it * 6 + 1)
                    hold(pool, tick)
                    pool.tensor_tensor(xh[x][P // 2:, 1, :], h1, xh[x][P // 2:, 1, :], ALU.subtract).then_inc(s["x_lo"][x], 1)
                    pool.wait_ge(s["x_lo"][x], it * 6 + 2)
                    hold(pool, tick)

                def pair(p, following):
                    it = l * PAIRS + p

                    def split_lo(x):
                        pool.wait_ge(s["x_hi"][x], it * 3 + 3)
                        pool.tensor_tensor(xl[x][:, :], xT[x][:, 0, :], xh[x][:, 0, :], ALU.subtract).then_inc(s["x_lo"][x], 1)
                        pool.wait_ge(s["x_lo"][x], it * 6 + 5)
                        pool.tensor_tensor(xh[x][P // 2:, 1, :], xT[x][P // 2:, 1, :], xh[x][P // 2:, 1, :], ALU.subtract).then_inc(s["x_lo"][x], 1)
                        pool.wait_ge(s["x_lo"][x], it * 6 + 6)

                    def residual(x, k):
                        pool.wait_ge(s["ln_x"][x], it * 6 + 3 * k + 3)
                        pool.wait_ge(rows_in, l * 16 + 16)
                        if k == 0:
                            dst = res2[x][:, :, :]
                            pool.wait_ge(s["ln_add"][x], it * 2)
                        else:
                            dst = t["res"][:, bass.ds(QB * (2 * p + x), QB), :]
                            hold(pool, tick)
                        sc = rows[:, 2 * k:2 * k + 1, :].to_broadcast([P, QB, D])
                        bi = rows[:, 2 * k + 1:2 * k + 2, :].to_broadcast([P, QB, D])
                        pool.tensor_tensor(dst, xtok[x][:, :, 0:D], sc, ALU.mult).then_inc(s["r_mul"][x], 1)
                        pool.wait_ge(s["r_mul"][x], it * 2 + k + 1)
                        if k:
                            hold(pool, tick)
                        pool.tensor_tensor(dst, dst, bi, ALU.add).then_inc(s["ln_res"][x], 1)

                    residual(0, 0)
                    split_lo(0)
                    split_lo(1)
                    residual(1, 0)
                    if following:
                        for x in range(2):
                            split_input(x, p + 1)
                    residual(0, 1)
                    residual(1, 1)

                for x in range(2):
                    split_input(x, 0)
                with pool.Fori(0, PAIRS - 1) as p:
                    pair(p, True)
                pair(PAIRS - 1, False)

        @block.scalar
        def _(act):
            for x in range(2):
                act.nop().then_inc(s["h_ready"][x], 2 * PAIRS)
            act.wait_ge(par_in, 16)
            with act.Fori(0, layers) as l:
                act.wait_ge(w_in, l * 16 + 16)
                for x in range(2):
                    act.wait_ge(s["ml_mm"][x], l * PAIRS)
                act.activation(whi[:, 0:2 * WCOLS], wraw[:, 0:2 * WCOLS], ACT.Copy).then_inc(w_hi, 1)
                act.activation(whi[:, 2 * WCOLS:], wraw[:, 2 * WCOLS:], ACT.Copy, scale=0.5).then_inc(w_hi, 1)
                for x in range(2):
                    act.wait_ge(s["h_ready"][x], l * (2 * PAIRS) + 2 * PAIRS)
                hold(act, tick)
                lp = par[:, bass.ds(l, 1), :].rearrange("p a c -> p (a c)")
                act.activation(parl[:, PK:], lp[:, PK:], ACT.Copy).then_inc(par_ok, 1)
                act.activation(parl[:, PQ:PK], lp[:, PQ:PK], ACT.Copy, scale=float(HD) ** -0.5).then_inc(par_ok, 1)
                act.wait_ge(par_ok, l * 2 + 2)
                def split_input(x, p):
                    it = l * PAIRS + p
                    act.wait_ge(s["fc_mm"][x], it * 3)
                    act.wait_ge(s["h_ready"][x], it * 2 + 2)
                    hold(act, tick)
                    act.activation(xh[x][:, :, :], t["hst"][:, bass.ds(2 * p + x, 1), :, :].rearrange("p b s n -> p (b s) n"),
                                   ACT.Copy).then_inc(s["x_hi"][x], 1)

                def qk_out(x, p):
                    it = l * PAIRS + p
                    act.wait_ge(s["ml_mm"][x], it)
                    for i in range(4):
                        if i % 2 == 0:
                            act.wait_ge(s["qk_mm"][x], it * 2 + i // 2 + 1)
                        src = ps[x][i // 2][0:CUT, (i % 2) * S:(i % 2 + 1) * S]
                        act.activation(qk[x][:, i, :], src, ACT.Identity, bias=parl[0:CUT, PQ + i:PQ + i + 1],
                                       scale=float(HD) ** -0.5 if i < 2 else 1.0).then_inc(s["qk32"][x], 1)

                def pair(p, following):
                    it = l * PAIRS + p

                    act.wait_ge(s["pt"][1], it * 9)
                    hold(act, tick)
                    act.activation(extp[:, :], t["ext"][:, bass.ds(2 * QB * p, 2 * QB)], ACT.Copy).then_inc(ext_ok, 1)

                    def split_hi(x, k):
                        act.wait_ge(s["v_mm"][x] if k == 1 else s["pj_mm"][x], it + 1)
                        act.wait_ge(s["a_ev"][x] if k == 1 else s["ln_ev"][x], it * 2 + 2)
                        act.activation(xh[x][:, :, :], xT[x][:, :, :], ACT.Copy).then_inc(s["x_hi"][x], 1)

                    def future_weight(x):
                        act.wait_ge(s["cp"][x], it * 2 + 2)
                        act.wait_ge(s["u_rd"][x], it)
                        act.activation(cfut[x][:, :, :], cpre[x][:, :, :], ACT.Exp).then_inc(s["cf"][x], 1)

                    def probs(x, js):
                        if js[0] == 0:
                            act.wait_ge(s["stacked"][x], it * 192 + 192)
                            act.wait_ge(ext_ok, it + 1)
                        for j in js:
                            act.wait_ge(s["v2_mm"][x], it * 9 + j + 1)
                            bank = ps[x][(2, 3, 0)[j % 3]]
                            if j < 6:
                                dst = pt0[x][:, 2 * j:2 * j + 2, :]
                                src = bank[:, :].rearrange("p (h n) -> p h n", h=2)
                            else:
                                dst = pt1[x][:, 4 * (j - 6):4 * (j - 6) + 4, :]
                                src = bank[:, :].rearrange("p (h n) -> p h n", h=4)
                            act.activation(dst, src, ACT.Exp, bias=extp[:, QB * x + j // 6:QB * x + j // 6 + 1]).then_inc(s["pt"][x], 1)

                    def o_out(x):
                        act.wait_ge(s["pv_mm"][x], it * 2 + 1)
                        act.activation(oT[x][:, 0:2, :], ps[x][1][:, :].rearrange("p (t n) -> p t n", t=2), ACT.Copy).then_inc(s["o_ev"][x], 1)
                        act.wait_ge(s["pv_mm"][x], it * 2 + 2)
                        act.activation(oT[x][:, 2, :], ps[x][2][:, 0:S], ACT.Copy).then_inc(s["o_ev"][x], 1)

                    def a_out(x):
                        act.wait_ge(s["a_t"][x], it + 1)
                        act.wait_ge(s["x_lo"][x], it * 6 + 2)
                        for c in range(2):
                            act.activation(xT[x][:, c, :], ps[x][1][:, c * S:(c + 1) * S], ACT.Identity,
                                           bias=parl[:, PV_ + c:PV_ + c + 1]).then_inc(s["a_ev"][x], 1)

                    def norm_out(x, k):
                        act.wait_ge(s["ln_t"][x], it * 2 + k + 1)
                        for c in range(2):
                            if k == 0:
                                act.wait_ge(s["x_lo"][x], it * 6 + 4)
                                dst, bank, done = xT[x][:, c, :], ps[x][3], s["ln_ev"][x]
                            else:
                                if c == 0:
                                    hold(act, tick)
                                dst = t["hst"][:, bass.ds(2 * p + x, 1), c, :].rearrange("p b n -> p (b n)")
                                bank, done = ps[x][3], s["h_ready"][x]
                            act.activation(dst, bank[:, c * S:(c + 1) * S], ACT.Identity,
                                           scale=parl[:, (PL1W, PL2W)[k] + c:(PL1W, PL2W)[k] + c + 1],
                                           bias=parl[:, (PL1B, PL2B)[k] + c:(PL1B, PL2B)[k] + c + 1]).then_inc(done, 1)

                    def hidden(x, g):
                        if g == 0:
                            act.wait_ge(s["pv_mm"][x], it * 2 + 2)
                        for c in range(g * HG, (g + 1) * HG):
                            act.wait_ge(s["fc_mm"][x], it * 3 + c // 2 + 1)
                            act.activation(gx[x][:, c, :], ps[x][c // 2][:, (c % 2) * S:(c % 2 + 1) * S], ACT.Identity,
                                           bias=parl[:, PFC + c:PFC + c + 1]).then_inc(s["gx"][x], 1)
                        act.wait_ge(s["gx"][x], it * HC + (g + 1) * HG)
                        cs = slice(g * HG, (g + 1) * HG)
                        act.activation(gt[x][:, cs, :], gx[x][:, cs, :], ACT.Square).then_inc(s["g_sq"][x], 1)

                    def tanh(x, g):
                        act.wait_ge(s["g_u"][x], it * 2 + g + 1)
                        cs = slice(g * HG, (g + 1) * HG)
                        act.activation(gt[x][:, cs, :], gt[x][:, cs, :], ACT.Tanh, scale=GELU_C * GELU_A).then_inc(s["g_th"][x], 1)

                    def gelu_hi(x, g):
                        act.wait_ge(s["g_g"][x], it * 2 + g + 1)
                        cs = slice(g * HG, (g + 1) * HG)
                        act.activation(gh[x][:, cs, :], gg[x][:, cs, :], ACT.Copy).then_inc(s["g_hi"][x], 1)

                    future_weight(0)
                    probs(0, range(9))
                    future_weight(1)
                    probs(1, range(6))
                    o_out(0)
                    probs(1, range(6, 9))
                    o_out(1)
                    for x in range(2):
                        a_out(x)
                        split_hi(x, 1)
                    for x in range(2):
                        norm_out(x, 0)
                        split_hi(x, 2)
                    hidden(0, 0)
                    hidden(0, 1)
                    if following:
                        split_input(0, p + 1)
                    tanh(0, 0)
                    tanh(0, 1)
                    hidden(1, 0)
                    gelu_hi(0, 0)
                    gelu_hi(0, 1)
                    hidden(1, 1)
                    if following:
                        split_input(1, p + 1)
                    tanh(1, 0)
                    tanh(1, 1)
                    gelu_hi(1, 0)
                    gelu_hi(1, 1)
                    for x in range(2):
                        if following:
                            qk_out(x, p + 1)
                        norm_out(x, 1)

                for x in range(2):
                    split_input(x, 0)
                for x in range(2):
                    qk_out(x, 0)
                with act.Fori(0, PAIRS - 1) as p:
                    pair(p, True)
                pair(PAIRS - 1, False)

        @block.vector
        def _(dve):
            with dve.Fori(0, layers) as l:
                dve.wait_ge(w_hi, l * 2 + 2)
                for x in range(2):
                    dve.wait_ge(s["ml_mm"][x], l * PAIRS)
                dve.tensor_tensor(wlo[:, 0:2 * WCOLS], wraw[:, 0:2 * WCOLS], whi[:, 0:2 * WCOLS], ALU.subtract).then_inc(w_lo, 1)
                dve.scalar_tensor_tensor(wlo[:, 2 * WCOLS:], wraw[:, 2 * WCOLS:], 0.5, whi[:, 2 * WCOLS:],
                                         ALU.mult, ALU.subtract).then_inc(w_lo, 1)
                def v_out(x, p):
                    it = l * PAIRS + p
                    dve.wait_ge(s["v_mm"][x], it + 1)
                    dve.wait_ge(s["pv_mm"][x], it * 2)
                    dve.tensor_copy(vtok[x][:, :, :, 0:HD].rearrange("p q h d -> p (q h) d"),
                                    ps[x][2][:, 0:QB * D].rearrange("p (g d) -> p g d", d=HD)).then_inc(s["v32"][x], 1)

                def parts(x, p):
                    it = l * PAIRS + p
                    dve.wait_ge(s["qk32"][x], it * 4 + 4)
                    dve.tensor_copy(prt[x][:, 0, :, :], qk[x][:, :, :]).then_inc(s["p1"][x], 1)
                    dve.wait_ge(s["p1"][x], it + 1)
                    dve.tensor_tensor(r1[x][:, :, :], qk[x][:, :, :], prt[x][:, 0, :, :], ALU.subtract).then_inc(s["rs1"][x], 1)
                    dve.wait_ge(s["rs1"][x], it + 1)
                    dve.tensor_copy(prt[x][:, 1, :, :], r1[x][:, :, :]).then_inc(s["p2"][x], 1)
                    dve.wait_ge(s["p2"][x], it + 1)
                    dve.tensor_tensor(prt[x][:, 2, :, :], r1[x][:, :, :], prt[x][:, 1, :, :], ALU.subtract).then_inc(s["p3"][x], 1)

                def pair(p, following):
                    it = l * PAIRS + p

                    def split_lo(x):
                        dve.wait_ge(s["x_hi"][x], it * 3 + 2)
                        dve.tensor_tensor(xl[x][:, :], xT[x][:, 0, :], xh[x][:, 0, :], ALU.subtract).then_inc(s["x_lo"][x], 1)
                        dve.tensor_tensor(xh[x][P // 2:, 1, :], xT[x][P // 2:, 1, :], xh[x][P // 2:, 1, :], ALU.subtract).then_inc(s["x_lo"][x], 1)

                    def row_max(x, js):
                        if js[0] == 0:
                            dve.wait_ge(s["mask_ld"][x], it * 16 + 16)
                            dve.wait_ge(s["nm"][x], it * 2)
                        for j in js:
                            dve.wait_ge(s["v1_mm"][x], it * 9 + j + 1)
                            hold(dve, tick)
                            bank = ps[x][j % 4]
                            heads, q, n, m0 = (range(4 * j, 4 * j + 4), 0, P, 0) if j < 3 else \
                                (range(2 * (j - 3), 2 * (j - 3) + 2), 1, S, P)
                            for i, h in enumerate(heads):
                                last = dve.tensor_tensor_reduce(
                                    out=bank[:, i * n:(i + 1) * n], in0=bank[:, i * n:(i + 1) * n], in1=m1[x][:, m0:m0 + n], scale=1.0,
                                    scalar=NEG2 * 4, op0=ALU.add, op1=ALU.max, accum_out=mmax[x][:, q, h:h + 1])
                            last.then_inc(s["v1_rd"][x], 1)

                    def shift(x):
                        dve.wait_ge(s["v1_rd"][x], it * 9 + 9)
                        dve.wait_ge(s["cp"][x], it * 2)
                        for q in range(QB):
                            e10 = t["e10"][:, bass.ds(QB * (2 * p + x) + q, 1)]
                            dve.tensor_scalar(negm[x][:, q, :], mmax[x][:, q, :], e10, -1.0, ALU.max, ALU.mult).then_inc(s["nm"][x], 1)
                        dve.wait_ge(s["nm"][x], it * 2 + 2)
                        dve.wait_ge(s["m_t"][x], it)
                        dve.tensor_copy(mtok[x][:, :, 0, :], negm[x][:, :, :]).then_inc(s["mp"][x], 1)
                        dve.wait_ge(s["cf"][x], it)
                        for q in range(QB):
                            e10 = t["e10"][:, bass.ds(QB * (2 * p + x) + q, 1)]
                            dve.tensor_scalar(cpre[x][:, q, :], negm[x][:, q, :], e10, None, ALU.add).then_inc(s["cp"][x], 1)
                        dve.wait_ge(s["mp"][x], it * 4 + 1)
                        dve.tensor_tensor(mres[x][:, :, :], negm[x][:, :, :], mtok[x][:, :, 0, :], ALU.subtract).then_inc(s["mp"][x], 1)
                        dve.wait_ge(s["mp"][x], it * 4 + 2)
                        dve.tensor_copy(mtok[x][:, :, 1, :], mres[x][:, :, :]).then_inc(s["mp"][x], 1)
                        dve.wait_ge(s["mp"][x], it * 4 + 3)
                        dve.tensor_tensor(mtok[x][:, :, 2, :], mres[x][:, :, :], mtok[x][:, :, 1, :], ALU.subtract).then_inc(s["mp"][x], 1)

                    def shift_out(x):
                        dve.wait_ge(s["m_t"][x], it + 1)
                        dve.wait_ge(s["m_st"][x], it * 16)
                        dve.tensor_copy(mparts[x][:, :], ps[x][0][:, 0:P].bitcast(BF16)[0:3 * HEADS, 0:S]).then_inc(s["m_ev"][x], 1)

                    def future(x):
                        dve.wait_ge(s["u_mm"][x], it + 1)
                        dve.wait_ge(s["cf"][x], it + 1)
                        dve.tensor_tensor(ufut[x][:, :, :, :].rearrange("p q h d -> p (q h) d"),
                                          ps[x][1][:, 0:QB * HEADS * (HD + 1)].rearrange("p (g d) -> p g d", d=HD + 1),
                                          cfut[x][:, :, :].rearrange("p q h -> p (q h)").unsqueeze(2).to_broadcast([P, QB * HEADS, HD + 1]),
                                          ALU.mult).then_inc(s["u_rd"][x], 1)

                    def attend(x):
                        dve.wait_ge(s["u_rd"][x], it + 1)
                        for q in range(QB):
                            dve.wait_ge(s["o_t"][x], it * 2 + q + 1)
                            dve.tensor_tensor(otok[x][:, q, :, :], ps[x][(3, 0)[q]][:, 0:HEADS * SLOT].rearrange(
                                "p (h d) -> p h d", d=SLOT)[:, :, 0:HD + 1], ufut[x][:, q, :, :], ALU.add).then_inc(s["o_rd"][x], 1)
                        dve.wait_ge(s["o_rd"][x], it * 2 + 2)
                        dve.reciprocal(rden[x][:, :, :].rearrange("p q h -> p (q h)").unsqueeze(2),
                                       otok[x][:, :, :, HD:HD + 1].rearrange("p q h d -> p (q h) d")).then_inc(s["den"][x], 1)
                        dve.wait_ge(s["den"][x], it + 1)
                        dve.wait_ge(s["ln_t"][x], it * 2)
                        dve.wait_ge(s["ln_res"][x], it * 2)
                        for q in range(QB):
                            dve.tensor_tensor(xtok[x][:, q, 0:D].rearrange("p (h d) -> p h d", d=HD), otok[x][:, q, :, 0:HD],
                                              rden[x][:, q, :].unsqueeze(2).to_broadcast([P, HEADS, HD]), ALU.mult).then_inc(s["atok"][x], 1)
                        dve.wait_ge(s["atok"][x], it * 3 + 2)
                        dve.tensor_copy(xtok[x][:, :, D:], xtok[x][:, :, P:D]).then_inc(s["atok"][x], 1)

                    def norm(x, k):
                        n = it * 2 + k
                        dve.wait_ge(s["pj_mm"][x] if k == 0 else s["ml_mm"][x], it + 1)
                        bank = ps[x][2] if k == 0 else ps[x][3]
                        if k == 0:
                            res = t["res"][:, bass.ds(QB * (2 * p + x), QB), :]
                        else:
                            res = res2[x][:, :, :]
                            dve.wait_ge(s["ln_res"][x], it * 2 + 1)
                        dve.tensor_tensor(ltok[x][:, :, :], bank[:, 0:QB * D].rearrange("p (q n) -> p q n", q=QB), res, ALU.add).then_inc(s["ln_add"][x], 1)
                        dve.wait_ge(s["ln_add"][x], n + 1)
                        for q in range(QB):
                            dve.bn_stats(lst[x][:, q, :], ltok[x][:, q, :]).then_inc(s["ln_st"][x], 1)
                        dve.wait_ge(s["ln_st"][x], n * 2 + 2)
                        hold(dve, tick)
                        for q in range(QB):
                            dve.bn_aggr(lmv[x][:, q, :], lst[x][:, q, :]).then_inc(s["ln_ag"][x], 1)
                        dve.wait_ge(s["ln_ag"][x], n * 2 + 2)
                        rsqrt_steps(dve, s["ln_rs"][x], n * RSQRT_STEPS, lmv[x][:, :, 1:2], lrs[x][:, :, :], lwk[x][:, 0, :, :], lwk[x][:, 1, :, :])
                        if k == 0:
                            dve.wait_ge(s["a_t"][x], it + 1)
                        else:
                            dve.wait_ge(s["ln_t"][x], it * 2 + 1)
                            dve.wait_ge(s["ln_res"][x], it * 2 + 1)
                        for q in range(QB):
                            dve.tensor_scalar(xtok[x][:, q, 0:D], ltok[x][:, q, :], lmv[x][:, q, 0:1], lrs[x][:, q, :],
                                              ALU.subtract, ALU.mult).then_inc(s["ln_x"][x], 1)
                        dve.wait_ge(s["ln_x"][x], n * 3 + 2)
                        dve.tensor_copy(xtok[x][:, :, D:], xtok[x][:, :, P:D]).then_inc(s["ln_x"][x], 1)

                    def gelu_arg(x, g):
                        dve.wait_ge(s["g_sq"][x], it * 2 + g + 1)
                        cs = slice(g * HG, (g + 1) * HG)
                        dve.scalar_tensor_tensor(gt[x][:, cs, :], gt[x][:, cs, :], 1.0 / GELU_A, gx[x][:, cs, :], ALU.add, ALU.mult).then_inc(s["g_u"][x], 1)

                    def gelu(x, g):
                        dve.wait_ge(s["g_th"][x], it * 2 + g + 1)
                        cs = slice(g * HG, (g + 1) * HG)
                        dve.scalar_tensor_tensor(gg[x][:, cs, :], gt[x][:, cs, :], 1.0, gx[x][:, cs, :], ALU.add, ALU.mult).then_inc(s["g_g"][x], 1)

                    def gelu_lo(x, g):
                        dve.wait_ge(s["g_hi"][x], it * 2 + g + 1)
                        cs = slice(g * HG, (g + 1) * HG)
                        dve.tensor_tensor(gl[x][:, cs, :], gg[x][:, cs, :], gh[x][:, cs, :], ALU.subtract).then_inc(s["g_lo"][x], 1)

                    row_max(0, range(9))
                    shift(0)
                    row_max(1, range(4))
                    shift_out(0)
                    row_max(1, range(4, 9))
                    shift(1)
                    future(0)
                    shift_out(1)
                    future(1)
                    for x in range(2):
                        attend(x)
                    for x in range(2):
                        split_lo(x)
                    for x in range(2):
                        norm(x, 0)
                    gelu_arg(0, 0)
                    gelu_arg(0, 1)
                    gelu(0, 0)
                    gelu(0, 1)
                    gelu_arg(1, 0)
                    gelu_lo(0, 0)
                    gelu_lo(0, 1)
                    gelu_arg(1, 1)
                    gelu(1, 0)
                    gelu(1, 1)
                    gelu_lo(1, 0)
                    gelu_lo(1, 1)
                    for x in range(2):
                        norm(x, 1)
                        if following:
                            parts(x, p + 1)
                            v_out(x, p + 1)

                for x in range(2):
                    parts(x, 0)
                    v_out(x, 0)
                with dve.Fori(0, PAIRS - 1) as p:
                    pair(p, True)
                pair(PAIRS - 1, False)

        @block.tensor
        def _(pe):
            ident, ident_b, trib = t["ident"], t["ident_b"], t["trib"]
            with pe.Fori(0, layers) as l:
                pe.wait_ge(w_hi, l * 2 + 2)
                pe.wait_ge(w_lo, l * 2 + 2)
                hold(pe, tick)
                def qkv(x, p):
                    it = l * PAIRS + p
                    pe.wait_ge(s["x_lo"][x], it * 6 + 2)
                    pe.wait_ge(s["gx"][x], it * HC)
                    for i in range(4):
                        last = product192(pe, ps[x][i // 2][0:CUT, (i % 2) * S:(i % 2 + 1) * S], True, x, CUT * i, CUT)
                        if i % 2:
                            last.then_inc(s["qk_mm"][x], 1)
                    for q in range(QB):
                        last = product192(pe, ps[x][2][:, q * D:(q + 1) * D], False, x, WV, D, q * P, P)
                    last.then_inc(s["v_mm"][x], 1)

                def pair(p, following):
                    it = l * PAIRS + p

                    def scores(x, js):
                        if js[0] == 0:
                            pe.wait_ge(s["stacked"][x], it * 192 + 192)
                            pe.wait_ge(s["qk32"][x], it * 4 + 4)
                            pe.wait_ge(s["v32"][x], it + 1)
                            pe.wait_ge(s["h_ready"][x], it * 2 + 2 * PAIRS)
                        for j in js:
                            if j >= 4:
                                pe.wait_ge(s["v1_rd"][x], it * 9 + j - 3)
                            bank = ps[x][j % 4]
                            heads, q, n = (range(4 * j, 4 * j + 4), 0, P) if j < 3 else (range(2 * (j - 3), 2 * (j - 3) + 2), 1, S)
                            for i, h in enumerate(heads):
                                last = pe.matmul(bank[:, i * n:(i + 1) * n], qs[x][0:KROWS, h, q * P:(q + 1) * P],
                                                 ks[x][0:KROWS, h, 0:n], start=True, stop=True)
                            last.then_inc(s["v1_mm"][x], 1)

                    def shift_t(x):
                        pe.wait_ge(s["mp"][x], it * 4 + 4)
                        pe.wait_ge(s["v1_rd"][x], it * 9 + 9)
                        hold(pe, tick)
                        for q in range(QB):
                            last = pe.transpose(ps[x][0][:, 0:P].bitcast(BF16)[0:3 * HEADS, q * P:(q + 1) * P],
                                                mtok[x][:, q, :, :].rearrange("p r h -> p (r h)"), ident_b[:, :])
                        last.then_inc(s["m_t"][x], 1)

                    def future(x):
                        pe.wait_ge(s["wt_ld"][x], it * 16 + 16)
                        n = HEADS * (HD + 1)
                        for q, kb, w in ((0, 0, 0), (0, 1, 1), (1, 1, 2)):
                            last = pe.matmul(ps[x][1][:, q * n:(q + 1) * n], wt[x][:, w * P:(w + 1) * P],
                                             vtok[x][:, kb, :, 0:HD + 1], start=w != 1, stop=w != 0)
                        last.then_inc(s["u_mm"][x], 1)

                    def scores_t(x, js):
                        if js[0] == 0:
                            pe.wait_ge(s["m_st"][x], it * 16 + 16)
                        for j in js:
                            if j == 2:
                                pe.wait_ge(s["m_ev"][x], it + 1)
                            if j >= 3:
                                pe.wait_ge(s["pt"][x], it * 9 + j - 2)
                            bank = ps[x][(2, 3, 0)[j % 3]]
                            heads, kb, q0, n = (range(2 * j, 2 * j + 2), 0, 0, S) if j < 6 else \
                                (range(4 * (j - 6), 4 * (j - 6) + 4), 1, P, P)
                            for i, h in enumerate(heads):
                                pe.matmul(bank[:, i * n:(i + 1) * n], ks[x][0:KROWS + 3, h, kb * P:(kb + 1) * P],
                                          qs[x][0:KROWS + 3, h, q0:q0 + n], start=i == 0, stop=False, skip_group_check=True)
                            m = len(heads)
                            last = pe.matmul(bank[:, :].rearrange("p (h n) -> p h n", h=m)[:, :, 0:P], ident_b[:, :],
                                             trib[:, :].unsqueeze(1).to_broadcast([P, m, P]), start=False, stop=True, skip_group_check=True)
                            last.then_inc(s["v2_mm"][x], 1)

                    def attend(x):
                        pe.wait_ge(s["u_rd"][x], it + 1)
                        pe.wait_ge(s["pt"][x], it * 9 + 9)
                        for h in range(HEADS):
                            a, j = divmod(h, HSLOT)
                            bank, c0 = (ps[x][1], a * S) if a < 2 else (ps[x][2], 0)
                            pe.matmul(bank[SLOT * j:SLOT * (j + 1), c0:c0 + S], vtok[x][:, 0, h, :], pt0[x][:, h, :],
                                      start=True, stop=False, skip_group_check=True)
                            last = pe.matmul(bank[SLOT * j:SLOT * (j + 1), c0 + P:c0 + S], vtok[x][:, 1, h, :], pt1[x][:, h, :],
                                             start=False, stop=True, skip_group_check=True)
                            if h in (7, 11):
                                last.then_inc(s["pv_mm"][x], 1)

                    def o_t(x):
                        pe.wait_ge(s["o_ev"][x], it * 2 + 2)
                        for q in range(QB):
                            for a in range(HT):
                                last = pe.transpose(ps[x][(3, 0)[q]][:, a * P:(a + 1) * P], oT[x][:, a, q * P:(q + 1) * P], ident[:, :])
                            last.then_inc(s["o_t"][x], 1)

                    def token_t(x, bank, ready, done):
                        pe.wait_ge(*ready)
                        for c in range(2):
                            for q in range(QB):
                                last = pe.transpose(bank[:, c * S + q * P:c * S + (q + 1) * P], xtok[x][:, q, c * P:(c + 1) * P], ident[:, :])
                        last.then_inc(done, 1)

                    def a_t(x):
                        token_t(x, ps[x][1], (s["atok"][x], it * 3 + 3), s["a_t"][x])

                    def proj(x):
                        pe.wait_ge(s["x_lo"][x], it * 6 + 4)
                        for q in range(QB):
                            last = product192(pe, ps[x][2][:, q * D:(q + 1) * D], False, x, WO, D, q * P, P)
                        last.then_inc(s["pj_mm"][x], 1)

                    def norm_t(x, k):
                        if k == 0:
                            pe.wait_ge(s["o_rd"][x], it * 2 + 2)
                        token_t(x, ps[x][3], (s["ln_x"][x], it * 6 + 3 * k + 3), s["ln_t"][x])

                    def fc(x):
                        pe.wait_ge(s["x_lo"][x], it * 6 + 6)
                        pe.wait_ge(s["ln_add"][x], it * 2 + 1)
                        for c in range(HC):
                            last = product192(pe, ps[x][c // 2][:, (c % 2) * S:(c % 2 + 1) * S], True, x, WFC + P * c, P)
                            if c % 2:
                                last.then_inc(s["fc_mm"][x], 1)

                    def mlp(x):
                        for g in range(2):
                            pe.wait_ge(s["g_lo"][x], it * 2 + g + 1)
                            for q in range(QB):
                                out = ps[x][3][:, q * D:(q + 1) * D]
                                for c in range(g * HG, (g + 1) * HG):
                                    g0, g1 = gh[x][:, c, q * P:(q + 1) * P], gl[x][:, c, q * P:(q + 1) * P]
                                    pe.matmul(out, g0, w2(whi, c), start=c == 0 and q == 0, stop=False, skip_group_check=True)
                                    pe.matmul(out, g0, w2(wlo, c), start=False, stop=False, skip_group_check=True)
                                    last = pe.matmul(out, g1, w2(whi, c), start=False, stop=c == HC - 1, skip_group_check=True)
                        last.then_inc(s["ml_mm"][x], 1)

                    scores(0, range(9))
                    scores(1, range(4))
                    shift_t(0)
                    scores(1, range(4, 9))
                    future(0)
                    scores_t(0, range(5))
                    shift_t(1)
                    scores_t(0, range(5, 9))
                    future(1)
                    scores_t(1, range(4))
                    attend(0)
                    scores_t(1, range(4, 9))
                    o_t(0)
                    attend(1)
                    o_t(1)
                    for x in range(2):
                        a_t(x)
                    for x in range(2):
                        proj(x)
                    for x in range(2):
                        norm_t(x, 0)
                    for x in range(2):
                        fc(x)
                    if following:
                        qkv(0, p + 1)
                    mlp(0)
                    mlp(1)
                    norm_t(0, 1)
                    if following:
                        qkv(1, p + 1)
                    norm_t(1, 1)

                for x in range(2):
                    qkv(x, 0)
                with pe.Fori(0, PAIRS - 1) as p:
                    pair(p, True)
                pair(PAIRS - 1, False)
        return s


WZ, WU, WDT = 0, DI, 2 * DI
SCOLS = 2 * DI + P
SP_DTB, SP_CB, SP_D, SP_NW, SP_CW = 0, DJ, 2 * DJ, 3 * DJ, 4 * DJ
NSPAR = SP_CW + DJ * KCONV
TOK2 = 2 * S
NT2 = TOK2 // P
PAD = KCONV - 1
DT_MIN, DT_MAX = 1e-4, 1.0


def five_passes(pe, out, whi, wlo, wcols, xh, xl, xcols, feature_major=True):
    A, L, C = xh[:, 0, xcols], xl[:, xcols], xh[:, 1, xcols]
    terms = [(whi[:, 0, wcols], A), (wlo[:, 0, wcols], A), (whi[:, 0, wcols], L), (whi[:, 1, wcols], C), (wlo[:, 1, wcols], C)]
    for i, (w, x) in enumerate(terms):
        lhs, rhs = (w, x) if feature_major else (x, w)
        last = pe.matmul(out, lhs, rhs, start=i == 0, stop=i == len(terms) - 1)
    return last


def layernorm_tokens(dve, tick, src, dst, st, mv, rs, v, w, sem_st, sem_ag, sem_rs, sem_x, it, blocks):
    for q in range(blocks):
        dve.bn_stats(st[:, q, :], src[:, q, :]).then_inc(sem_st, 1)
    dve.wait_ge(sem_st, it * blocks + blocks)
    hold(dve, tick)
    for q in range(blocks):
        dve.bn_aggr(mv[:, q, :], st[:, q, :]).then_inc(sem_ag, 1)
    dve.wait_ge(sem_ag, it * blocks + blocks)
    rsqrt_steps(dve, sem_rs, it * RSQRT_STEPS, mv[:, :, 1:2], rs, v, w)
    for q in range(blocks):
        dve.tensor_scalar(dst[:, q, 0:D], src[:, q, :], mv[:, q, 0:1], rs[:, q, :], ALU.subtract, ALU.mult).then_inc(sem_x, 1)
    dve.wait_ge(sem_x, it * (blocks + 1) + blocks)
    dve.tensor_copy(dst[:, :, D:], dst[:, :, P:D]).then_inc(sem_x, 1)


def scan_input_phase(nc, io, t):
    with ExitStack() as ctx:
        def sb(name, shape, dt=F32):
            return ctx.enter_context(nc.sbuf_tensor(name, shape, dt))

        def sem(name):
            return nc.alloc_semaphore("si_" + name)

        tick = sem("tick")

        wraw = t["zs"][:, 0, 0:2 * SCOLS].rearrange("p (s n) -> p s n", s=2)
        rraw, oraw = t["y"][:, 0:2, 0:DI], t["dtu"][:, :, 0:D]
        whi, wlo = sb("si_whi", [P, 2, SCOLS], F32R), sb("si_wlo", [P, 2, SCOLS], F32R)
        rhi, rlo = sb("si_rhi", [P, 2, DI], F32R), sb("si_rlo", [P, 2, DI], F32R)
        ohi, olo = sb("si_ohi", [P, DJ, D], F32R), sb("si_olo", [P, DJ, D], F32R)
        dhi, dlo = sb("si_dhi", [P, DI], F32R), sb("si_dlo", [P, DI], F32R)
        par, lnp = sb("si_par", [P, NSPAR]), sb("si_lnp", [P, 4])
        x1, x2 = sb("si_x1", [P, NT2, 2 * P]), sb("si_x2", [P, NT2, 2 * P])
        st, mv = sb("si_st", [P, NT2, 6]), sb("si_mv", [P, NT2, 2])
        rs, v, w = sb("si_rs", [P, NT2, 1]), sb("si_v", [P, NT2, 1]), sb("si_w", [P, NT2, 1])
        xT = sb("si_xT", [P, 2, TOK2])
        xh, xl = sb("si_xh", [P, 2, TOK2], F32R), sb("si_xl", [P, TOK2], F32R)
        dth = sb("si_dth", [P, TOK2], F32R)
        up = sb("si_up", [P, DJ, 2, S + PAD])
        u = sb("si_u", [P, DJ, TOK2])
        rTh, rTl = sb("si_rTh", [P, DJ, TOK2], F32R), sb("si_rTl", [P, DJ, TOK2], F32R)
        psm = ctx.enter_context(nc.psum_tensor("si_ps", [P, 8, 512], F32))
        names = ("w_in", "r_in", "o_in", "d_in", "par_in", "whi", "wlo", "rhi", "rlo", "ohi", "olo", "dhi", "dlo", "pad0",
                 "st1", "ag1", "rs1", "x1", "st2", "ag2", "rs2", "x2", "t_mm", "t_ev", "xhi", "xlo", "r_mm", "r_hi", "r_lo",
                 "o_mm", "res", "z_mm", "nz", "ez", "sz", "u_mm", "u_ev", "cv", "dh_mm", "dh_hi", "dh_lo", "dt_mm", "dm", "de", "dd",
                 "dl", "dc", "yi", "out")
        q = {n: sem(n) for n in names}
        block = ctx.enter_context(nc.Block())
        flat = "p j n -> p (j n)"

        def pair(tile, p):
            return tile[:, :, bass.ds(p * TOK2, TOK2)]

        @block.sync
        def _(sp):
            sp.dma_start(par[:, :], io["s_params"]).then_inc(q["par_in"], 16)
            sp.dma_start(lnp[:, :], io["s_ln"]).then_inc(q["par_in"], 16)
            sp.dma_start(wraw, io["s_w"]).then_inc(q["w_in"], 16)
            sp.dma_start(rraw, io["s_wres"]).then_inc(q["r_in"], 16)
            sp.dma_start(oraw, io["s_wout"]).then_inc(q["o_in"], 16)
            sp.dma_start(u[:, 0, 0:DI], io["s_wdt"]).then_inc(q["d_in"], 16)

        @block.gpsimd
        def _(pool):
            pool.memset(up[:, :, :, 0:PAD], 0.0).then_inc(q["pad0"], 1)
            pool.wait_ge(q["whi"], 1)
            pool.tensor_tensor(wlo[:, :, :], wraw, whi[:, :, :], ALU.subtract).then_inc(q["wlo"], 1)

        @block.scalar
        def _(act):
            act.wait_ge(q["w_in"], 16)
            act.activation(whi[:, :, :], wraw, ACT.Copy).then_inc(q["whi"], 1)
            act.wait_ge(q["r_in"], 16)
            act.activation(rhi[:, :, :], rraw, ACT.Copy).then_inc(q["rhi"], 1)
            act.wait_ge(q["o_in"], 16)
            act.activation(ohi[:, :, :], oraw, ACT.Copy).then_inc(q["ohi"], 1)
            act.wait_ge(q["d_in"], 16)
            act.activation(dhi[:, :], u[:, 0, 0:DI], ACT.Copy).then_inc(q["dhi"], 1)
            act.wait_ge(q["par_in"], 32)
            for m in ("rlo", "olo", "dlo"):
                act.wait_ge(q[m], 1)
            act.wait_ge(q["wlo"], 1)
            with act.Fori(0, PAIRS) as p:
                a, b = pair(t["y"], p), pair(t["dtu"], p)
                for c in range(2):
                    act.wait_ge(q["t_mm"], p * 4 + c + 1)
                    act.wait_ge(q["xlo"], p * 4)
                    act.activation(xT[:, c, :], psm[:, c, :], ACT.Copy).then_inc(q["t_ev"], 1)
                act.wait_ge(q["t_ev"], p * 4 + 2)
                act.wait_ge(q["u_mm"], p)
                act.activation(xh[:, :, :], xT[:, :, :], ACT.Copy).then_inc(q["xhi"], 1)
                for c in range(2):
                    act.wait_ge(q["t_mm"], p * 4 + c + 3)
                    act.wait_ge(q["xlo"], p * 4 + 2)
                    act.activation(xT[:, c, :], psm[:, c, :], ACT.Identity, scale=lnp[:, c:c + 1], bias=lnp[:, 2 + c:3 + c]).then_inc(q["t_ev"], 1)
                act.wait_ge(q["t_ev"], p * 4 + 4)
                hold(act, tick)
                act.activation(pair(t["xnh"], p), xT[:, :, :], ACT.Copy).then_inc(q["xhi"], 1)
                act.wait_ge(q["r_mm"], p + 1)
                act.wait_ge(q["o_mm"], p)
                act.activation(rTh[:, :, :], psm[:, 2:5, :], ACT.Copy).then_inc(q["r_hi"], 1)
                act.wait_ge(q["dh_mm"], p + 1)
                act.wait_ge(q["dt_mm"], p)
                act.activation(dth[:, :], psm[:, 1, :], ACT.Copy).then_inc(q["dh_hi"], 1)
                act.wait_ge(q["u_mm"], p + 1)
                act.wait_ge(q["pad0"], 1)
                act.wait_ge(q["cv"], p * (DJ * KCONV))
                act.activation(up[:, :, :, PAD:].rearrange("p j s n -> p (j s) n"),
                               psm[:, 5:8, :].rearrange("p j (s n) -> p (j s) n", s=2), ACT.Copy).then_inc(q["u_ev"], 1)
                act.wait_ge(q["nz"], p + 1)
                hold(act, tick)
                act.activation(a, a, ACT.Exp).then_inc(q["ez"], 1)
                act.wait_ge(q["dm"], p * DJ + DJ)
                hold(act, tick)
                act.activation(b, b, ACT.Exp).then_inc(q["de"], 1)
                act.wait_ge(q["dd"], p * 3 + 1)
                act.wait_ge(q["yi"], p * 4)
                hold(act, tick)
                act.activation(pair(t["dt"], p), a, ACT.Ln).then_inc(q["dl"], 1)

        @block.vector
        def _(dve):
            dve.wait_ge(q["rhi"], 1)
            dve.tensor_tensor(rlo[:, :, :], rraw, rhi[:, :, :], ALU.subtract).then_inc(q["rlo"], 1)
            dve.wait_ge(q["ohi"], 1)
            dve.tensor_tensor(olo[:, :, :], oraw, ohi[:, :, :], ALU.subtract).then_inc(q["olo"], 1)
            dve.wait_ge(q["dhi"], 1)
            dve.tensor_tensor(dlo[:, :], u[:, 0, 0:DI], dhi[:, :], ALU.subtract).then_inc(q["dlo"], 1)
            dve.wait_ge(q["par_in"], 32)
            for m in ("rlo", "olo", "dlo"):
                dve.wait_ge(q[m], 1)
            dve.wait_ge(q["wlo"], 1)
            with dve.Fori(0, PAIRS) as p:
                a, b = pair(t["y"], p), pair(t["dtu"], p)
                res = t["res"][:, bass.ds(NT2 * p, NT2), :]
                dve.wait_ge(q["t_mm"], p * 4)
                layernorm_tokens(dve, tick, res, x1, st, mv, rs[:, :, :], v[:, :, :], w[:, :, :], q["st1"], q["ag1"], q["rs1"], q["x1"], p, NT2)
                dve.wait_ge(q["x1"], p * (NT2 + 1) + NT2 + 1)
                layernorm_tokens(dve, tick, x1[:, :, 0:D], x2, st, mv, rs[:, :, :], v[:, :, :], w[:, :, :], q["st2"], q["ag2"], q["rs2"], q["x2"], p, NT2)
                dve.wait_ge(q["xhi"], p * 2 + 1)
                dve.tensor_tensor(xl[:, :], xT[:, 0, :], xh[:, 0, :], ALU.subtract).then_inc(q["xlo"], 1)
                dve.tensor_tensor(xh[P // 2:, 1, :], xT[P // 2:, 1, :], xh[P // 2:, 1, :], ALU.subtract).then_inc(q["xlo"], 1)
                dve.wait_ge(q["xhi"], p * 2 + 2)
                dve.tensor_tensor(t["xnl"][:, bass.ds(p * TOK2, TOK2)], xT[:, 0, :], t["xnh"][:, 0, bass.ds(p * TOK2, TOK2)],
                                  ALU.subtract).then_inc(q["xlo"], 1)
                s1 = t["xnh"][P // 2:, 1, bass.ds(p * TOK2, TOK2)]
                dve.tensor_tensor(s1, xT[P // 2:, 1, :], s1, ALU.subtract).then_inc(q["xlo"], 1)
                dve.wait_ge(q["r_hi"], p + 1)
                dve.tensor_tensor(rTl[:, :, :], psm[:, 2:5, :], rTh[:, :, :], ALU.subtract).then_inc(q["r_lo"], 1)
                dve.wait_ge(q["dh_hi"], p + 1)
                dve.tensor_tensor(dth[P // 2:, :], psm[P // 2:, 1, :], dth[P // 2:, :], ALU.subtract).then_inc(q["dh_lo"], 1)
                dve.wait_ge(q["z_mm"], p + 1)
                dve.wait_ge(q["dl"], p)
                dve.tensor_scalar(a, psm[:, 2:5, :], -1.0, 80.0, ALU.mult, ALU.min).then_inc(q["nz"], 1)
                dve.wait_ge(q["ez"], p + 1)
                dve.tensor_scalar(a, a, 1.0, None, ALU.add).then_inc(q["sz"], 1)
                dve.wait_ge(q["sz"], p * 3 + 1)
                hold(dve, tick)
                dve.reciprocal(u[:, :, :], a).then_inc(q["sz"], 1)
                dve.wait_ge(q["sz"], p * 3 + 2)
                dve.tensor_tensor(pair(t["zs"], p), psm[:, 2:5, :], u[:, :, :], ALU.mult).then_inc(q["sz"], 1)
                dve.wait_ge(q["u_ev"], p + 1)
                dve.wait_ge(q["sz"], p * 3 + 3)
                for k in range(KCONV):
                    if k:
                        dve.wait_ge(q["cv"], p * (DJ * KCONV) + k * DJ)
                    for j in range(DJ):
                        src, dst = up[:, j, :, k:k + S], u[:, j, :].rearrange("p (s n) -> p s n", s=2)
                        wk = par[:, SP_CW + j * KCONV + k:SP_CW + j * KCONV + k + 1]
                        if k == 0:
                            i = dve.tensor_scalar(dst, src, wk, par[:, SP_CB + j:SP_CB + j + 1], ALU.mult, ALU.add)
                        else:
                            i = dve.scalar_tensor_tensor(dst, src, wk, dst, ALU.mult, ALU.add)
                        i.then_inc(q["cv"], 1)
                dve.wait_ge(q["dt_mm"], p + 1)
                dve.wait_ge(q["dc"], p * 2)
                for j in range(DJ):
                    dve.tensor_scalar(t["dtu"][:, j, bass.ds(p * TOK2, TOK2)], psm[:, 2 + j, :], par[:, SP_DTB + j:SP_DTB + j + 1], 20.0, ALU.add, ALU.min).then_inc(q["dm"], 1)
                dve.wait_ge(q["de"], p + 1)
                dve.tensor_scalar(a, b, 1.0, None, ALU.add).then_inc(q["dd"], 1)
                dve.wait_ge(q["dd"], p * 3 + 1)
                dve.wait_ge(q["r_lo"], p + 1)
                dve.tensor_scalar(up[:, :, :, 0:S], a.rearrange("p j (s n) -> p j s n", s=2),
                                  -1.0, 1e-30, ALU.add, ALU.max).then_inc(q["dd"], 1)
                dve.wait_ge(q["dl"], p + 1)
                dve.wait_ge(q["dd"], p * 3 + 2)
                hold(dve, tick)
                dve.reciprocal(a.rearrange("p j (s n) -> p j s n", s=2), up[:, :, :, 0:S]).then_inc(q["dd"], 1)
                dve.wait_ge(q["dd"], p * 3 + 3)
                dve.tensor_tensor(b, b, a, ALU.mult).then_inc(q["dc"], 1)
                dve.wait_ge(q["dc"], p * 2 + 1)
                dt = pair(t["dt"], p)
                dve.tensor_tensor(a, dt, b, ALU.mult).then_inc(q["dc"], 1)
                dve.wait_ge(q["dc"], p * 2 + 2)
                dve.tensor_scalar(dt, a, DT_MIN, DT_MAX, ALU.max, ALU.min).then_inc(q["yi"], 1)
                dve.wait_ge(q["yi"], p * 4 + 1)
                dve.tensor_tensor(pair(t["dtu"], p), dt, u[:, :, :], ALU.mult).then_inc(q["out"], 1)
                for j in range(DJ):
                    dve.tensor_scalar(t["y"][:, j, bass.ds(p * TOK2, TOK2)], u[:, j, :], par[:, SP_D + j:SP_D + j + 1], None, ALU.mult).then_inc(q["yi"], 1)
                dve.wait_ge(q["dd"], p * 3 + 3)
                dve.memset(up[:, :, :, 0:PAD], 0.0).then_inc(q["out"], 1)
                dve.wait_ge(q["o_mm"], p + 1)
                dve.tensor_tensor(res, psm[:, 4:8, 0:D], res, ALU.add).then_inc(q["res"], 1)

        @block.tensor
        def _(pe):
            for m in ("wlo", "rlo", "olo", "dlo"):
                pe.wait_ge(q[m], 1)
            with pe.Fori(0, PAIRS) as p:
                for k, (x, ready) in enumerate(((x1, "x1"), (x2, "x2"))):
                    pe.wait_ge(q[ready], p * (NT2 + 1) + NT2 + 1)
                    if k == 0:
                        pe.wait_ge(q["dh_lo"], p)
                        pe.wait_ge(q["t_ev"], p * 4)
                    else:
                        pe.wait_ge(q["t_ev"], p * 4 + 2)
                    for c in range(2):
                        for i in range(NT2):
                            last = pe.transpose(psm[:, c, i * P:(i + 1) * P], x[:, i, c * P:(c + 1) * P], t["ident"][:, :])
                        last.then_inc(q["t_mm"], 1)
                pe.wait_ge(q["xlo"], p * 4 + 2)
                pe.wait_ge(q["dm"], p * DJ)
                pe.wait_ge(q["res"], p)
                for j in range(DJ):
                    last = five_passes(pe, psm[:, 2 + j, :], rhi, rlo, slice(j * P, (j + 1) * P), xh, xl, slice(0, TOK2))
                last.then_inc(q["r_mm"], 1)
                pe.wait_ge(q["xlo"], p * 4 + 4)
                pe.wait_ge(q["t_ev"], p * 4 + 4)
                for j in range(DJ + 1):
                    out, col = (psm[:, 1, :], WDT) if j == DJ else (psm[:, 5 + j, :], WU + j * P)
                    cols = slice(col, col + P)
                    terms = [(whi[:, 0, cols], t["xnh"][:, 0, bass.ds(p * TOK2, TOK2)]), (wlo[:, 0, cols], t["xnh"][:, 0, bass.ds(p * TOK2, TOK2)]),
                             (whi[:, 0, cols], t["xnl"][:, bass.ds(p * TOK2, TOK2)]),
                             (whi[:, 1, cols], t["xnh"][:, 1, bass.ds(p * TOK2, TOK2)]), (wlo[:, 1, cols], t["xnh"][:, 1, bass.ds(p * TOK2, TOK2)])]
                    for i, (w_, x_) in enumerate(terms):
                        last = pe.matmul(out, w_, x_, start=i == 0, stop=i == 4)
                    if j >= DJ - 1:
                        last.then_inc(q["u_mm" if j == DJ - 1 else "dh_mm"], 1)
                pe.wait_ge(q["r_lo"], p + 1)
                for j in range(DJ):
                    cols = slice(WZ + j * P, WZ + (j + 1) * P)
                    terms = [(whi[:, 0, cols], t["xnh"][:, 0, bass.ds(p * TOK2, TOK2)]), (wlo[:, 0, cols], t["xnh"][:, 0, bass.ds(p * TOK2, TOK2)]),
                             (whi[:, 0, cols], t["xnl"][:, bass.ds(p * TOK2, TOK2)]),
                             (whi[:, 1, cols], t["xnh"][:, 1, bass.ds(p * TOK2, TOK2)]), (wlo[:, 1, cols], t["xnh"][:, 1, bass.ds(p * TOK2, TOK2)])]
                    for i, (w_, x_) in enumerate(terms):
                        last = pe.matmul(psm[:, 2 + j, :], w_, x_, start=i == 0, stop=i == 4)
                last.then_inc(q["z_mm"], 1)
                pe.wait_ge(q["dh_lo"], p + 1)
                pe.wait_ge(q["sz"], p * 3 + 3)
                for j in range(DJ):
                    cols = slice(j * P, (j + 1) * P)
                    pe.matmul(psm[:, 2 + j, :], dhi[:, cols], dth[:, :], start=True, stop=False)
                    last = pe.matmul(psm[:, 2 + j, :], dlo[:, cols], dth[:, :], start=False, stop=True)
                last.then_inc(q["dt_mm"], 1)
                pe.wait_ge(q["u_ev"], p + 1)
                pe.wait_ge(q["dm"], p * DJ + DJ)
                for i in range(NT2):
                    out = psm[:, 4 + i, 0:D]
                    for j in range(DJ):
                        tk = slice(i * P, (i + 1) * P)
                        pe.matmul(out, rTh[:, j, tk], ohi[:, j, :], start=j == 0, stop=False)
                        pe.matmul(out, rTh[:, j, tk], olo[:, j, :], start=False, stop=False)
                        last = pe.matmul(out, rTl[:, j, tk], ohi[:, j, :], start=False, stop=j == DJ - 1)
                last.then_inc(q["o_mm"], 1)


def scan_phase(nc, io, t):
    with ExitStack() as ctx:
        def sb(name, shape, dt=F32):
            return ctx.enter_context(nc.sbuf_tensor(name, shape, dt))

        def sem(name):
            return nc.alloc_semaphore("sc_" + name)

        tick = sem("tick")

        raw = sb("sc_raw", [P, 2, 2, 2, P])
        whi, wlo = sb("sc_whi", [P, 2, 2, 2, P], F32R), sb("sc_wlo", [P, 2, 2, 2, P], F32R)
        al = sb("sc_a", [P, DJ, NS])
        w_in = [sem(f"w_in{k}") for k in range(2)]
        R = 4
        dA, dB, hs, hc = (sb(f"sc_{n}", [P, R, TOK2]) for n in ("dA", "dB", "h", "hc"))
        psB = ctx.enter_context(nc.psum_tensor("sc_psB", [P, 4, 512], F32))
        psC = ctx.enter_context(nc.psum_tensor("sc_psC", [P, 4, 512], F32))
        q = {n: sem(n) for n in ("a_in", "a_neg", "whi", "wlo", "b_mm", "c_mm", "dA", "dB", "scan", "hc", "y")}
        block = ctx.enter_context(nc.Block())
        J2 = NS // 2

        @block.sync
        def _(sp):
            sp.dma_start(al[:, :, :], io["s_alog"]).then_inc(q["a_in"], 16)
            with sp.Fori(0, DJ * J2) as g:
                for k in range(2):
                    i = g * 2 + k
                    sp.wait_ge(q["wlo"], g * 2)
                    sp.dma_start(raw[:, k, :, :, :], io["s_wbc"][i, :, :]).then_inc(w_in[k], 16)

        @block.scalar
        def _(act):
            act.wait_ge(q["a_in"], 16)
            act.activation(al[:, :, :], al[:, :, :], ACT.Exp).then_inc(q["a_neg"], 1)
            act.wait_ge(q["a_neg"], 2)
            with act.Fori(0, DJ) as j:
                with act.Fori(0, J2) as m:
                    g = j * J2 + m
                    for k in range(2):
                        act.wait_ge(w_in[k], g * 16 + 16)
                        act.wait_ge(q["c_mm"], g * 8)
                        act.activation(whi[:, k, :, :, :], raw[:, k, :, :, :], ACT.Copy).then_inc(q["whi"], 1)
                    for k in range(2):
                        act.wait_ge(q["scan"], g * 16 + k * 8)
                        hold(act, tick)
                        for pr in range(PAIRS):
                            act.activation(dA[:, pr, :], t["dt"][:, bass.ds(j, 1), pr * TOK2:(pr + 1) * TOK2].rearrange("p a n -> p (a n)"), ACT.Exp,
                                           scale=al[:, bass.ds(j, 1), bass.ds(m * 2 + k, 1)].rearrange("p a b -> p (a b)")).then_inc(q["dA"], 1)

        @block.gpsimd
        def _(pool):
            with pool.Fori(0, DJ) as j:
                with pool.Fori(0, J2) as m:
                    g = j * J2 + m
                    for k in range(2):
                        pool.wait_ge(q["whi"], g * 2 + k + 1)
                        pool.tensor_tensor(wlo[:, k, :, :, :], raw[:, k, :, :, :], whi[:, k, :, :, :], ALU.subtract).then_inc(q["wlo"], 1)
                    for k in range(2):
                        for pr in range(PAIRS):
                            i = g * 8 + k * PAIRS + pr
                            y = t["y"][:, bass.ds(j, 1), pr * TOK2:(pr + 1) * TOK2].rearrange("p a n -> p (a n)")
                            pool.wait_ge(q["hc"], i + 1)
                            pool.wait_ge(q["y"], g * 8 + k * PAIRS)
                            hold(pool, tick)
                            pool.tensor_tensor(y, y, hc[:, pr, :], ALU.add).then_inc(q["y"], 1)

        @block.vector
        def _(dve):
            dve.wait_ge(q["a_neg"], 1)
            dve.tensor_scalar(al[:, :, :], al[:, :, :], -1.0, None, ALU.mult).then_inc(q["a_neg"], 1)
            with dve.Fori(0, DJ) as j:
                with dve.Fori(0, J2) as m:
                    g = j * J2 + m

                    def input_(k, pr):
                        i = g * 8 + k * PAIRS + pr
                        dve.wait_ge(q["b_mm"], i + 1)
                        dve.tensor_tensor(dB[:, pr, :], psB[:, pr, :], t["dtu"][:, bass.ds(j, 1), pr * TOK2:(pr + 1) * TOK2].rearrange("p a n -> p (a n)"),
                                          ALU.mult).then_inc(q["dB"], 1)

                    def scan(k, pr):
                        i = g * 8 + k * PAIRS + pr
                        dve.wait_ge(q["dB"], i + 1)
                        dve.wait_ge(q["dA"], i + 1)
                        for s_ in range(2):
                            c = slice(s_ * S, (s_ + 1) * S)
                            dve.tensor_tensor_scan(hs[:, pr, c], dA[:, pr, c], dB[:, pr, c], 0.0, ALU.mult, ALU.add).then_inc(q["scan"], 1)

                    def output(k, pr):
                        i = g * 8 + k * PAIRS + pr
                        dve.wait_ge(q["scan"], i * 2 + 2)
                        dve.wait_ge(q["c_mm"], i + 1)
                        dve.wait_ge(q["y"], g * 8 + k * PAIRS)
                        dve.tensor_tensor(hc[:, pr, :], hs[:, pr, :], psC[:, pr, :], ALU.mult).then_inc(q["hc"], 1)

                    for k in range(2):
                        for step in range(PAIRS + 2):
                            if step < PAIRS:
                                input_(k, step)
                            if 0 <= step - 1 < PAIRS:
                                scan(k, step - 1)
                            if step - 2 >= 0:
                                output(k, step - 2)

        @block.tensor
        def _(pe):
            with pe.Fori(0, DJ * J2) as g:
                for k in range(2):
                    pe.wait_ge(q["wlo"], g * 2 + k + 1)
                    for pr in range(PAIRS):
                        cols = slice(pr * TOK2, (pr + 1) * TOK2)
                        pe.wait_ge(q["dB"], g * 8 + (pr + 1 if k else 0))
                        five_passes(pe, psB[:, pr, :], whi[:, k, 0, :, :], wlo[:, k, 0, :, :], slice(0, P), t["xnh"], t["xnl"], cols).then_inc(q["b_mm"], 1)
                        pe.wait_ge(q["hc"], g * 8 + (pr + 1 if k else 0))
                        five_passes(pe, psC[:, pr, :], whi[:, k, 1, :, :], wlo[:, k, 1, :, :], slice(0, P), t["xnh"], t["xnl"], cols).then_inc(q["c_mm"], 1)


def scan_output_phase(nc, io, t):
    with ExitStack() as ctx:
        def sb(name, shape, dt=F32):
            return ctx.enter_context(nc.sbuf_tensor(name, shape, dt))

        def sem(name):
            return nc.alloc_semaphore("so_" + name)

        oraw = sb("so_oraw", [P, DJ, D])
        ohi, olo = sb("so_ohi", [P, DJ, D], F32R), sb("so_olo", [P, DJ, D], F32R)
        par = sb("so_par", [P, NSPAR])
        ones = sb("so_ones", [P, 1])
        gm = [sb(f"so_g{x}", [P, DJ, TOK2]) for x in range(2)]
        sq = sb("so_sq", [P, DJ, TOK2])
        gh, gl = sb("so_gh", [P, DJ, TOK2], F32R), sb("so_gl", [P, DJ, TOK2], F32R)
        ms, rr, v, w = (sb(f"so_{n}", [P, NT2, 1]) for n in ("ms", "rr", "v", "w"))
        psq = ctx.enter_context(nc.psum_tensor("so_psq", [P, NT2], F32))
        pso = ctx.enter_context(nc.psum_tensor("so_pso", [P, 4, 512], F32))
        q = {n: sem(n) for n in ("o_in", "ohi", "olo", "one", "g", "sq", "hi", "lo", "ss", "ms", "rs", "mm", "res")}
        block = ctx.enter_context(nc.Block())

        @block.sync
        def _(sp):
            sp.dma_start(oraw[:, :, :], io["s_wout"]).then_inc(q["o_in"], 16)
            sp.dma_start(par[:, :], io["s_params"]).then_inc(q["o_in"], 16)

        @block.gpsimd
        def _(pool):
            pool.memset(ones[:, :], 1.0).then_inc(q["one"], 1)

        @block.scalar
        def _(act):
            act.wait_ge(q["o_in"], 32)
            act.activation(ohi[:, :, :], oraw[:, :, :], ACT.Copy).then_inc(q["ohi"], 1)
            for p in range(PAIRS):
                g = gm[p % 2]
                act.wait_ge(q["g"], p + 1)
                if p:
                    act.wait_ge(q["ss"], p)
                act.activation(sq[:, :, :], g[:, :, :], ACT.Square).then_inc(q["sq"], 1)
                if p:
                    act.wait_ge(q["mm"], p)
                for j in range(DJ):
                    act.activation(gh[:, j, :], g[:, j, :], ACT.Copy, scale=par[:, SP_NW + j:SP_NW + j + 1]).then_inc(q["hi"], 1)

        @block.vector
        def _(dve):
            dve.wait_ge(q["ohi"], 1)
            dve.tensor_tensor(olo[:, :, :], oraw[:, :, :], ohi[:, :, :], ALU.subtract).then_inc(q["olo"], 1)
            for p in range(PAIRS):
                g = gm[p % 2]
                if p >= 2:
                    dve.wait_ge(q["sq"], p - 1)
                    dve.wait_ge(q["hi"], DJ * (p - 1))
                cols = slice(p * TOK2, (p + 1) * TOK2)
                dve.tensor_tensor(g[:, :, :], t["y"][:, :, cols], t["zs"][:, :, cols], ALU.mult).then_inc(q["g"], 1)
                for j in range(DJ):
                    dve.wait_ge(q["hi"], DJ * p + j + 1)
                    dve.scalar_tensor_tensor(gl[:, j, :], g[:, j, :], par[:, SP_NW + j:SP_NW + j + 1], gh[:, j, :], ALU.mult, ALU.subtract).then_inc(q["lo"], 1)
                dve.wait_ge(q["ss"], p + 1)
                dve.tensor_scalar(ms[:, :, :], psq[:, :].unsqueeze(2), 1.0 / DI, None, ALU.mult).then_inc(q["ms"], 1)
                dve.wait_ge(q["ms"], p + 1)
                rsqrt_steps(dve, q["rs"], p * RSQRT_STEPS, ms[:, :, :], rr[:, :, :], v[:, :, :], w[:, :, :], eps=1e-6)
                dve.wait_ge(q["mm"], p + 1)
                for i in range(NT2):
                    r = t["res"][:, NT2 * p + i, :]
                    dve.scalar_tensor_tensor(r, pso[:, i, 0:D], rr[:, i, :], r, ALU.mult, ALU.add).then_inc(q["res"], 1)

        @block.tensor
        def _(pe):
            pe.wait_ge(q["olo"], 1)
            pe.wait_ge(q["one"], 1)
            for p in range(PAIRS):
                pe.wait_ge(q["sq"], p + 1)
                if p:
                    pe.wait_ge(q["ms"], p)
                    pe.wait_ge(q["res"], NT2 * p)
                for i in range(NT2):
                    for j in range(DJ):
                        last = pe.matmul(psq[:, i:i + 1], sq[:, j, i * P:(i + 1) * P], ones[:, :], start=j == 0, stop=j == DJ - 1)
                last.then_inc(q["ss"], 1)
                pe.wait_ge(q["lo"], DJ * (p + 1))
                for i in range(NT2):
                    tk = slice(i * P, (i + 1) * P)
                    for j in range(DJ):
                        pe.matmul(pso[:, i, 0:D], gh[:, j, tk], ohi[:, j, :], start=j == 0, stop=False)
                        pe.matmul(pso[:, i, 0:D], gh[:, j, tk], olo[:, j, :], start=False, stop=False)
                        last = pe.matmul(pso[:, i, 0:D], gl[:, j, tk], ohi[:, j, :], start=False, stop=j == DJ - 1)
                last.then_inc(q["mm"], 1)


def gate_phase(nc, io, t):
    with ExitStack() as ctx:
        def sb(name, shape, dt=F32):
            return ctx.enter_context(nc.sbuf_tensor(name, shape, dt))

        def sem(name):
            return nc.alloc_semaphore("ga_" + name)

        tick = sem("tick")

        E, NB = EXPERTS, B * QB
        x3 = sb("ga_x", [P, NB, 2 * P])
        st, mv = sb("ga_st", [P, NB, 6]), sb("ga_mv", [P, NB, 2])
        rs, v, w = (sb(f"ga_{n}", [P, NB, 1]) for n in ("rs", "v", "w"))
        xT = [sb(f"ga_xT{i}", [P, 2, TOK2]) for i in range(2)]
        graw = sb("ga_graw", [P, 2, E])
        ghi, glo = sb("ga_ghi", [P, 2, E], F32R), sb("ga_glo", [P, 2, E], F32R)
        gb, b2 = sb("ga_gb", [P, E]), sb("ga_b2", [E, D])
        lg, pr, c1, c2, rank = (sb(f"ga_{n}", [P, NB, E]) for n in ("lg", "pr", "c1", "c2", "rank"))
        m = sb("ga_m", [P, NB, 1])
        wT = sb("ga_wT", [E, NB, P])
        psx = ctx.enter_context(nc.psum_tensor("ga_psx", [P, 2, 2, 512], F32))
        psg = ctx.enter_context(nc.psum_tensor("ga_psg", [P, NB, E], F32))
        pst = ctx.enter_context(nc.psum_tensor("ga_pst", [E, 512], F32))
        psb = ctx.enter_context(nc.psum_tensor("ga_psb", [P, 2, 512], F32))
        q = {n: sem(n) for n in ("in", "ghi", "glo", "rank", "st", "ag", "rs", "x", "t_mm", "t_ev", "hi", "lo", "g_mm", "k", "exp",
                                 "wt_mm", "wt_ev", "b_mm", "res")}
        block = ctx.enter_context(nc.Block())

        @block.sync
        def _(sp):
            sp.dma_start(graw[:, :, :], io["g_w"]).then_inc(q["in"], 16)
            sp.dma_start(gb[:, :], io["g_b"].partition_broadcast(P)).then_inc(q["in"], 16)
            sp.dma_start(b2[:, :], io["g_b2"]).then_inc(q["in"], 16)

        @block.gpsimd
        def _(pool):
            for e in range(E):
                pool.memset(rank[:, :, e:e + 1], float(E - e)).then_inc(q["rank"], 1)

        @block.scalar
        def _(act):
            act.wait_ge(q["in"], 48)
            act.activation(ghi[:, :, :], graw[:, :, :], ACT.Copy).then_inc(q["ghi"], 1)
            for p in range(PAIRS):
                x = xT[p % 2]
                act.wait_ge(q["t_mm"], p + 1)
                if p >= 2:
                    act.wait_ge(q["lo"], 2 * (p - 1))
                act.activation(x[:, :, :], psx[:, p % 2, :, :], ACT.Copy).then_inc(q["t_ev"], 1)
                act.wait_ge(q["t_ev"], p + 1)
                act.activation(t["xnh"][:, :, p * TOK2:(p + 1) * TOK2], x[:, :, :], ACT.Copy).then_inc(q["hi"], 1)
            act.wait_ge(q["k"], 3)
            act.activation(pr[:, :, :], lg[:, :, :], ACT.Exp).then_inc(q["exp"], 1)
            for i in range(NB // 4):
                act.wait_ge(q["wt_mm"], i + 1)
                act.activation(wT[:, 4 * i:4 * i + 4, :], pst[:, :].rearrange("e (b n) -> e b n", b=4), ACT.Copy).then_inc(q["wt_ev"], 1)

        @block.vector
        def _(dve):
            dve.wait_ge(q["ghi"], 1)
            dve.tensor_tensor(glo[:, :, :], graw[:, :, :], ghi[:, :, :], ALU.subtract).then_inc(q["glo"], 1)
            layernorm_tokens(dve, tick, t["res"], x3, st, mv, rs[:, :, :], v[:, :, :], w[:, :, :], q["st"], q["ag"], q["rs"], q["x"], 0, NB)
            for p in range(PAIRS):
                x, cols = xT[p % 2], slice(p * TOK2, (p + 1) * TOK2)
                dve.wait_ge(q["hi"], p + 1)
                dve.tensor_tensor(t["xnl"][:, cols], x[:, 0, :], t["xnh"][:, 0, cols], ALU.subtract).then_inc(q["lo"], 1)
                s1 = t["xnh"][P // 2:, 1, cols]
                dve.tensor_tensor(s1, x[P // 2:, 1, :], s1, ALU.subtract).then_inc(q["lo"], 1)
            n = 0

            def step(instruction):
                nonlocal n
                n += 1
                instruction.then_inc(q["k"], 1)
                dve.wait_ge(q["k"], n)

            def over_e(x):
                return x.to_broadcast([P, NB, E])

            dve.wait_ge(q["g_mm"], 1)
            dve.wait_ge(q["in"], 48)
            step(dve.tensor_tensor(lg[:, :, :], psg[:, :, :], gb[:, :].unsqueeze(1).to_broadcast([P, NB, E]), ALU.add))
            step(dve.tensor_reduce(m[:, :, :], lg[:, :, :], AX, ALU.max))
            step(dve.tensor_tensor(lg[:, :, :], lg[:, :, :], over_e(m[:, :, :]), ALU.subtract))
            dve.wait_ge(q["exp"], 1)
            step(dve.tensor_reduce(m[:, :, :], pr[:, :, :], AX, ALU.add))
            step(dve.reciprocal(w[:, :, :], m[:, :, :]))
            step(dve.tensor_tensor(pr[:, :, :], pr[:, :, :], over_e(w[:, :, :]), ALU.mult))
            dve.wait_ge(q["rank"], E)
            for best in range(2):
                step(dve.tensor_reduce(m[:, :, :], pr[:, :, :], AX, ALU.max))
                step(dve.tensor_tensor(c1[:, :, :], pr[:, :, :], over_e(m[:, :, :]), ALU.is_equal))
                step(dve.tensor_tensor(c1[:, :, :], c1[:, :, :], rank[:, :, :], ALU.mult))
                step(dve.tensor_reduce(m[:, :, :], c1[:, :, :], AX, ALU.max))
                step(dve.tensor_tensor(c1[:, :, :], c1[:, :, :], over_e(m[:, :, :]), ALU.is_equal))
                dst = c2 if best == 0 else lg
                step(dve.tensor_tensor(dst[:, :, :], pr[:, :, :], c1[:, :, :], ALU.mult))
                if best == 0:
                    step(dve.scalar_tensor_tensor(c1[:, :, :], c1[:, :, :], 2.0, pr[:, :, :], ALU.mult, ALU.subtract))
                    step(dve.tensor_scalar(pr[:, :, :], c1[:, :, :], -1.0, None, ALU.mult))
                else:
                    step(dve.tensor_tensor(c2[:, :, :], c2[:, :, :], lg[:, :, :], ALU.add))
            step(dve.tensor_reduce(m[:, :, :], c2[:, :, :], AX, ALU.add))
            step(dve.reciprocal(w[:, :, :], m[:, :, :]))
            step(dve.tensor_tensor(t["tokw"][:, :, :], c2[:, :, :], over_e(w[:, :, :]), ALU.mult))
            for i in range(NB):
                dve.wait_ge(q["b_mm"], i + 1)
                r = t["res"][:, i, :]
                dve.tensor_tensor(r, psb[:, i % 2, 0:D], r, ALU.add).then_inc(q["res"], 1)

        @block.tensor
        def _(pe):
            pe.wait_ge(q["x"], NB + 1)
            for p in range(PAIRS):
                if p >= 2:
                    pe.wait_ge(q["t_ev"], p - 1)
                for c in range(2):
                    for i in range(NT2):
                        last = pe.transpose(psx[:, p % 2, c, i * P:(i + 1) * P], x3[:, NT2 * p + i, c * P:(c + 1) * P], t["ident"][:, :])
                last.then_inc(q["t_mm"], 1)
            pe.wait_ge(q["glo"], 1)
            pe.wait_ge(q["lo"], 2 * PAIRS)
            for i in range(NB):
                last = five_passes(pe, psg[:, i, :], ghi, glo, slice(0, E), t["xnh"], t["xnl"], slice(i * P, (i + 1) * P), feature_major=False)
            last.then_inc(q["g_mm"], 1)
            pe.wait_ge(q["k"], 24)
            for i in range(NB // 4):
                if i:
                    pe.wait_ge(q["wt_ev"], i)
                for b in range(4):
                    last = pe.matmul(pst[:, b * P:(b + 1) * P], t["tokw"][:, 4 * i + b, :], t["ident"][:, :], start=True, stop=True)
                last.then_inc(q["wt_mm"], 1)
            pe.wait_ge(q["wt_ev"], NB // 4)
            for i in range(NB):
                if i >= 2:
                    pe.wait_ge(q["res"], i - 1)
                pe.matmul(psb[:, i % 2, 0:D], wT[:, i, :], b2[:, :], start=True, stop=True).then_inc(q["b_mm"], 1)


def expert_phase(nc, io, t, out):
    with ExitStack() as ctx:
        def sb(name, shape, dt=F32):
            return ctx.enter_context(nc.sbuf_tensor(name, shape, dt))

        def sem(name):
            return nc.alloc_semaphore("ex_" + name)

        tick = sem("tick")

        W1 = 2 * HID
        NW = W1 + HC * D
        raw = sb("ex_raw", [P, NW])
        whi, wlo = sb("ex_whi", [P, 2, NW], F32R), sb("ex_wlo", [P, 2, NW], F32R)
        b1 = sb("ex_b1", [P, EXPERTS, HC])
        b1e = sb("ex_b1e", [P, 2, HC])
        R = 4
        hr = sb("ex_hr", [P, R, TOK2])
        hh, hl = sb("ex_hh", [P, 2, HC, TOK2], F32R), sb("ex_hl", [P, 2, HC, TOK2], F32R)
        psh = ctx.enter_context(nc.psum_tensor("ex_psh", [P, R, 512], F32))
        psy = ctx.enter_context(nc.psum_tensor("ex_psy", [P, NT2, 512], F32))
        q = {n: sem(n) for n in ("b_in", "b1e", "w_in", "whi", "wlo", "h_mm", "relu", "hi", "lo", "y_mm", "y", "stored")}
        block = ctx.enter_context(nc.Block())
        per = PAIRS * HC

        def w1(w, k):
            return w[:, k, 0:W1].rearrange("p (s n) -> p s n", s=2)

        def w2(w, k, c):
            return w[:, k, W1 + c * D:W1 + (c + 1) * D]

        @block.sync
        def _(sp):
            sp.dma_start(b1[:, :, :], io["e_b1"]).then_inc(q["b_in"], 16)
            with sp.Fori(0, EXPERTS) as e:
                sp.wait_ge(q["wlo"], e)
                sp.dma_start(raw[:, :], io["e_w"][e, :, :]).then_inc(q["w_in"], 16)
            sp.wait_ge(q["y"], EXPERTS * B * QB)
            sp.dma_start(out.rearrange("b (k p) d -> p (b k) d", p=P), t["res"][:, :, :]).then_inc(q["stored"], 16)
            sp.wait_ge(q["stored"], 16)

        @block.scalar
        def _(act):
            act.wait_ge(q["b_in"], 16)

            def split(e2, e, k):
                act.wait_ge(q["w_in"], e * 16 + 16)
                act.activation(whi[:, k, :], raw[:, :], ACT.Copy).then_inc(q["whi"], 1)
                act.wait_ge(q["relu"], e2 * (2 * per) + k * per)
                hold(act, tick)
                act.activation(b1e[:, k, :], b1[:, bass.ds(e, 1), :].rearrange("p a c -> p (a c)"), ACT.Copy).then_inc(q["b1e"], 1)
                act.wait_ge(q["b1e"], e + 1)

            with act.Fori(0, EXPERTS // 2) as e2:
                for k in range(2):
                    e = e2 * 2 + k
                    act.wait_ge(q["y_mm"], e2 * (2 * PAIRS))
                    split(e2, e, k)
                    for p in range(PAIRS):
                        for c in range(HC):
                            i = e * per + p * HC + c
                            act.wait_ge(q["h_mm"], i + 1)
                            act.wait_ge(q["lo"], e2 * (2 * per) + max(k * per + p * HC + c + 1 - R, 0))
                            act.activation(hr[:, (p * HC + c) % R, :], psh[:, (p * HC + c) % R, :], ACT.Relu,
                                           bias=b1e[:, k, c:c + 1]).then_inc(q["relu"], 1)

        @block.gpsimd
        def _(pool):
            with pool.Fori(0, EXPERTS // 2) as e2:
                for k in range(2):
                    pool.wait_ge(q["whi"], e2 * 2 + k + 1)
                    pool.tensor_tensor(wlo[:, k, :], raw[:, :], whi[:, k, :], ALU.subtract).then_inc(q["wlo"], 1)

        @block.vector
        def _(dve):
            with dve.Fori(0, EXPERTS // 2) as e2:
                for k in range(2):
                    e = e2 * 2 + k

                    def weigh(p):
                        dve.wait_ge(q["y_mm"], e * PAIRS + p + 1)
                        for i in range(NT2):
                            r = t["res"][:, NT2 * p + i, :]
                            dve.scalar_tensor_tensor(r, psy[:, i, 0:D], t["tokw"][:, NT2 * p + i, bass.ds(e, 1)], r, ALU.mult, ALU.add).then_inc(q["y"], 1)

                    for p in range(PAIRS):
                        for c in range(HC):
                            i = e * per + p * HC + c
                            src = hr[:, (p * HC + c) % R, :]
                            if c == 0:
                                n = k * PAIRS + p
                                dve.wait_ge(q["y_mm"], e2 * (2 * PAIRS) + max(n - 1, 0))
                            dve.wait_ge(q["relu"], i + 1)
                            dve.tensor_copy(hh[:, p % 2, c, :], src).then_inc(q["hi"], 1)
                            dve.wait_ge(q["hi"], i + 1)
                            dve.tensor_tensor(hl[:, p % 2, c, :], src, hh[:, p % 2, c, :], ALU.subtract).then_inc(q["lo"], 1)
                        weigh(p)

        @block.tensor
        def _(pe):
            with pe.Fori(0, EXPERTS // 2) as e2:
                for k in range(2):
                    e = e2 * 2 + k
                    pe.wait_ge(q["wlo"], e + 1)
                    for p in range(PAIRS):
                        cols = slice(p * TOK2, (p + 1) * TOK2)
                        for c in range(HC):
                            i = e * per + p * HC + c
                            pe.wait_ge(q["relu"], e2 * (2 * per) + max(k * per + p * HC + c + 1 - R, 0))
                            five_passes(pe, psh[:, (p * HC + c) % R, :], w1(whi, k), w1(wlo, k), slice(c * P, (c + 1) * P),
                                        t["xnh"], t["xnl"], cols).then_inc(q["h_mm"], 1)
                        pe.wait_ge(q["lo"], e * per + (p + 1) * HC)
                        pe.wait_ge(q["y"], (e * PAIRS + p) * NT2)
                        for i in range(NT2):
                            tk = slice(i * P, (i + 1) * P)
                            for c in range(HC):
                                pe.matmul(psy[:, i, 0:D], hh[:, p % 2, c, tk], w2(whi, k, c), start=c == 0, stop=False)
                                pe.matmul(psy[:, i, 0:D], hh[:, p % 2, c, tk], w2(wlo, k, c), start=False, stop=False)
                                last = pe.matmul(psy[:, i, 0:D], hl[:, p % 2, c, tk], w2(whi, k, c), start=False, stop=c == HC - 1)
                        last.then_inc(q["y_mm"], 1)


def host_layout(inp):
    def a(n):
        return np.asarray(inp[n])

    def fold(w):
        return np.stack([w[0:P], np.concatenate([w[P:], w[P:]])], axis=1)

    def fold_b(v):
        return fold(v[:, None])[:, :, 0]

    def by_dim(w):
        c = w.reshape(w.shape[:-1] + (HPC, 2, HD))
        return np.moveaxis(c, -3, -1).reshape(w.shape)

    out = {}
    out["ids"] = np.ascontiguousarray(a("x").reshape(B * QB, P).T)
    out["pos_ids"] = np.ascontiguousarray(a("pos_S").reshape(QB, P).T)
    mask = a("mask_BS_f1_0")
    out["mask_rows"] = mask
    out["mask_cols"] = np.ascontiguousarray(mask.reshape(B * QB, P).T)
    out["tok_emb"], out["pos_emb"] = a("L0_tok_tok_emb"), a("L0_tok_pos_emb")
    ws, ps, rs = [], [], []
    pb = a("L0_tok_c_proj_b")
    out["proj_b0"] = pb[0]
    for l in range(LAYERS):
        w = np.concatenate([by_dim(a("L0_tok_c_attn_w")[l][:, 0:D]), by_dim(a("L0_tok_c_attn_w")[l][:, D:2 * D]),
                            a("L0_tok_c_attn_w")[l][:, 2 * D:], a("L0_tok_c_proj_w")[l], a("L0_tok_c_fc_w")[l]], axis=1)
        m = a("L0_tok_mlp_proj_w")[l].reshape(HC, P, D).transpose(1, 0, 2)
        ws.append(np.concatenate([fold(w).reshape(P, -1), m.reshape(P, -1)], axis=1))
        par = np.zeros((P, NPAR), np.float32)
        bqkv = a("L0_tok_c_attn_b")[l]
        for c in range(2):
            par[0:CUT, PQ + c] = by_dim(bqkv[0:D])[c * CUT:(c + 1) * CUT]
            par[0:CUT, PK + c] = by_dim(bqkv[D:2 * D])[c * CUT:(c + 1) * CUT]
        par[:, PV_:PV_ + 2] = fold_b(bqkv[2 * D:])
        par[:, PL1W:PL1W + 2] = fold_b(a("L0_tok_ln1_w")[l])
        par[:, PL1B:PL1B + 2] = fold_b(a("L0_tok_ln1_b")[l])
        par[:, PL2W:PL2W + 2] = fold_b(a("L0_tok_ln2_w")[l])
        par[:, PL2B:PL2B + 2] = fold_b(a("L0_tok_ln2_b")[l])
        par[:, PFC:] = a("L0_tok_c_fc_b")[l].reshape(HC, P).T
        ps.append(par)
        nxt = pb[l + 1] if l + 1 < LAYERS else np.zeros(D, np.float32)
        rs.append(np.stack([a("L0_tok_ln1_w")[l], a("L0_tok_ln1_b")[l], a("L0_tok_mlp_proj_b")[l],
                            a("L0_tok_ln2_w")[l], a("L0_tok_ln2_b")[l], nxt]))
    out["weights"] = np.stack(ws)
    out["params"] = np.ascontiguousarray(np.stack(ps).transpose(1, 0, 2))
    out["rows"] = np.stack(rs)
    w_in = a("L0_attn_W_in")
    rank = np.zeros((D, P), np.float32)
    rank[:, 0:RANK] = w_in[2 * DI:2 * DI + RANK].T
    rank[:, P // 2:P // 2 + RANK] = w_in[2 * DI:2 * DI + RANK].T
    out["s_w"] = fold(np.concatenate([w_in[0:2 * DI].T, rank], axis=1))
    out["s_wres"] = fold(a("L0_attn_W_res").T)
    out["s_wout"] = a("L0_attn_W_out").T.reshape(DJ, P, D).transpose(1, 0, 2)
    wdt = np.zeros((P, DI), np.float32)
    wdt[0:RANK] = a("L0_attn_W_dt").T
    wdt[P // 2:P // 2 + RANK] = a("L0_attn_W_dt").T
    out["s_wdt"] = wdt

    def chan(v):
        return v.reshape(DJ, P).T

    cw = a("L0_attn_conv_w").reshape(DJ, P, KCONV).transpose(1, 0, 2).reshape(P, DJ * KCONV)
    out["s_params"] = np.concatenate([chan(a("L0_attn_" + n)) for n in ("dt_bias", "conv_b", "Dskip", "norm_w")] + [cw], axis=1)
    out["s_ln"] = np.concatenate([fold_b(a("L0_attn_ln_w")), fold_b(a("L0_attn_ln_b"))], axis=1)
    out["s_alog"] = a("L0_attn_A_log").reshape(DJ, P, NS).transpose(1, 0, 2)
    bc = w_in[2 * DI + RANK:].reshape(2, DJ, P, NS, D)
    bc = bc.transpose(1, 3, 4, 0, 2).reshape(DJ * NS, D, 2, P)
    out["s_wbc"] = np.concatenate([bc[:, 0:P], np.zeros_like(bc[:, 0:P])], axis=2).reshape(DJ * NS, P, 2, 2, P)
    out["s_wbc"][:, :, 0, 0], out["s_wbc"][:, :, 1, 0] = bc[:, 0:P, 0], bc[:, 0:P, 1]
    out["s_wbc"][:, 0:P // 2, :, 1], out["s_wbc"][:, P // 2:, :, 1] = bc[:, P:], bc[:, P:]
    out["s_wbc"] = out["s_wbc"].reshape(DJ * NS, P, 4 * P)
    out["g_w"] = fold(a("L0_ffn_gate_w").T)
    out["g_b"], out["g_b2"] = a("L0_ffn_gate_b"), a("L0_ffn_b2")
    out["e_b1"] = a("L0_ffn_b1").reshape(EXPERTS, HC, P).transpose(2, 0, 1)
    out["e_w"] = np.stack([np.concatenate([
        fold(a("L0_ffn_w1")[e].T).reshape(P, -1),
        a("L0_ffn_w2")[e].T.reshape(HC, P, D).transpose(1, 0, 2).reshape(P, -1)], axis=1) for e in range(EXPERTS)])
    return {k: np.ascontiguousarray(v) for k, v in out.items()}


def shared(nc, ctx):
    def sb(name, shape, dt=F32):
        return ctx.enter_context(nc.sbuf_tensor(name, shape, dt))

    return {
        "ident": sb("ident", [P, P]),
        "ident_b": sb("ident_b", [P, P], BF16),
        "trib": sb("trib", [P, P], BF16),
        "ext": sb("ext_cols", [P, B * QB]),
        "e10": sb("e10", [P, B * QB]),
        "res": sb("res", [P, B * QB, D]),
        "m1_dram": nc.dram_tensor("m1_dram", (B, P, 3 * P), F32, kind="Internal").ap(),
        "rows_dram": nc.dram_tensor("rows_dram", (LAYERS, 4, D), F32, kind="Internal").ap(),
        "wt_dram": nc.dram_tensor("wt_dram", (B, P, 3 * P), F32, kind="Internal").ap(),
    }


def tower_kernel(nc, io, out):
    with ExitStack() as ctx:
        t = shared(nc, ctx)

        def phase(build, *args):
            with nc.cleanup_on_exit():
                build(nc, io, t, *args)

        with ExitStack() as c1:
            t["hst"] = c1.enter_context(nc.sbuf_tensor("hst", [P, B, 2, S], F32))
            phase(setup_phase, LAYERS)
            phase(tower_phase, LAYERS)
        t["xnh"] = ctx.enter_context(nc.sbuf_tensor("xnh", [P, 2, B * S], F32R))
        t["xnl"] = ctx.enter_context(nc.sbuf_tensor("xnl", [P, B * S], F32R))
        t["tokw"] = ctx.enter_context(nc.sbuf_tensor("tokw", [P, B * QB, EXPERTS], F32))
        with ExitStack() as c2:
            for n in ("dt", "dtu", "zs", "y"):
                t[n] = c2.enter_context(nc.sbuf_tensor("sc_" + n + "_all", [P, DJ, B * S], F32))
            phase(scan_input_phase)
            phase(scan_phase)
            phase(scan_output_phase)
        phase(gate_phase)
        phase(expert_phase, out)


def kernel(**inputs):
    import concourse.bacc as _bacc
    from concourse.bass_utils import run_bass_kernel_spmd as _run

    arrays = host_layout(inputs)
    nc = _bacc.Bacc("TRN2", target_bir_lowering=False, num_devices=1)
    io = {k: nc.dram_tensor("in_" + k, v.shape, mybir.dt.from_np(v.dtype), kind="ExternalInput").ap() for k, v in arrays.items()}
    out = nc.dram_tensor("out_0_dram", (B, S, D), F32, kind="ExternalOutput").ap()
    tower_kernel(nc, io, out)
    r = _run(nc, [{"in_" + k: v for k, v in arrays.items()}], core_ids=[0])
    return r.results[0]["out_0_dram"]
```

```python
from contextlib import ExitStack

import numpy as np

import concourse.bass as bass
from concourse import mybir

F32 = mybir.dt.float32
F32R = mybir.dt.float32r
BF16 = mybir.dt.bfloat16
I32 = mybir.dt.int32
ALU = mybir.AluOpType
ACT = mybir.ActivationFunctionType
AX = mybir.AxisListType.X

B, S, D = 8, 256, 192
P = 128
LAYERS, HEADS = 5, 12
HD = D // HEADS
HID = 4 * D
QB = S // P
PAIRS = B // 2
HC = HID // P
DI, NS, RANK, KCONV = 384, 16, 48, 4
DJ = DI // P
EXPERTS = 8
SLOT = 32
HSLOT = P // SLOT
HT = HEADS // HSLOT
KROWS = 6 * HD
CUT = 96
HPC = CUT // HD
NEG = -2.0 ** 100
NEG2 = -2.0 ** 110
EPS = 1e-5
GELU_A = 0.044715
GELU_C = float(np.sqrt(2.0 / np.pi))

WQ, WK, WV, WO, WFC = 0, D, 2 * D, 3 * D, 4 * D
WCOLS = 4 * D + HID
W2COLS = HC * D
PQ, PK, PV_, PL1W, PL1B, PL2W, PL2B, PFC = 0, 2, 4, 6, 8, 10, 12, 14
NPAR = PFC + HC
R_L1W, R_L1B, R_MB, R_L2W, R_L2B, R_PB = range(6)

Q_PARTS = (0, 0, 0, 1, 1, 2)
K_PARTS = (0, 1, 2, 0, 1, 0)


RSQRT_STEPS = 11
FIRST = 1


def start_at_first(nc, semaphores):
    engines = (nc.sync, nc.gpsimd, nc.vector, nc.scalar, nc.tensor)
    for i, semaphore in enumerate(semaphores):
        engines[i % len(engines)].sem_inc(semaphore, FIRST)


def hold(eng, tick):
    eng.sem_inc(tick, 1)


def rsqrt_steps(eng, done, base, var, out, v, t, eps=EPS):
    n = base

    def step(instruction):
        nonlocal n
        instruction.then_inc(done, 1)
        n = n + 1
        eng.wait_ge(done, n)

    step(eng.tensor_scalar(v, var, eps, None, ALU.add))
    step(eng.tensor_scalar(out.bitcast(I32), v.bitcast(I32), -0.5, float(0x5F3759DF), ALU.mult, ALU.add))
    for _ in range(3):
        step(eng.scalar_tensor_tensor(t, out, -0.5, out, ALU.mult, ALU.mult))
        step(eng.tensor_tensor(t, t, v, ALU.mult))
        step(eng.scalar_tensor_tensor(out, t, 1.5, out, ALU.add, ALU.mult))


def setup_phase(nc, io, t, layers):
    with ExitStack() as ctx:
        def sb(name, shape, dt=F32):
            return ctx.enter_context(nc.sbuf_tensor(name, shape, dt))

        def sem(name):
            return nc.alloc_semaphore(name)

        NB = B * QB
        idx, pidx = sb("idx", [P, NB], I32), sb("pidx", [P, QB], I32)
        tok, pos = sb("tok", [P, NB, D]), sb("pos", [P, QB, D])
        htok = sb("htok", [P, NB, 2 * P])
        pb0 = sb("pb0", [P, D])
        lrow = sb("lrow", [LAYERS, 6, D])
        mrow, mcol = sb("mrow", [P, B, S]), sb("mcol", [P, B * QB])
        tri = sb("tri", [P, 3 * P])
        low = sb("low", [P, 3 * P])
        m1 = sb("m1", [P, B, 3 * P])
        fut = sb("fut", [P, B, 3 * P])
        emax, eneg = sb("emax", [P, B * QB]), sb("eneg", [P, B * QB])
        wt = sb("wt", [P, B, 3 * P])
        ps = [ctx.enter_context(nc.psum_tensor(f"set_ps{i}", [P, 512], F32)) for i in range(4)]
        idx_in, pidx_in, pb_in, mask_in = sem("idx_in"), sem("pidx_in"), sem("pb_in"), sem("mask_in")
        tok_in, pos_in = sem("tok_in"), sem("pos_in")
        zeroed, consts = sem("zeroed"), sem("consts")
        added, dup = sem("added"), sem("dup")
        ext, m1_done, fut_done, e_done, en_done = sem("ext"), sem("m1_done"), sem("fut_done"), sem("e_done"), sem("en_done")
        w_done, w_t, wt_done, h_t, h_done = sem("w_done"), sem("w_t"), sem("wt_done"), sem("h_t"), sem("h_done")
        stored, row_in, row_add = sem("stored"), sem("row_in"), sem("row_add")
        block = ctx.enter_context(nc.Block())

        @block.sync
        def _(sp):
            sp.dma_start(idx[:, :], io["ids"]).then_inc(idx_in, 16)
            sp.dma_start(pidx[:, :], io["pos_ids"]).then_inc(pidx_in, 16)
            sp.dma_start(pb0[:, :], io["proj_b0"].partition_broadcast(P)).then_inc(pb_in, 16)
            sp.dma_start(lrow[:, :, :], io["rows"]).then_inc(row_in, 16)
            sp.dma_start(mrow[:, :, :], io["mask_rows"].partition_broadcast(P)).then_inc(mask_in, 16)
            sp.dma_start(mcol[:, :], io["mask_cols"]).then_inc(mask_in, 16)
            sp.wait_ge(m1_done, 2 * B)
            sp.dma_start(t["m1_dram"].rearrange("b p n -> p b n"), m1[:, :, :]).then_inc(stored, 16)
            sp.wait_ge(wt_done, B)
            sp.dma_start(t["wt_dram"].rearrange("b p n -> p b n"), wt[:, :, :]).then_inc(stored, 16)
            sp.wait_ge(row_add, 2)
            for i, r in enumerate((R_L1W, R_L1B, R_L2W, R_L2B)):
                sp.dma_start(t["rows_dram"][:, i, :], lrow[:, r, :]).then_inc(stored, 16)
            sp.wait_ge(stored, 96)

        @block.gpsimd
        def _(pool):
            pool.memset(t["ident"][:, :], 0.0).then_inc(zeroed, 1)
            pool.memset(t["ident_b"][:, :], 0.0).then_inc(zeroed, 1)
            pool.memset(t["trib"][:, :], 0.0).then_inc(zeroed, 1)
            pool.memset(tri[:, :], 0.0).then_inc(zeroed, 1)
            pool.memset(low[:, :], 0.0).then_inc(zeroed, 1)
            pool.wait_ge(zeroed, 5)
            for m in (t["ident"], t["ident_b"]):
                pool.affine_select(out=m[:, :], in_=m[:, :], compare_op=ALU.not_equal, fill=1.0, base=0,
                                   pattern=[[-1, P]], channel_multiplier=1).then_inc(consts, 1)
            pool.affine_select(out=t["trib"][:, :], in_=t["trib"][:, :], compare_op=ALU.is_ge, fill=NEG2,
                               base=0, pattern=[[1, P]], channel_multiplier=-1).then_inc(consts, 1)
            for c in (0, 2):
                m = tri[:, c * P:(c + 1) * P]
                pool.affine_select(out=m, in_=m, compare_op=ALU.is_ge, fill=NEG2, base=0,
                                   pattern=[[-1, P]], channel_multiplier=1).then_inc(consts, 1)
                m = low[:, c * P:(c + 1) * P]
                pool.affine_select(out=m, in_=m, compare_op=ALU.is_gt, fill=NEG2, base=0,
                                   pattern=[[1, P]], channel_multiplier=-1).then_inc(consts, 1)
            pool.wait_ge(pidx_in, 16)
            for i in range(QB):
                pool.indirect_dma_start(pos[:, i, :], None, io["pos_emb"],
                                        bass.IndirectOffsetOnAxis(ap=pidx[:, i:i + 1], axis=0)).then_inc(pos_in, 16)
            pool.wait_ge(idx_in, 16)
            for i in range(NB):
                pool.indirect_dma_start(tok[:, i, :], None, io["tok_emb"],
                                        bass.IndirectOffsetOnAxis(ap=idx[:, i:i + 1], axis=0)).then_inc(tok_in, 16)

        @block.vector
        def _(dve):
            dve.wait_ge(row_in, 16)
            dve.tensor_tensor(lrow[:, R_L1B, :], lrow[:, R_L1B, :], lrow[:, R_MB, :], ALU.add).then_inc(row_add, 1)
            dve.tensor_tensor(lrow[:, R_L2B, :], lrow[:, R_L2B, :], lrow[:, R_PB, :], ALU.add).then_inc(row_add, 1)
            dve.wait_ge(mask_in, 32)
            dve.tensor_scalar(mrow[:, :, :], mrow[:, :, :], -NEG, NEG, ALU.mult, ALU.add).then_inc(ext, 1)
            dve.tensor_scalar(t["ext"][:, :], mcol[:, :], -NEG, NEG, ALU.mult, ALU.add).then_inc(ext, 1)
            dve.wait_ge(ext, 2)
            dve.wait_ge(consts, 7)
            for b in range(B):
                dve.tensor_tensor(m1[:, b, 0:P], mrow[:, b, 0:P], tri[:, 0:P], ALU.add).then_inc(m1_done, 1)
                dve.tensor_tensor(m1[:, b, P:], mrow[:, b, :], tri[:, P:], ALU.add).then_inc(m1_done, 1)
                dve.tensor_tensor(fut[:, b, 0:S], mrow[:, b, :], low[:, 0:S], ALU.add).then_inc(fut_done, 1)
                dve.tensor_tensor(fut[:, b, S:], mrow[:, b, P:], low[:, S:], ALU.add).then_inc(fut_done, 1)
                dve.wait_ge(fut_done, 2 * b + 2)
                dve.tensor_reduce(emax[:, 2 * b:2 * b + 1], fut[:, b, 0:S], AX, ALU.max).then_inc(e_done, 1)
                dve.tensor_reduce(emax[:, 2 * b + 1:2 * b + 2], fut[:, b, S:], AX, ALU.max).then_inc(e_done, 1)
            dve.wait_ge(e_done, 2 * B)
            dve.tensor_scalar(eneg[:, :], emax[:, :], -1.0, None, ALU.mult).then_inc(en_done, 1)
            dve.tensor_scalar(t["e10"][:, :], emax[:, :], -10000.0, None, ALU.add).then_inc(en_done, 1)
            for b in range(B):
                dve.wait_ge(w_t, b + 1)
                dve.tensor_copy(wt[:, b, :], ps[b % 2][:, 0:3 * P]).then_inc(wt_done, 1)
            dve.wait_ge(pos_in, 16 * QB)
            dve.wait_ge(tok_in, 16 * NB)
            dve.wait_ge(pb_in, 16)
            for i in range(NB):
                dve.tensor_tensor(htok[:, i, 0:D], tok[:, i, :], pos[:, i % QB, :], ALU.add).then_inc(added, 1)
                dve.wait_ge(added, i + 1)
                dve.tensor_copy(htok[:, i, D:], htok[:, i, P:D]).then_inc(dup, 1)
                dve.tensor_tensor(t["res"][:, i, :], htok[:, i, 0:D], pb0[:, :], ALU.add).then_inc(dup, 1)
            for b in range(B):
                dve.wait_ge(h_t, b + 1)
                dve.tensor_copy(t["hst"][:, b, :, :], ps[2 + b % 2][:, :].rearrange("p (s n) -> p s n", s=2)).then_inc(h_done, 1)

        @block.scalar
        def _(act):
            act.wait_ge(en_done, 2)
            for b in range(B):
                act.activation(fut[:, b, 0:S], fut[:, b, 0:S], ACT.Exp, bias=eneg[:, 2 * b:2 * b + 1]).then_inc(w_done, 1)
                act.activation(fut[:, b, S:], fut[:, b, S:], ACT.Exp, bias=eneg[:, 2 * b + 1:2 * b + 2]).then_inc(w_done, 1)

        @block.tensor
        def _(pe):
            pe.wait_ge(consts, 7)
            for b in range(B):
                pe.wait_ge(w_done, 2 * b + 2)
                if b >= 2:
                    pe.wait_ge(wt_done, b - 1)
                for c in range(3):
                    last = pe.transpose(ps[b % 2][:, c * P:(c + 1) * P], fut[:, b, c * P:(c + 1) * P], t["ident"][:, :])
                last.then_inc(w_t, 1)
            for b in range(B):
                pe.wait_ge(dup, 4 * b + 4)
                if b >= 2:
                    pe.wait_ge(h_done, b - 1)
                for s in range(2):
                    for q in range(QB):
                        last = pe.transpose(ps[2 + b % 2][:, s * S + q * P:s * S + (q + 1) * P],
                                            htok[:, QB * b + q, s * P:(s + 1) * P], t["ident"][:, :])
                last.then_inc(h_t, 1)


def tower_phase(nc, io, t, layers):
    with ExitStack() as ctx:
        def sb(name, shape, dt=F32):
            return ctx.enter_context(nc.sbuf_tensor(name, shape, dt))

        def both(name, shape, dt=F32):
            return [sb(f"{name}{x}", shape, dt) for x in range(2)]

        def sem(name):
            return nc.alloc_semaphore(name)

        def sems(*names):
            return {n: [sem(f"{n}_{x}") for x in range(2)] for n in names}

        wraw = sb("wraw", [P, 2 * WCOLS + W2COLS])
        whi = sb("whi", [P, 2 * WCOLS + W2COLS], F32R)
        wlo = sb("wlo", [P, 2 * WCOLS + W2COLS], F32R)
        rows = sb("rows", [P, 4, D])
        par = sb("par", [P, LAYERS, NPAR])
        parl = sb("parl", [P, NPAR])
        extp = sb("extp", [P, 2 * QB])

        xh, xl = both("xh", [P, 2, S], F32R), both("xl", [P, S], F32R)
        big, gl, gh = [], [], []
        for x in range(2):
            with nc.sbuf_tensor(f"big{x}", [P, HEADS * 3 * P], F32) as g:
                big.append(g)
            gl.append(sb(f"gl{x}", [P, HC, S], F32R))
            gh.append(sb(f"gh{x}", [P, HC, S], F32R))
            sb(f"big_rest{x}", [P, HEADS * 3 * P - 2 * HC * S])
        stk = both("stk", [P, 2 * HEADS * S], BF16)
        vtok = both("vtok", [P, QB, HEADS, SLOT])
        m1 = both("m1h", [P, 3 * P])
        wt = both("wth", [P, 3 * P])
        mmax = both("mmax", [P, QB, HEADS])
        negm = both("negm", [P, QB, HEADS])
        cpre, cfut = both("cpre", [P, QB, HEADS]), both("cfut", [P, QB, HEADS])
        mres, mtok = both("mres", [P, QB, HEADS]), both("mtok", [P, QB, 3, HEADS], BF16)
        mparts = both("mparts", [3 * HEADS, S], BF16)
        oT = both("oT", [P, HT, S])
        ufut = both("ufut", [P, QB, HEADS, HD + 1])
        otok = both("otok", [P, QB, HEADS, HD + 1])
        rden = both("rden", [P, QB, HEADS])
        xtok = both("xtok", [P, QB, 2 * P])
        xT = both("xT", [P, 2, S])
        ltok = both("ltok", [P, QB, D])
        lst, lmv, lrs = both("lst", [P, QB, 6]), both("lmv", [P, QB, 2]), both("lrs", [P, QB, 1])
        lwk = both("lwk", [P, 2, QB, 1])
        res2 = both("res2", [P, QB, D])
        ps = [[ctx.enter_context(nc.psum_tensor(f"ps{x}{i}", [P, 512], F32)) for i in range(4)] for x in range(2)]

        def w192(tile, slot, col, n):
            return tile[:, slot * WCOLS + col:slot * WCOLS + col + n]

        def w_attn(tile):
            return tile[:, 0:2 * WCOLS].rearrange("p (s n) -> p s n", s=2)[:, :, 0:WFC]

        def w_fc(tile):
            return tile[:, 0:2 * WCOLS].rearrange("p (s n) -> p s n", s=2)[:, :, WFC:]

        def w2(tile, c):
            return tile[:, 2 * WCOLS + c * D:2 * WCOLS + (c + 1) * D]

        qk, r1, prt, pt0, pt1, gx, gt, gg = [], [], [], [], [], [], [], []
        qs, ks = [], []
        for x in range(2):
            g = big[x]
            qk.append(g[0:CUT, 0:4 * S].rearrange("p (t n) -> p t n", t=4))
            r1.append(g[0:CUT, 4 * S:8 * S].rearrange("p (t n) -> p t n", t=4))
            prt.append(g[0:CUT, 8 * S:14 * S].bitcast(BF16).rearrange("p (r t n) -> p r t n", t=4, r=3))
            pt0.append(g[:, 0:HEADS * S].rearrange("p (h n) -> p h n", h=HEADS))
            pt1.append(g[:, HEADS * S:].rearrange("p (h n) -> p h n", h=HEADS))
            gx.append(g[:, 0:HC * S].rearrange("p (c n) -> p c n", c=HC))
            gt.append(g[:, HC * S:2 * HC * S].rearrange("p (c n) -> p c n", c=HC))
            gg.append(g[:, 2 * HC * S:3 * HC * S].rearrange("p (c n) -> p c n", c=HC))
            qs.append(stk[x][:, 0:HEADS * S].rearrange("p (h n) -> p h n", h=HEADS))
            ks.append(stk[x][:, HEADS * S:].rearrange("p (h n) -> p h n", h=HEADS))
        HG = HC // 2

        w_in, rows_in, par_in = sem("w_in"), sem("rows_in"), sem("par_in")
        w_hi, w_lo, par_ok, ext_ok = sem("w_hi"), sem("w_lo"), sem("par_ok"), sem("ext_ok")
        init, tick = sem("init"), sem("tick")
        s = sems("h_ready", "x_hi", "x_lo", "qk_mm", "v_mm", "qk32", "v32",
                 "p1", "rs1", "p2", "p3", "stacked", "v1_mm", "v1_rd", "mask_ld", "wt_ld", "mx", "nm", "cp", "cf",
                 "m_t", "mp", "m_ev", "m_st", "u_mm", "u_rd", "v2_mm", "pt", "pv_mm", "o_ev", "o_t", "o_rd", "den", "atok",
                 "a_t", "a_ev", "pj_mm", "ln_add", "ln_st", "ln_ag", "ln_rs", "ln_x", "ln_t", "ln_ev", "ln_res", "r_mul",
                 "fc_mm", "gx", "g_sq", "g_u", "g_th", "g_g", "g_hi", "g_lo", "ml_mm")
        start_at_first(nc, [w_in, rows_in, par_in, w_hi, w_lo, par_ok, ext_ok, init] + [m for n, both_ in s.items() if n != "ln_rs" for m in both_])
        block = ctx.enter_context(nc.Block())

        def product192(pe, out, feature_major, x, col, n, tok0=0, toks=S):
            A, B2, C = xh[x][:, 0, tok0:tok0 + toks], xl[x][:, tok0:tok0 + toks], xh[x][:, 1, tok0:tok0 + toks]
            terms = [(whi, 0, A), (wlo, 0, A), (whi, 0, B2), (whi, 1, C), (wlo, 1, C)]
            for i, (w, slot, act_) in enumerate(terms):
                wa = w192(w, slot, col, n)
                lhs, rhs = (wa, act_) if feature_major else (act_, wa)
                last = pe.matmul(out, lhs, rhs, start=i == 0, stop=i == len(terms) - 1)
            return last

        @block.sync
        def _(sp):
            sp.dma_start(par[:, :, :], io["params"]).then_inc(par_in, 16)
            sp.wait_ge(init, 6 + FIRST)
            with sp.Fori(0, layers) as l:
                sp.wait_ge(w_lo, l * 3 + FIRST)
                sp.wait_ge(w_hi, l * 3 + FIRST)
                hold(sp, tick)
                sp.dma_start(wraw[:, :], io["weights"][l, :, :]).then_inc(w_in, 16)
                for x in range(2):
                    sp.wait_ge(s["ln_res"][x], l * (2 * PAIRS) + FIRST)
                hold(sp, tick)
                sp.dma_start(rows[:, :, :], t["rows_dram"][l, :, :].partition_broadcast(P)).then_inc(rows_in, 16)
                with sp.Fori(0, PAIRS) as p:
                    it = l * PAIRS + p

                    def masks(x):
                        sp.wait_ge(s["v1_rd"][x], it * 9 + FIRST)
                        hold(sp, tick)
                        sp.dma_start(m1[x][:, :], t["m1_dram"][2 * p + x, :, :]).then_inc(s["mask_ld"][x], 16)
                        sp.wait_ge(s["u_mm"][x], it + FIRST)
                        hold(sp, tick)
                        sp.dma_start(wt[x][:, :], t["wt_dram"][2 * p + x, :, :]).then_inc(s["wt_ld"][x], 16)

                    def stacks(x):
                        sp.wait_ge(s["v2_mm"][x], it * 9 + FIRST)
                        hold(sp, tick)
                        for part, ready in ((0, "p1"), (1, "p2"), (2, "p3")):
                            sp.wait_ge(s[ready][x], it + 1 + FIRST)
                            for role, (dst, parts) in enumerate(((qs[x], Q_PARTS), (ks[x], K_PARTS))):
                                for r in range(6):
                                    if parts[r] != part:
                                        continue
                                    sp.dma_start(
                                        dst[HD * r:HD * (r + 1), :, :], prt[x][:, part, 2 * role:2 * role + 2, :],
                                    ).then_inc(s["stacked"][x], 16)

                    def shifts(x):
                        sp.wait_ge(s["m_ev"][x], it + 1 + FIRST)
                        sp.dma_start(qs[x][KROWS:KROWS + 3, :, :], mparts[x][:, :]).then_inc(s["m_st"][x], 16)

                    for stage in (masks, stacks, shifts):
                        for x in range(2):
                            stage(x)

        @block.gpsimd
        def _(pool):
            n = 0
            for x in range(2):
                for m, value in ((ks[x][KROWS:KROWS + 3, :, :], 1.0), (vtok[x][:, :, :, HD + 1:], 0.0),
                                 (vtok[x][:, :, :, HD:HD + 1], 1.0)):
                    if n:
                        pool.wait_ge(init, n + FIRST)
                    pool.memset(m, value).then_inc(init, 1)
                    n += 1
            with pool.Fori(0, layers) as l:
                def split_input(x, p):
                    it = l * PAIRS + p
                    pool.wait_ge(s["x_hi"][x], it * 3 + 1 + FIRST)
                    hold(pool, tick)
                    h0 = t["hst"][:, bass.ds(2 * p + x, 1), 0, :].rearrange("p b n -> p (b n)")
                    h1 = t["hst"][P // 2:, bass.ds(2 * p + x, 1), 1, :].rearrange("p b n -> p (b n)")
                    pool.tensor_tensor(xl[x][:, :], h0, xh[x][:, 0, :], ALU.subtract).then_inc(s["x_lo"][x], 1)
                    pool.wait_ge(s["x_lo"][x], it * 6 + 1 + FIRST)
                    hold(pool, tick)
                    pool.tensor_tensor(xh[x][P // 2:, 1, :], h1, xh[x][P // 2:, 1, :], ALU.subtract).then_inc(s["x_lo"][x], 1)
                    pool.wait_ge(s["x_lo"][x], it * 6 + 2 + FIRST)
                    hold(pool, tick)

                def pair(p, following):
                    it = l * PAIRS + p

                    def split_lo(x):
                        pool.wait_ge(s["x_hi"][x], it * 3 + 3 + FIRST)
                        pool.tensor_tensor(xl[x][:, :], xT[x][:, 0, :], xh[x][:, 0, :], ALU.subtract).then_inc(s["x_lo"][x], 1)
                        pool.wait_ge(s["x_lo"][x], it * 6 + 5 + FIRST)
                        pool.tensor_tensor(xh[x][P // 2:, 1, :], xT[x][P // 2:, 1, :], xh[x][P // 2:, 1, :], ALU.subtract).then_inc(s["x_lo"][x], 1)
                        pool.wait_ge(s["x_lo"][x], it * 6 + 6 + FIRST)

                    def residual(x, k):
                        pool.wait_ge(s["ln_x"][x], it * 6 + 3 * k + 3 + FIRST)
                        pool.wait_ge(rows_in, l * 16 + 16 + FIRST)
                        if k == 0:
                            dst = res2[x][:, :, :]
                            pool.wait_ge(s["ln_add"][x], it * 2 + FIRST)
                        else:
                            dst = t["res"][:, bass.ds(QB * (2 * p + x), QB), :]
                            hold(pool, tick)
                        sc = rows[:, 2 * k:2 * k + 1, :].to_broadcast([P, QB, D])
                        bi = rows[:, 2 * k + 1:2 * k + 2, :].to_broadcast([P, QB, D])
                        pool.tensor_tensor(dst, xtok[x][:, :, 0:D], sc, ALU.mult).then_inc(s["r_mul"][x], 1)
                        pool.wait_ge(s["r_mul"][x], it * 2 + k + 1 + FIRST)
                        if k:
                            hold(pool, tick)
                        pool.tensor_tensor(dst, dst, bi, ALU.add).then_inc(s["ln_res"][x], 1)

                    residual(0, 0)
                    split_lo(0)
                    split_lo(1)
                    residual(1, 0)
                    if following:
                        for x in range(2):
                            split_input(x, p + 1)
                    residual(0, 1)
                    residual(1, 1)

                for x in range(2):
                    split_input(x, 0)
                with pool.Fori(0, PAIRS - 1) as p:
                    pair(p, True)
                pair(PAIRS - 1, False)

        @block.scalar
        def _(act):
            for x in range(2):
                act.nop().then_inc(s["h_ready"][x], 2 * PAIRS)
            act.wait_ge(par_in, 16 + FIRST)
            with act.Fori(0, layers) as l:
                act.wait_ge(w_in, l * 16 + 16 + FIRST)
                for x in range(2):
                    act.wait_ge(s["ml_mm"][x], l * PAIRS + FIRST)
                act.activation(w_attn(whi), w_attn(wraw), ACT.Copy).then_inc(w_hi, 1)
                for x in range(2):
                    act.wait_ge(s["h_ready"][x], l * (2 * PAIRS) + 2 * PAIRS + FIRST)
                hold(act, tick)
                lp = par[:, bass.ds(l, 1), :].rearrange("p a c -> p (a c)")
                act.activation(parl[:, PK:], lp[:, PK:], ACT.Copy).then_inc(par_ok, 1)
                act.activation(parl[:, PQ:PK], lp[:, PQ:PK], ACT.Copy, scale=float(HD) ** -0.5).then_inc(par_ok, 1)
                act.wait_ge(par_ok, l * 2 + 2 + FIRST)
                def split_input(x, p):
                    it = l * PAIRS + p
                    act.wait_ge(s["fc_mm"][x], it * 3 + FIRST)
                    act.wait_ge(s["h_ready"][x], it * 2 + 2 + FIRST)
                    hold(act, tick)
                    act.activation(xh[x][:, :, :], t["hst"][:, bass.ds(2 * p + x, 1), :, :].rearrange("p b s n -> p (b s) n"),
                                   ACT.Copy).then_inc(s["x_hi"][x], 1)

                def qk_out(x, p):
                    it = l * PAIRS + p
                    act.wait_ge(s["ml_mm"][x], it + FIRST)
                    for i in range(4):
                        if i % 2 == 0:
                            act.wait_ge(s["qk_mm"][x], it * 2 + i // 2 + 1 + FIRST)
                        src = ps[x][i // 2][0:CUT, (i % 2) * S:(i % 2 + 1) * S]
                        act.activation(qk[x][:, i, :], src, ACT.Identity, bias=parl[0:CUT, PQ + i:PQ + i + 1],
                                       scale=float(HD) ** -0.5 if i < 2 else 1.0).then_inc(s["qk32"][x], 1)

                def pair(p, following):
                    it = l * PAIRS + p

                    act.wait_ge(s["pt"][1], it * 9 + FIRST)
                    hold(act, tick)
                    act.activation(extp[:, :], t["ext"][:, bass.ds(2 * QB * p, 2 * QB)], ACT.Copy).then_inc(ext_ok, 1)

                    def split_hi(x, k):
                        act.wait_ge(s["v_mm"][x] if k == 1 else s["pj_mm"][x], it + 1 + FIRST)
                        act.wait_ge(s["a_ev"][x] if k == 1 else s["ln_ev"][x], it * 2 + 2 + FIRST)
                        act.activation(xh[x][:, :, :], xT[x][:, :, :], ACT.Copy).then_inc(s["x_hi"][x], 1)

                    def future_weight(x):
                        act.wait_ge(s["cp"][x], it * 2 + 2 + FIRST)
                        act.wait_ge(s["u_rd"][x], it + FIRST)
                        act.activation(cfut[x][:, :, :], cpre[x][:, :, :], ACT.Exp).then_inc(s["cf"][x], 1)

                    def probs(x, js):
                        if js[0] == 0:
                            act.wait_ge(s["stacked"][x], it * 192 + 192 + FIRST)
                            act.wait_ge(ext_ok, it + 1 + FIRST)
                        for j in js:
                            act.wait_ge(s["v2_mm"][x], it * 9 + j + 1 + FIRST)
                            bank = ps[x][(2, 3, 0)[j % 3]]
                            if j < 6:
                                dst = pt0[x][:, 2 * j:2 * j + 2, :]
                                src = bank[:, :].rearrange("p (h n) -> p h n", h=2)
                            else:
                                dst = pt1[x][:, 4 * (j - 6):4 * (j - 6) + 4, :]
                                src = bank[:, :].rearrange("p (h n) -> p h n", h=4)
                            act.activation(dst, src, ACT.Exp, bias=extp[:, QB * x + j // 6:QB * x + j // 6 + 1]).then_inc(s["pt"][x], 1)

                    def o_out(x):
                        act.wait_ge(s["pv_mm"][x], it * 2 + 1 + FIRST)
                        act.activation(oT[x][:, 0:2, :], ps[x][1][:, :].rearrange("p (t n) -> p t n", t=2), ACT.Copy).then_inc(s["o_ev"][x], 1)
                        act.wait_ge(s["pv_mm"][x], it * 2 + 2 + FIRST)
                        act.activation(oT[x][:, 2, :], ps[x][2][:, 0:S], ACT.Copy).then_inc(s["o_ev"][x], 1)

                    def a_out(x):
                        act.wait_ge(s["a_t"][x], it + 1 + FIRST)
                        act.wait_ge(s["x_lo"][x], it * 6 + 2 + FIRST)
                        for c in range(2):
                            act.activation(xT[x][:, c, :], ps[x][1][:, c * S:(c + 1) * S], ACT.Identity,
                                           bias=parl[:, PV_ + c:PV_ + c + 1]).then_inc(s["a_ev"][x], 1)

                    def norm_out(x, k):
                        act.wait_ge(s["ln_t"][x], it * 2 + k + 1 + FIRST)
                        for c in range(2):
                            if k == 0:
                                act.wait_ge(s["x_lo"][x], it * 6 + 4 + FIRST)
                                dst, bank, done = xT[x][:, c, :], ps[x][3], s["ln_ev"][x]
                            else:
                                if c == 0:
                                    hold(act, tick)
                                dst = t["hst"][:, bass.ds(2 * p + x, 1), c, :].rearrange("p b n -> p (b n)")
                                bank, done = ps[x][3], s["h_ready"][x]
                            act.activation(dst, bank[:, c * S:(c + 1) * S], ACT.Identity,
                                           scale=parl[:, (PL1W, PL2W)[k] + c:(PL1W, PL2W)[k] + c + 1],
                                           bias=parl[:, (PL1B, PL2B)[k] + c:(PL1B, PL2B)[k] + c + 1]).then_inc(done, 1)

                    def hidden(x, g):
                        if g == 0:
                            act.wait_ge(s["pv_mm"][x], it * 2 + 2 + FIRST)
                        for c in range(g * HG, (g + 1) * HG):
                            act.wait_ge(s["fc_mm"][x], it * 3 + c // 2 + 1 + FIRST)
                            act.activation(gx[x][:, c, :], ps[x][c // 2][:, (c % 2) * S:(c % 2 + 1) * S], ACT.Identity,
                                           bias=parl[:, PFC + c:PFC + c + 1]).then_inc(s["gx"][x], 1)
                        act.wait_ge(s["gx"][x], it * HC + (g + 1) * HG + FIRST)
                        cs = slice(g * HG, (g + 1) * HG)
                        act.activation(gt[x][:, cs, :], gx[x][:, cs, :], ACT.Square).then_inc(s["g_sq"][x], 1)

                    def tanh(x, g):
                        act.wait_ge(s["g_u"][x], it * 2 + g + 1 + FIRST)
                        cs = slice(g * HG, (g + 1) * HG)
                        act.activation(gt[x][:, cs, :], gt[x][:, cs, :], ACT.Tanh, scale=GELU_C * GELU_A).then_inc(s["g_th"][x], 1)

                    def gelu_hi(x, g):
                        act.wait_ge(s["g_g"][x], it * 2 + g + 1 + FIRST)
                        cs = slice(g * HG, (g + 1) * HG)
                        act.activation(gh[x][:, cs, :], gg[x][:, cs, :], ACT.Copy).then_inc(s["g_hi"][x], 1)

                    future_weight(0)
                    probs(0, range(9))
                    future_weight(1)
                    probs(1, range(3))
                    o_out(0)
                    probs(1, range(3, 9))
                    o_out(1)
                    for x in range(2):
                        a_out(x)
                        split_hi(x, 1)
                    for x in range(2):
                        norm_out(x, 0)
                        split_hi(x, 2)
                    hidden(0, 0)
                    hidden(0, 1)
                    if following:
                        split_input(0, p + 1)
                    tanh(0, 0)
                    tanh(0, 1)
                    hidden(1, 0)
                    gelu_hi(0, 0)
                    gelu_hi(0, 1)
                    hidden(1, 1)
                    if following:
                        split_input(1, p + 1)
                    tanh(1, 0)
                    tanh(1, 1)
                    gelu_hi(1, 0)
                    gelu_hi(1, 1)
                    for x in range(2):
                        if following:
                            qk_out(x, p + 1)
                        norm_out(x, 1)

                for x in range(2):
                    split_input(x, 0)
                act.activation(w_fc(whi), w_fc(wraw), ACT.Copy).then_inc(w_hi, 1)
                act.activation(whi[:, 2 * WCOLS:], wraw[:, 2 * WCOLS:], ACT.Copy, scale=0.5).then_inc(w_hi, 1)
                for x in range(2):
                    qk_out(x, 0)
                with act.Fori(0, PAIRS - 1) as p:
                    pair(p, True)
                pair(PAIRS - 1, False)

        @block.vector
        def _(dve):
            with dve.Fori(0, layers) as l:
                dve.wait_ge(w_hi, l * 3 + 1 + FIRST)
                for x in range(2):
                    dve.wait_ge(s["ml_mm"][x], l * PAIRS + FIRST)
                dve.tensor_tensor(w_attn(wlo), w_attn(wraw), w_attn(whi), ALU.subtract).then_inc(w_lo, 1)
                dve.wait_ge(w_hi, l * 3 + 3 + FIRST)
                dve.tensor_tensor(w_fc(wlo), w_fc(wraw), w_fc(whi), ALU.subtract).then_inc(w_lo, 1)
                dve.scalar_tensor_tensor(wlo[:, 2 * WCOLS:], wraw[:, 2 * WCOLS:], 0.5, whi[:, 2 * WCOLS:],
                                         ALU.mult, ALU.subtract).then_inc(w_lo, 1)
                def v_out(x, p):
                    it = l * PAIRS + p
                    dve.wait_ge(s["v_mm"][x], it + 1 + FIRST)
                    dve.wait_ge(s["pv_mm"][x], it * 2 + FIRST)
                    dve.tensor_copy(vtok[x][:, :, :, 0:HD].rearrange("p q h d -> p (q h) d"),
                                    ps[x][2][:, 0:QB * D].rearrange("p (g d) -> p g d", d=HD)).then_inc(s["v32"][x], 1)

                def parts(x, p):
                    it = l * PAIRS + p
                    dve.wait_ge(s["qk32"][x], it * 4 + 4 + FIRST)
                    dve.tensor_copy(prt[x][:, 0, :, :], qk[x][:, :, :]).then_inc(s["p1"][x], 1)
                    dve.wait_ge(s["p1"][x], it + 1 + FIRST)
                    dve.tensor_tensor(r1[x][:, :, :], qk[x][:, :, :], prt[x][:, 0, :, :], ALU.subtract).then_inc(s["rs1"][x], 1)
                    dve.wait_ge(s["rs1"][x], it + 1 + FIRST)
                    dve.tensor_copy(prt[x][:, 1, :, :], r1[x][:, :, :]).then_inc(s["p2"][x], 1)
                    dve.wait_ge(s["p2"][x], it + 1 + FIRST)
                    dve.tensor_tensor(prt[x][:, 2, :, :], r1[x][:, :, :], prt[x][:, 1, :, :], ALU.subtract).then_inc(s["p3"][x], 1)

                def pair(p, following):
                    it = l * PAIRS + p

                    def split_lo(x):
                        dve.wait_ge(s["x_hi"][x], it * 3 + 2 + FIRST)
                        dve.tensor_tensor(xl[x][:, :], xT[x][:, 0, :], xh[x][:, 0, :], ALU.subtract).then_inc(s["x_lo"][x], 1)
                        dve.tensor_tensor(xh[x][P // 2:, 1, :], xT[x][P // 2:, 1, :], xh[x][P // 2:, 1, :], ALU.subtract).then_inc(s["x_lo"][x], 1)

                    def row_max(x, js):
                        if js[0] == 0:
                            dve.wait_ge(s["mask_ld"][x], it * 16 + 16 + FIRST)
                            dve.wait_ge(s["nm"][x], it * 2 + FIRST)
                        for j in js:
                            dve.wait_ge(s["v1_mm"][x], it * 9 + j + 1 + FIRST)
                            hold(dve, tick)
                            bank = ps[x][j % 4]
                            heads, q, n, m0 = (range(4 * j, 4 * j + 4), 0, P, 0) if j < 3 else \
                                (range(2 * (j - 3), 2 * (j - 3) + 2), 1, S, P)
                            for i, h in enumerate(heads):
                                last = dve.tensor_tensor_reduce(
                                    out=bank[:, i * n:(i + 1) * n], in0=bank[:, i * n:(i + 1) * n], in1=m1[x][:, m0:m0 + n], scale=1.0,
                                    scalar=NEG2 * 4, op0=ALU.add, op1=ALU.max, accum_out=mmax[x][:, q, h:h + 1])
                            last.then_inc(s["v1_rd"][x], 1)

                    def shift(x):
                        dve.wait_ge(s["v1_rd"][x], it * 9 + 9 + FIRST)
                        dve.wait_ge(s["cp"][x], it * 2 + FIRST)
                        for q in range(QB):
                            e10 = t["e10"][:, bass.ds(QB * (2 * p + x) + q, 1)]
                            dve.tensor_scalar(negm[x][:, q, :], mmax[x][:, q, :], e10, -1.0, ALU.max, ALU.mult).then_inc(s["nm"][x], 1)
                        dve.wait_ge(s["nm"][x], it * 2 + 2 + FIRST)
                        dve.wait_ge(s["m_t"][x], it + FIRST)
                        dve.tensor_copy(mtok[x][:, :, 0, :], negm[x][:, :, :]).then_inc(s["mp"][x], 1)
                        dve.wait_ge(s["cf"][x], it + FIRST)
                        for q in range(QB):
                            e10 = t["e10"][:, bass.ds(QB * (2 * p + x) + q, 1)]
                            dve.tensor_scalar(cpre[x][:, q, :], negm[x][:, q, :], e10, None, ALU.add).then_inc(s["cp"][x], 1)
                        dve.wait_ge(s["mp"][x], it * 4 + 1 + FIRST)
                        dve.tensor_tensor(mres[x][:, :, :], negm[x][:, :, :], mtok[x][:, :, 0, :], ALU.subtract).then_inc(s["mp"][x], 1)
                        dve.wait_ge(s["mp"][x], it * 4 + 2 + FIRST)
                        dve.tensor_copy(mtok[x][:, :, 1, :], mres[x][:, :, :]).then_inc(s["mp"][x], 1)
                        dve.wait_ge(s["mp"][x], it * 4 + 3 + FIRST)
                        dve.tensor_tensor(mtok[x][:, :, 2, :], mres[x][:, :, :], mtok[x][:, :, 1, :], ALU.subtract).then_inc(s["mp"][x], 1)

                    def shift_out(x):
                        dve.wait_ge(s["m_t"][x], it + 1 + FIRST)
                        dve.wait_ge(s["m_st"][x], it * 16 + FIRST)
                        dve.tensor_copy(mparts[x][:, :], ps[x][0][:, 0:P].bitcast(BF16)[0:3 * HEADS, 0:S]).then_inc(s["m_ev"][x], 1)

                    def future(x):
                        dve.wait_ge(s["u_mm"][x], it + 1 + FIRST)
                        dve.wait_ge(s["cf"][x], it + 1 + FIRST)
                        dve.tensor_tensor(ufut[x][:, :, :, :].rearrange("p q h d -> p (q h) d"),
                                          ps[x][1][:, 0:QB * HEADS * (HD + 1)].rearrange("p (g d) -> p g d", d=HD + 1),
                                          cfut[x][:, :, :].rearrange("p q h -> p (q h)").unsqueeze(2).to_broadcast([P, QB * HEADS, HD + 1]),
                                          ALU.mult).then_inc(s["u_rd"][x], 1)

                    def attend(x):
                        dve.wait_ge(s["u_rd"][x], it + 1 + FIRST)
                        for q in range(QB):
                            dve.wait_ge(s["o_t"][x], it * 2 + q + 1 + FIRST)
                            dve.tensor_tensor(otok[x][:, q, :, :], ps[x][(3, 0)[q]][:, 0:HEADS * SLOT].rearrange(
                                "p (h d) -> p h d", d=SLOT)[:, :, 0:HD + 1], ufut[x][:, q, :, :], ALU.add).then_inc(s["o_rd"][x], 1)
                        dve.wait_ge(s["o_rd"][x], it * 2 + 2 + FIRST)
                        dve.reciprocal(rden[x][:, :, :].rearrange("p q h -> p (q h)").unsqueeze(2),
                                       otok[x][:, :, :, HD:HD + 1].rearrange("p q h d -> p (q h) d")).then_inc(s["den"][x], 1)
                        dve.wait_ge(s["den"][x], it + 1 + FIRST)
                        dve.wait_ge(s["ln_t"][x], it * 2 + FIRST)
                        dve.wait_ge(s["ln_res"][x], it * 2 + FIRST)
                        for q in range(QB):
                            dve.tensor_tensor(xtok[x][:, q, 0:D].rearrange("p (h d) -> p h d", d=HD), otok[x][:, q, :, 0:HD],
                                              rden[x][:, q, :].unsqueeze(2).to_broadcast([P, HEADS, HD]), ALU.mult).then_inc(s["atok"][x], 1)
                        dve.wait_ge(s["atok"][x], it * 3 + 2 + FIRST)
                        dve.tensor_copy(xtok[x][:, :, D:], xtok[x][:, :, P:D]).then_inc(s["atok"][x], 1)

                    def norm(x, k):
                        n = it * 2 + k
                        dve.wait_ge(s["pj_mm"][x] if k == 0 else s["ml_mm"][x], it + 1 + FIRST)
                        bank = ps[x][2] if k == 0 else ps[x][3]
                        if k == 0:
                            res = t["res"][:, bass.ds(QB * (2 * p + x), QB), :]
                        else:
                            res = res2[x][:, :, :]
                            dve.wait_ge(s["ln_res"][x], it * 2 + 1 + FIRST)
                        dve.tensor_tensor(ltok[x][:, :, :], bank[:, 0:QB * D].rearrange("p (q n) -> p q n", q=QB), res, ALU.add).then_inc(s["ln_add"][x], 1)
                        dve.wait_ge(s["ln_add"][x], n + 1 + FIRST)
                        for q in range(QB):
                            dve.bn_stats(lst[x][:, q, :], ltok[x][:, q, :]).then_inc(s["ln_st"][x], 1)
                        dve.wait_ge(s["ln_st"][x], n * 2 + 2 + FIRST)
                        hold(dve, tick)
                        for q in range(QB):
                            dve.bn_aggr(lmv[x][:, q, :], lst[x][:, q, :]).then_inc(s["ln_ag"][x], 1)
                        dve.wait_ge(s["ln_ag"][x], n * 2 + 2 + FIRST)
                        rsqrt_steps(dve, s["ln_rs"][x], n * RSQRT_STEPS, lmv[x][:, :, 1:2], lrs[x][:, :, :], lwk[x][:, 0, :, :], lwk[x][:, 1, :, :])
                        if k == 0:
                            dve.wait_ge(s["a_t"][x], it + 1 + FIRST)
                        else:
                            dve.wait_ge(s["ln_t"][x], it * 2 + 1 + FIRST)
                            dve.wait_ge(s["ln_res"][x], it * 2 + 1 + FIRST)
                        for q in range(QB):
                            dve.tensor_scalar(xtok[x][:, q, 0:D], ltok[x][:, q, :], lmv[x][:, q, 0:1], lrs[x][:, q, :],
                                              ALU.subtract, ALU.mult).then_inc(s["ln_x"][x], 1)
                        dve.wait_ge(s["ln_x"][x], n * 3 + 2 + FIRST)
                        dve.tensor_copy(xtok[x][:, :, D:], xtok[x][:, :, P:D]).then_inc(s["ln_x"][x], 1)

                    def gelu_arg(x, g):
                        dve.wait_ge(s["g_sq"][x], it * 2 + g + 1 + FIRST)
                        cs = slice(g * HG, (g + 1) * HG)
                        dve.scalar_tensor_tensor(gt[x][:, cs, :], gt[x][:, cs, :], 1.0 / GELU_A, gx[x][:, cs, :], ALU.add, ALU.mult).then_inc(s["g_u"][x], 1)

                    def gelu(x, g):
                        dve.wait_ge(s["g_th"][x], it * 2 + g + 1 + FIRST)
                        cs = slice(g * HG, (g + 1) * HG)
                        dve.scalar_tensor_tensor(gg[x][:, cs, :], gt[x][:, cs, :], 1.0, gx[x][:, cs, :], ALU.add, ALU.mult).then_inc(s["g_g"][x], 1)

                    def gelu_lo(x, g):
                        dve.wait_ge(s["g_hi"][x], it * 2 + g + 1 + FIRST)
                        cs = slice(g * HG, (g + 1) * HG)
                        dve.tensor_tensor(gl[x][:, cs, :], gg[x][:, cs, :], gh[x][:, cs, :], ALU.subtract).then_inc(s["g_lo"][x], 1)

                    row_max(0, range(9))
                    shift(0)
                    row_max(1, range(4))
                    shift_out(0)
                    row_max(1, range(4, 9))
                    shift(1)
                    future(0)
                    shift_out(1)
                    future(1)
                    for x in range(2):
                        attend(x)
                    for x in range(2):
                        split_lo(x)
                    for x in range(2):
                        norm(x, 0)
                    gelu_arg(0, 0)
                    gelu_arg(0, 1)
                    gelu(0, 0)
                    gelu(0, 1)
                    gelu_arg(1, 0)
                    gelu_lo(0, 0)
                    gelu_lo(0, 1)
                    gelu_arg(1, 1)
                    gelu(1, 0)
                    gelu(1, 1)
                    gelu_lo(1, 0)
                    gelu_lo(1, 1)
                    for x in range(2):
                        norm(x, 1)
                        if following:
                            parts(x, p + 1)
                            v_out(x, p + 1)

                for x in range(2):
                    parts(x, 0)
                    v_out(x, 0)
                with dve.Fori(0, PAIRS - 1) as p:
                    pair(p, True)
                pair(PAIRS - 1, False)

        @block.tensor
        def _(pe):
            ident, ident_b, trib = t["ident"], t["ident_b"], t["trib"]
            with pe.Fori(0, layers) as l:
                pe.wait_ge(w_hi, l * 3 + 1 + FIRST)
                pe.wait_ge(w_lo, l * 3 + 1 + FIRST)
                hold(pe, tick)
                def qkv(x, p):
                    it = l * PAIRS + p
                    pe.wait_ge(s["x_lo"][x], it * 6 + 2 + FIRST)
                    pe.wait_ge(s["gx"][x], it * HC + FIRST)
                    for i in range(4):
                        last = product192(pe, ps[x][i // 2][0:CUT, (i % 2) * S:(i % 2 + 1) * S], True, x, CUT * i, CUT)
                        if i % 2:
                            last.then_inc(s["qk_mm"][x], 1)
                    for q in range(QB):
                        last = product192(pe, ps[x][2][:, q * D:(q + 1) * D], False, x, WV, D, q * P, P)
                    last.then_inc(s["v_mm"][x], 1)

                def pair(p, following):
                    it = l * PAIRS + p

                    def scores(x, js):
                        if js[0] == 0:
                            pe.wait_ge(s["stacked"][x], it * 192 + 192 + FIRST)
                            pe.wait_ge(s["qk32"][x], it * 4 + 4 + FIRST)
                            pe.wait_ge(s["v32"][x], it + 1 + FIRST)
                            pe.wait_ge(s["h_ready"][x], it * 2 + 2 * PAIRS + FIRST)
                        for j in js:
                            if j >= 4:
                                pe.wait_ge(s["v1_rd"][x], it * 9 + j - 3 + FIRST)
                            bank = ps[x][j % 4]
                            heads, q, n = (range(4 * j, 4 * j + 4), 0, P) if j < 3 else (range(2 * (j - 3), 2 * (j - 3) + 2), 1, S)
                            for i, h in enumerate(heads):
                                last = pe.matmul(bank[:, i * n:(i + 1) * n], qs[x][0:KROWS, h, q * P:(q + 1) * P],
                                                 ks[x][0:KROWS, h, 0:n], start=True, stop=True)
                            last.then_inc(s["v1_mm"][x], 1)

                    def shift_t(x):
                        pe.wait_ge(s["mp"][x], it * 4 + 4 + FIRST)
                        pe.wait_ge(s["v1_rd"][x], it * 9 + 9 + FIRST)
                        hold(pe, tick)
                        for q in range(QB):
                            last = pe.transpose(ps[x][0][:, 0:P].bitcast(BF16)[0:3 * HEADS, q * P:(q + 1) * P],
                                                mtok[x][:, q, :, :].rearrange("p r h -> p (r h)"), ident_b[:, :])
                        last.then_inc(s["m_t"][x], 1)

                    def future(x):
                        pe.wait_ge(s["wt_ld"][x], it * 16 + 16 + FIRST)
                        n = HEADS * (HD + 1)
                        for q, kb, w in ((0, 0, 0), (0, 1, 1), (1, 1, 2)):
                            last = pe.matmul(ps[x][1][:, q * n:(q + 1) * n], wt[x][:, w * P:(w + 1) * P],
                                             vtok[x][:, kb, :, 0:HD + 1], start=w != 1, stop=w != 0)
                        last.then_inc(s["u_mm"][x], 1)

                    def scores_t(x, js):
                        if js[0] == 0:
                            pe.wait_ge(s["m_st"][x], it * 16 + 16 + FIRST)
                        for j in js:
                            if j == 2:
                                pe.wait_ge(s["m_ev"][x], it + 1 + FIRST)
                            if j >= 3:
                                pe.wait_ge(s["pt"][x], it * 9 + j - 2 + FIRST)
                            bank = ps[x][(2, 3, 0)[j % 3]]
                            heads, kb, q0, n = (range(2 * j, 2 * j + 2), 0, 0, S) if j < 6 else \
                                (range(4 * (j - 6), 4 * (j - 6) + 4), 1, P, P)
                            for i, h in enumerate(heads):
                                pe.matmul(bank[:, i * n:(i + 1) * n], ks[x][0:KROWS + 3, h, kb * P:(kb + 1) * P],
                                          qs[x][0:KROWS + 3, h, q0:q0 + n], start=i == 0, stop=False, skip_group_check=True)
                            m = len(heads)
                            last = pe.matmul(bank[:, :].rearrange("p (h n) -> p h n", h=m)[:, :, 0:P], ident_b[:, :],
                                             trib[:, :].unsqueeze(1).to_broadcast([P, m, P]), start=False, stop=True, skip_group_check=True)
                            last.then_inc(s["v2_mm"][x], 1)

                    def attend(x):
                        pe.wait_ge(s["u_rd"][x], it + 1 + FIRST)
                        pe.wait_ge(s["pt"][x], it * 9 + 9 + FIRST)
                        for h in range(HEADS):
                            a, j = divmod(h, HSLOT)
                            bank, c0 = (ps[x][1], a * S) if a < 2 else (ps[x][2], 0)
                            pe.matmul(bank[SLOT * j:SLOT * (j + 1), c0:c0 + S], vtok[x][:, 0, h, :], pt0[x][:, h, :],
                                      start=True, stop=False, skip_group_check=True)
                            last = pe.matmul(bank[SLOT * j:SLOT * (j + 1), c0 + P:c0 + S], vtok[x][:, 1, h, :], pt1[x][:, h, :],
                                             start=False, stop=True, skip_group_check=True)
                            if h in (7, 11):
                                last.then_inc(s["pv_mm"][x], 1)

                    def o_t(x):
                        pe.wait_ge(s["o_ev"][x], it * 2 + 2 + FIRST)
                        for q in range(QB):
                            for a in range(HT):
                                last = pe.transpose(ps[x][(3, 0)[q]][:, a * P:(a + 1) * P], oT[x][:, a, q * P:(q + 1) * P], ident[:, :])
                            last.then_inc(s["o_t"][x], 1)

                    def token_t(x, bank, ready, done):
                        pe.wait_ge(ready[0], ready[1] + FIRST)
                        for c in range(2):
                            for q in range(QB):
                                last = pe.transpose(bank[:, c * S + q * P:c * S + (q + 1) * P], xtok[x][:, q, c * P:(c + 1) * P], ident[:, :])
                        last.then_inc(done, 1)

                    def a_t(x):
                        token_t(x, ps[x][1], (s["atok"][x], it * 3 + 3), s["a_t"][x])

                    def proj(x):
                        pe.wait_ge(s["x_lo"][x], it * 6 + 4 + FIRST)
                        for q in range(QB):
                            last = product192(pe, ps[x][2][:, q * D:(q + 1) * D], False, x, WO, D, q * P, P)
                        last.then_inc(s["pj_mm"][x], 1)

                    def norm_t(x, k):
                        if k == 0:
                            pe.wait_ge(s["o_rd"][x], it * 2 + 2 + FIRST)
                        token_t(x, ps[x][3], (s["ln_x"][x], it * 6 + 3 * k + 3), s["ln_t"][x])

                    def fc(x):
                        pe.wait_ge(s["x_lo"][x], it * 6 + 6 + FIRST)
                        pe.wait_ge(s["ln_add"][x], it * 2 + 1 + FIRST)
                        for c in range(HC):
                            last = product192(pe, ps[x][c // 2][:, (c % 2) * S:(c % 2 + 1) * S], True, x, WFC + P * c, P)
                            if c % 2:
                                last.then_inc(s["fc_mm"][x], 1)

                    def mlp(x):
                        for g in range(2):
                            pe.wait_ge(s["g_lo"][x], it * 2 + g + 1 + FIRST)
                            for q in range(QB):
                                out = ps[x][3][:, q * D:(q + 1) * D]
                                for c in range(g * HG, (g + 1) * HG):
                                    g0, g1 = gh[x][:, c, q * P:(q + 1) * P], gl[x][:, c, q * P:(q + 1) * P]
                                    pe.matmul(out, g0, w2(whi, c), start=c == 0 and q == 0, stop=False, skip_group_check=True)
                                    pe.matmul(out, g0, w2(wlo, c), start=False, stop=False, skip_group_check=True)
                                    last = pe.matmul(out, g1, w2(whi, c), start=False, stop=c == HC - 1, skip_group_check=True)
                        last.then_inc(s["ml_mm"][x], 1)

                    scores(0, range(9))
                    scores(1, range(4))
                    shift_t(0)
                    scores(1, range(4, 9))
                    future(0)
                    scores_t(0, range(5))
                    shift_t(1)
                    scores_t(0, range(5, 9))
                    future(1)
                    scores_t(1, range(3))
                    attend(0)
                    scores_t(1, range(3, 6))
                    o_t(0)
                    scores_t(1, range(6, 9))
                    attend(1)
                    o_t(1)
                    for x in range(2):
                        a_t(x)
                    for x in range(2):
                        proj(x)
                    for x in range(2):
                        norm_t(x, 0)
                    for x in range(2):
                        fc(x)
                    if following:
                        qkv(0, p + 1)
                    mlp(0)
                    mlp(1)
                    norm_t(0, 1)
                    if following:
                        qkv(1, p + 1)
                    norm_t(1, 1)

                for x in range(2):
                    qkv(x, 0)
                pe.wait_ge(w_hi, l * 3 + 3 + FIRST)
                pe.wait_ge(w_lo, l * 3 + 3 + FIRST)
                hold(pe, tick)
                with pe.Fori(0, PAIRS - 1) as p:
                    pair(p, True)
                pair(PAIRS - 1, False)
        return s


WZ, WU, WDT = 0, DI, 2 * DI
SCOLS = 2 * DI + P
SP_DTB, SP_CB, SP_D, SP_NW, SP_CW = 0, DJ, 2 * DJ, 3 * DJ, 4 * DJ
NSPAR = SP_CW + DJ * KCONV
TOK2 = 2 * S
NT2 = TOK2 // P
PAD = KCONV - 1
DT_MIN, DT_MAX = 1e-4, 1.0


def five_passes(pe, out, whi, wlo, wcols, xh, xl, xcols, feature_major=True):
    A, L, C = xh[:, 0, xcols], xl[:, xcols], xh[:, 1, xcols]
    terms = [(whi[:, 0, wcols], A), (wlo[:, 0, wcols], A), (whi[:, 0, wcols], L), (whi[:, 1, wcols], C), (wlo[:, 1, wcols], C)]
    for i, (w, x) in enumerate(terms):
        lhs, rhs = (w, x) if feature_major else (x, w)
        last = pe.matmul(out, lhs, rhs, start=i == 0, stop=i == len(terms) - 1)
    return last


def layernorm_tokens(dve, tick, src, dst, st, mv, rs, v, w, sem_st, sem_ag, sem_rs, sem_x, it, blocks):
    for q in range(blocks):
        dve.bn_stats(st[:, q, :], src[:, q, :]).then_inc(sem_st, 1)
    dve.wait_ge(sem_st, it * blocks + blocks)
    hold(dve, tick)
    for q in range(blocks):
        dve.bn_aggr(mv[:, q, :], st[:, q, :]).then_inc(sem_ag, 1)
    dve.wait_ge(sem_ag, it * blocks + blocks)
    rsqrt_steps(dve, sem_rs, it * RSQRT_STEPS, mv[:, :, 1:2], rs, v, w)
    for q in range(blocks):
        dve.tensor_scalar(dst[:, q, 0:D], src[:, q, :], mv[:, q, 0:1], rs[:, q, :], ALU.subtract, ALU.mult).then_inc(sem_x, 1)
    dve.wait_ge(sem_x, it * (blocks + 1) + blocks)
    dve.tensor_copy(dst[:, :, D:], dst[:, :, P:D]).then_inc(sem_x, 1)


def scan_input_phase(nc, io, t):
    with ExitStack() as ctx:
        def sb(name, shape, dt=F32):
            return ctx.enter_context(nc.sbuf_tensor(name, shape, dt))

        def sem(name):
            return nc.alloc_semaphore("si_" + name)

        tick = sem("tick")

        wraw = t["zs"][:, 0, 0:2 * SCOLS].rearrange("p (s n) -> p s n", s=2)
        rraw, oraw = t["y"][:, 0:2, 0:DI], t["dtu"][:, :, 0:D]
        whi, wlo = sb("si_whi", [P, 2, SCOLS], F32R), sb("si_wlo", [P, 2, SCOLS], F32R)
        rhi, rlo = sb("si_rhi", [P, 2, DI], F32R), sb("si_rlo", [P, 2, DI], F32R)
        ohi, olo = sb("si_ohi", [P, DJ, D], F32R), sb("si_olo", [P, DJ, D], F32R)
        dhi, dlo = sb("si_dhi", [P, DI], F32R), sb("si_dlo", [P, DI], F32R)
        par, lnp = sb("si_par", [P, NSPAR]), sb("si_lnp", [P, 4])
        x1, x2 = sb("si_x1", [P, NT2, 2 * P]), sb("si_x2", [P, NT2, 2 * P])
        st, mv = sb("si_st", [P, NT2, 6]), sb("si_mv", [P, NT2, 2])
        rs, v, w = sb("si_rs", [P, NT2, 1]), sb("si_v", [P, NT2, 1]), sb("si_w", [P, NT2, 1])
        xT = sb("si_xT", [P, 2, TOK2])
        xh, xl = sb("si_xh", [P, 2, TOK2], F32R), sb("si_xl", [P, TOK2], F32R)
        dth = sb("si_dth", [P, TOK2], F32R)
        up = sb("si_up", [P, DJ, 2, S + PAD])
        u = sb("si_u", [P, DJ, TOK2])
        rTh, rTl = sb("si_rTh", [P, DJ, TOK2], F32R), sb("si_rTl", [P, DJ, TOK2], F32R)
        psm = ctx.enter_context(nc.psum_tensor("si_ps", [P, 8, 512], F32))
        names = ("w_in", "r_in", "o_in", "d_in", "par_in", "whi", "wlo", "rhi", "rlo", "ohi", "olo", "dhi", "dlo", "pad0",
                 "st1", "ag1", "rs1", "x1", "st2", "ag2", "rs2", "x2", "t_mm", "t_ev", "xhi", "xlo", "r_mm", "r_hi", "r_lo",
                 "o_mm", "res", "z_mm", "th", "sz", "u_mm", "u_ev", "cv", "dh_mm", "dh_hi", "dh_lo", "dt_mm", "dm", "de", "dd",
                 "dl", "rw", "dc", "dt", "y0", "dtu")
        q = {n: sem(n) for n in names}
        start_at_first(nc, [m for n, m in q.items() if n not in ("st1", "ag1", "rs1", "x1", "st2", "ag2", "rs2", "x2")])
        block = ctx.enter_context(nc.Block())
        flat = "p j n -> p (j n)"

        def pair(tile, p):
            return tile[:, :, bass.ds(p * TOK2, TOK2)]

        @block.sync
        def _(sp):
            sp.dma_start(par[:, :], io["s_params"]).then_inc(q["par_in"], 16)
            sp.dma_start(lnp[:, :], io["s_ln"]).then_inc(q["par_in"], 16)
            sp.dma_start(wraw, io["s_w"]).then_inc(q["w_in"], 16)
            sp.dma_start(rraw, io["s_wres"]).then_inc(q["r_in"], 16)
            sp.dma_start(oraw, io["s_wout"]).then_inc(q["o_in"], 16)
            sp.dma_start(u[:, 0, 0:DI], io["s_wdt"]).then_inc(q["d_in"], 16)

        @block.gpsimd
        def _(pool):
            pool.memset(up[:, :, :, 0:PAD], 0.0).then_inc(q["pad0"], 1)
            pool.wait_ge(q["whi"], 1 + FIRST)
            pool.tensor_tensor(wlo[:, :, :], wraw, whi[:, :, :], ALU.subtract).then_inc(q["wlo"], 1)
            with pool.Fori(0, PAIRS) as p:
                pool.wait_ge(q["dt"], p + 1 + FIRST)
                hold(pool, tick)
                pool.tensor_tensor(pair(t["dtu"], p), pair(t["dt"], p), u[:, :, :], ALU.mult).then_inc(q["dtu"], 1)

        @block.scalar
        def _(act):
            act.wait_ge(q["w_in"], 16 + FIRST)
            act.activation(whi[:, :, :], wraw, ACT.Copy).then_inc(q["whi"], 1)
            act.wait_ge(q["r_in"], 16 + FIRST)
            act.activation(rhi[:, :, :], rraw, ACT.Copy).then_inc(q["rhi"], 1)
            act.wait_ge(q["o_in"], 16 + FIRST)
            act.activation(ohi[:, :, :], oraw, ACT.Copy).then_inc(q["ohi"], 1)
            act.wait_ge(q["d_in"], 16 + FIRST)
            act.activation(dhi[:, :], u[:, 0, 0:DI], ACT.Copy).then_inc(q["dhi"], 1)
            act.wait_ge(q["par_in"], 32 + FIRST)
            for m in ("rlo", "olo", "dlo"):
                act.wait_ge(q[m], 1 + FIRST)
            act.wait_ge(q["wlo"], 1 + FIRST)
            with act.Fori(0, PAIRS) as p:
                a, b = pair(t["y"], p), pair(t["dtu"], p)
                for c in range(2):
                    act.wait_ge(q["t_mm"], p * 4 + c + 1 + FIRST)
                    act.wait_ge(q["xlo"], p * 4 + FIRST)
                    act.activation(xT[:, c, :], psm[:, c, :], ACT.Copy).then_inc(q["t_ev"], 1)
                act.wait_ge(q["t_ev"], p * 4 + 2 + FIRST)
                act.wait_ge(q["u_mm"], p + FIRST)
                act.activation(xh[:, :, :], xT[:, :, :], ACT.Copy).then_inc(q["xhi"], 1)
                for c in range(2):
                    act.wait_ge(q["t_mm"], p * 4 + c + 3 + FIRST)
                    act.wait_ge(q["xlo"], p * 4 + 2 + FIRST)
                    act.activation(xT[:, c, :], psm[:, c, :], ACT.Identity, scale=lnp[:, c:c + 1], bias=lnp[:, 2 + c:3 + c]).then_inc(q["t_ev"], 1)
                act.wait_ge(q["t_ev"], p * 4 + 4 + FIRST)
                hold(act, tick)
                act.activation(pair(t["xnh"], p), xT[:, :, :], ACT.Copy).then_inc(q["xhi"], 1)
                act.wait_ge(q["r_mm"], p + 1 + FIRST)
                act.wait_ge(q["o_mm"], p + FIRST)
                act.activation(rTh[:, :, :], psm[:, 2:5, :], ACT.Copy).then_inc(q["r_hi"], 1)
                act.wait_ge(q["dh_mm"], p + 1 + FIRST)
                act.wait_ge(q["dt_mm"], p + FIRST)
                act.activation(dth[:, :], psm[:, 1, :], ACT.Copy).then_inc(q["dh_hi"], 1)
                act.wait_ge(q["u_mm"], p + 1 + FIRST)
                act.wait_ge(q["pad0"], 1 + FIRST)
                act.wait_ge(q["cv"], p * (DJ * KCONV) + FIRST)
                act.activation(up[:, :, :, PAD:].rearrange("p j s n -> p (j s) n"),
                               psm[:, 5:8, :].rearrange("p j (s n) -> p (j s) n", s=2), ACT.Copy).then_inc(q["u_ev"], 1)
                act.wait_ge(q["z_mm"], p + 1 + FIRST)
                hold(act, tick)
                act.activation(a, psm[:, 2:5, :], ACT.Tanh, scale=0.5).then_inc(q["th"], 1)
                act.wait_ge(q["dm"], p * DJ + DJ + FIRST)
                hold(act, tick)
                act.activation(b, b, ACT.Exp).then_inc(q["de"], 1)
                act.wait_ge(q["dd"], p * 2 + 1 + FIRST)
                hold(act, tick)
                act.activation(pair(t["dt"], p), a, ACT.Ln).then_inc(q["dl"], 1)
                act.wait_ge(q["dl"], p + 1 + FIRST)
                act.wait_ge(q["dd"], p * 2 + 2 + FIRST)
                hold(act, tick)
                act.activation(a, pair(t["dt"], p), ACT.Exp, scale=-1.0).then_inc(q["rw"], 1)

        @block.vector
        def _(dve):
            dve.wait_ge(q["rhi"], 1 + FIRST)
            dve.tensor_tensor(rlo[:, :, :], rraw, rhi[:, :, :], ALU.subtract).then_inc(q["rlo"], 1)
            dve.wait_ge(q["ohi"], 1 + FIRST)
            dve.tensor_tensor(olo[:, :, :], oraw, ohi[:, :, :], ALU.subtract).then_inc(q["olo"], 1)
            dve.wait_ge(q["dhi"], 1 + FIRST)
            dve.tensor_tensor(dlo[:, :], u[:, 0, 0:DI], dhi[:, :], ALU.subtract).then_inc(q["dlo"], 1)
            dve.wait_ge(q["par_in"], 32 + FIRST)
            for m in ("rlo", "olo", "dlo"):
                dve.wait_ge(q[m], 1 + FIRST)
            dve.wait_ge(q["wlo"], 1 + FIRST)
            with dve.Fori(0, PAIRS) as p:
                a, b = pair(t["y"], p), pair(t["dtu"], p)
                res = t["res"][:, bass.ds(NT2 * p, NT2), :]
                dve.wait_ge(q["t_mm"], p * 4 + FIRST)
                layernorm_tokens(dve, tick, res, x1, st, mv, rs[:, :, :], v[:, :, :], w[:, :, :], q["st1"], q["ag1"], q["rs1"], q["x1"], p, NT2)
                dve.wait_ge(q["x1"], p * (NT2 + 1) + NT2 + 1)
                layernorm_tokens(dve, tick, x1[:, :, 0:D], x2, st, mv, rs[:, :, :], v[:, :, :], w[:, :, :], q["st2"], q["ag2"], q["rs2"], q["x2"], p, NT2)
                dve.wait_ge(q["xhi"], p * 2 + 1 + FIRST)
                dve.tensor_tensor(xl[:, :], xT[:, 0, :], xh[:, 0, :], ALU.subtract).then_inc(q["xlo"], 1)
                dve.tensor_tensor(xh[P // 2:, 1, :], xT[P // 2:, 1, :], xh[P // 2:, 1, :], ALU.subtract).then_inc(q["xlo"], 1)
                dve.wait_ge(q["xhi"], p * 2 + 2 + FIRST)
                dve.tensor_tensor(t["xnl"][:, bass.ds(p * TOK2, TOK2)], xT[:, 0, :], t["xnh"][:, 0, bass.ds(p * TOK2, TOK2)],
                                  ALU.subtract).then_inc(q["xlo"], 1)
                s1 = t["xnh"][P // 2:, 1, bass.ds(p * TOK2, TOK2)]
                dve.tensor_tensor(s1, xT[P // 2:, 1, :], s1, ALU.subtract).then_inc(q["xlo"], 1)
                dve.wait_ge(q["r_hi"], p + 1 + FIRST)
                dve.tensor_tensor(rTl[:, :, :], psm[:, 2:5, :], rTh[:, :, :], ALU.subtract).then_inc(q["r_lo"], 1)
                dve.wait_ge(q["dh_hi"], p + 1 + FIRST)
                dve.tensor_tensor(dth[P // 2:, :], psm[P // 2:, 1, :], dth[P // 2:, :], ALU.subtract).then_inc(q["dh_lo"], 1)
                def conv(ks):
                    for k in ks:
                        if k:
                            dve.wait_ge(q["cv"], p * (DJ * KCONV) + k * DJ + FIRST)
                        for j in range(DJ):
                            src, dst = up[:, j, :, k:k + S], u[:, j, :].rearrange("p (s n) -> p s n", s=2)
                            wk = par[:, SP_CW + j * KCONV + k:SP_CW + j * KCONV + k + 1]
                            if k == 0:
                                i = dve.tensor_scalar(dst, src, wk, par[:, SP_CB + j:SP_CB + j + 1], ALU.mult, ALU.add)
                            else:
                                i = dve.scalar_tensor_tensor(dst, src, wk, dst, ALU.mult, ALU.add)
                            i.then_inc(q["cv"], 1)

                dve.wait_ge(q["th"], p + 1 + FIRST)
                dve.scalar_tensor_tensor(pair(t["zs"], p), a, 1.0, psm[:, 2:5, :], ALU.add, ALU.mult).then_inc(q["sz"], 1)
                dve.wait_ge(q["u_ev"], p + 1 + FIRST)
                dve.wait_ge(q["dtu"], p + FIRST)
                conv((0, 1))
                dve.wait_ge(q["dt_mm"], p + 1 + FIRST)
                for j in range(DJ):
                    dve.tensor_scalar(t["dtu"][:, j, bass.ds(p * TOK2, TOK2)], psm[:, 2 + j, :], par[:, SP_DTB + j:SP_DTB + j + 1], 20.0, ALU.add, ALU.min).then_inc(q["dm"], 1)
                dve.wait_ge(q["de"], p + 1 + FIRST)
                dve.tensor_scalar(a, b, 1.0, None, ALU.add).then_inc(q["dd"], 1)
                dve.wait_ge(q["dd"], p * 2 + 1 + FIRST)
                dve.scalar_tensor_tensor(b, a, -1.0, b, ALU.add, ALU.subtract).then_inc(q["dd"], 1)
                dve.wait_ge(q["o_mm"], p + 1 + FIRST)
                dve.tensor_tensor(res, psm[:, 4:8, 0:D], res, ALU.add).then_inc(q["res"], 1)
                conv((2, 3))
                dve.wait_ge(q["rw"], p + 1 + FIRST)
                dve.tensor_tensor(b, b, a, ALU.mult).then_inc(q["dc"], 1)
                dve.wait_ge(q["dc"], p * 2 + 1 + FIRST)
                dt = pair(t["dt"], p)
                dve.tensor_tensor(dt, dt, b, ALU.subtract).then_inc(q["dc"], 1)
                dve.wait_ge(q["dc"], p * 2 + 2 + FIRST)
                dve.tensor_scalar(dt, dt, DT_MIN, DT_MAX, ALU.max, ALU.min).then_inc(q["dt"], 1)
                dve.wait_ge(q["cv"], p * (DJ * KCONV) + DJ * KCONV + FIRST)
                for j in range(DJ):
                    dve.tensor_scalar(t["y"][:, j, bass.ds(p * TOK2, TOK2)], u[:, j, :], par[:, SP_D + j:SP_D + j + 1], None, ALU.mult).then_inc(q["y0"], 1)

        @block.tensor
        def _(pe):
            for m in ("wlo", "rlo", "olo", "dlo"):
                pe.wait_ge(q[m], 1 + FIRST)
            with pe.Fori(0, PAIRS) as p:
                for k, (x, ready) in enumerate(((x1, "x1"), (x2, "x2"))):
                    pe.wait_ge(q[ready], p * (NT2 + 1) + NT2 + 1)
                    if k == 0:
                        pe.wait_ge(q["dh_lo"], p + FIRST)
                        pe.wait_ge(q["t_ev"], p * 4 + FIRST)
                    else:
                        pe.wait_ge(q["t_ev"], p * 4 + 2 + FIRST)
                    for c in range(2):
                        for i in range(NT2):
                            last = pe.transpose(psm[:, c, i * P:(i + 1) * P], x[:, i, c * P:(c + 1) * P], t["ident"][:, :])
                        last.then_inc(q["t_mm"], 1)
                pe.wait_ge(q["xlo"], p * 4 + 2 + FIRST)
                pe.wait_ge(q["dm"], p * DJ + FIRST)
                pe.wait_ge(q["res"], p + FIRST)
                for j in range(DJ):
                    last = five_passes(pe, psm[:, 2 + j, :], rhi, rlo, slice(j * P, (j + 1) * P), xh, xl, slice(0, TOK2))
                last.then_inc(q["r_mm"], 1)
                pe.wait_ge(q["xlo"], p * 4 + 4 + FIRST)
                pe.wait_ge(q["t_ev"], p * 4 + 4 + FIRST)
                for j in range(DJ + 1):
                    out, col = (psm[:, 1, :], WDT) if j == DJ else (psm[:, 5 + j, :], WU + j * P)
                    cols = slice(col, col + P)
                    terms = [(whi[:, 0, cols], t["xnh"][:, 0, bass.ds(p * TOK2, TOK2)]), (wlo[:, 0, cols], t["xnh"][:, 0, bass.ds(p * TOK2, TOK2)]),
                             (whi[:, 0, cols], t["xnl"][:, bass.ds(p * TOK2, TOK2)]),
                             (whi[:, 1, cols], t["xnh"][:, 1, bass.ds(p * TOK2, TOK2)]), (wlo[:, 1, cols], t["xnh"][:, 1, bass.ds(p * TOK2, TOK2)])]
                    for i, (w_, x_) in enumerate(terms):
                        last = pe.matmul(out, w_, x_, start=i == 0, stop=i == 4)
                    if j >= DJ - 1:
                        last.then_inc(q["u_mm" if j == DJ - 1 else "dh_mm"], 1)
                pe.wait_ge(q["r_lo"], p + 1 + FIRST)
                for j in range(DJ):
                    cols = slice(WZ + j * P, WZ + (j + 1) * P)
                    terms = [(whi[:, 0, cols], t["xnh"][:, 0, bass.ds(p * TOK2, TOK2)]), (wlo[:, 0, cols], t["xnh"][:, 0, bass.ds(p * TOK2, TOK2)]),
                             (whi[:, 0, cols], t["xnl"][:, bass.ds(p * TOK2, TOK2)]),
                             (whi[:, 1, cols], t["xnh"][:, 1, bass.ds(p * TOK2, TOK2)]), (wlo[:, 1, cols], t["xnh"][:, 1, bass.ds(p * TOK2, TOK2)])]
                    for i, (w_, x_) in enumerate(terms):
                        last = pe.matmul(psm[:, 2 + j, :], w_, x_, start=i == 0, stop=i == 4)
                last.then_inc(q["z_mm"], 1)
                pe.wait_ge(q["dh_lo"], p + 1 + FIRST)
                pe.wait_ge(q["sz"], p + 1 + FIRST)
                for j in range(DJ):
                    cols = slice(j * P, (j + 1) * P)
                    pe.matmul(psm[:, 2 + j, :], dhi[:, cols], dth[:, :], start=True, stop=False)
                    last = pe.matmul(psm[:, 2 + j, :], dlo[:, cols], dth[:, :], start=False, stop=True)
                last.then_inc(q["dt_mm"], 1)
                pe.wait_ge(q["u_ev"], p + 1 + FIRST)
                pe.wait_ge(q["dm"], p * DJ + DJ + FIRST)
                for i in range(NT2):
                    out = psm[:, 4 + i, 0:D]
                    for j in range(DJ):
                        tk = slice(i * P, (i + 1) * P)
                        pe.matmul(out, rTh[:, j, tk], ohi[:, j, :], start=j == 0, stop=False)
                        pe.matmul(out, rTh[:, j, tk], olo[:, j, :], start=False, stop=False)
                        last = pe.matmul(out, rTl[:, j, tk], ohi[:, j, :], start=False, stop=j == DJ - 1)
                last.then_inc(q["o_mm"], 1)


def scan_phase(nc, io, t):
    with ExitStack() as ctx:
        def sb(name, shape, dt=F32):
            return ctx.enter_context(nc.sbuf_tensor(name, shape, dt))

        def sem(name):
            return nc.alloc_semaphore("sc_" + name)

        tick = sem("tick")

        raw = sb("sc_raw", [P, 2, 2, 2, P])
        whi, wlo = sb("sc_whi", [P, 2, 2, 2, P], F32R), sb("sc_wlo", [P, 2, 2, 2, P], F32R)
        al = sb("sc_a", [P, DJ, NS])
        w_in = [sem(f"w_in{k}") for k in range(2)]
        R = 4
        dA, dB, hs, hc = (sb(f"sc_{n}", [P, R, TOK2]) for n in ("dA", "dB", "h", "hc"))
        psB = ctx.enter_context(nc.psum_tensor("sc_psB", [P, 4, 512], F32))
        psC = ctx.enter_context(nc.psum_tensor("sc_psC", [P, 4, 512], F32))
        q = {n: sem(n) for n in ("a_in", "a_neg", "whi", "wlo", "b_mm", "c_mm", "dA", "dB", "scan", "hc", "y")}
        block = ctx.enter_context(nc.Block())
        J2 = NS // 2

        for name, count in (("dB", PAIRS), ("hc", PAIRS), ("y", PAIRS), ("c_mm", PAIRS), ("scan", 2 * PAIRS), ("wlo", 1)):
            nc.gpsimd.sem_inc(q[name], count)

        @block.sync
        def _(sp):
            sp.dma_start(al[:, :, :], io["s_alog"]).then_inc(q["a_in"], 16)
            sp.dma_start(raw[:, 0, :, :, :], io["s_wbc"][0, :, :]).then_inc(w_in[0], 16)
            with sp.Fori(0, DJ * J2) as g:
                for k in range(2):
                    n = g * 2 + k
                    sp.wait_ge(q["wlo"], n + 1)
                    sp.dma_start(raw[:, (k + 1) % 2, :, :, :], io["s_wbc"][n + 1, :, :]).then_inc(w_in[(k + 1) % 2], 16)

        @block.scalar
        def _(act):
            act.wait_ge(q["a_in"], 16)
            act.activation(al[:, :, :], al[:, :, :], ACT.Exp).then_inc(q["a_neg"], 1)
            act.wait_ge(q["a_neg"], 2)
            act.wait_ge(w_in[0], 16)
            act.activation(whi[:, 0, :, :, :], raw[:, 0, :, :, :], ACT.Copy).then_inc(q["whi"], 1)
            with act.Fori(0, DJ) as j:
                with act.Fori(0, J2) as m:
                    g = j * J2 + m
                    for k in range(2):
                        n = g * 2 + k
                        for pr in range(PAIRS):
                            if pr == 2:
                                b = (k + 1) % 2
                                act.wait_ge(w_in[b], g * 16 + 16 * (k + 1))
                                act.wait_ge(q["c_mm"], n * PAIRS + PAIRS)
                                act.activation(whi[:, b, :, :, :], raw[:, b, :, :, :], ACT.Copy).then_inc(q["whi"], 1)
                            act.wait_ge(q["scan"], n * (2 * PAIRS) + 2 * pr + 2)
                            hold(act, tick)
                            act.activation(dA[:, pr, :], t["dt"][:, bass.ds(j, 1), pr * TOK2:(pr + 1) * TOK2].rearrange("p a n -> p (a n)"), ACT.Exp,
                                           scale=al[:, bass.ds(j, 1), bass.ds(m * 2 + k, 1)].rearrange("p a b -> p (a b)")).then_inc(q["dA"], 1)

        @block.gpsimd
        def _(pool):
            pool.wait_ge(q["whi"], 1)
            pool.tensor_tensor(wlo[:, 0, :, :, :], raw[:, 0, :, :, :], whi[:, 0, :, :, :], ALU.subtract).then_inc(q["wlo"], 1)
            with pool.Fori(0, DJ) as j:
                with pool.Fori(0, J2) as m:
                    g = j * J2 + m
                    for k in range(2):
                        n = g * 2 + k
                        for pr in range(PAIRS):
                            if pr == 1:
                                b = (k + 1) % 2
                                pool.wait_ge(q["whi"], n + 2)
                                pool.tensor_tensor(wlo[:, b, :, :, :], raw[:, b, :, :, :], whi[:, b, :, :, :], ALU.subtract).then_inc(q["wlo"], 1)
                            y = t["y"][:, bass.ds(j, 1), pr * TOK2:(pr + 1) * TOK2].rearrange("p a n -> p (a n)")
                            pool.wait_ge(q["hc"], n * PAIRS + pr + 1 + PAIRS)
                            pool.wait_ge(q["y"], n * PAIRS + pr + 1)
                            hold(pool, tick)
                            pool.tensor_tensor(y, y, hc[:, pr, :], ALU.add).then_inc(q["y"], 1)

        @block.vector
        def _(dve):
            dve.wait_ge(q["a_neg"], 1)
            dve.tensor_scalar(al[:, :, :], al[:, :, :], -1.0, None, ALU.mult).then_inc(q["a_neg"], 1)
            with dve.Fori(0, DJ) as j:
                with dve.Fori(0, J2) as m:
                    g = j * J2 + m

                    def input_(k, pr):
                        i = g * 8 + k * PAIRS + pr
                        dve.wait_ge(q["b_mm"], i + 1)
                        dve.tensor_tensor(dB[:, pr, :], psB[:, pr, :], t["dtu"][:, bass.ds(j, 1), pr * TOK2:(pr + 1) * TOK2].rearrange("p a n -> p (a n)"),
                                          ALU.mult).then_inc(q["dB"], 1)

                    def scan(k, pr):
                        i = g * 8 + k * PAIRS + pr
                        dve.wait_ge(q["dB"], i + 1 + PAIRS)
                        dve.wait_ge(q["dA"], i + 1)
                        for s_ in range(2):
                            c = slice(s_ * S, (s_ + 1) * S)
                            dve.tensor_tensor_scan(hs[:, pr, c], dA[:, pr, c], dB[:, pr, c], 0.0, ALU.mult, ALU.add).then_inc(q["scan"], 1)

                    def output(k, pr):
                        i = g * 8 + k * PAIRS + pr
                        dve.wait_ge(q["scan"], i * 2 + 2 + 2 * PAIRS)
                        dve.wait_ge(q["c_mm"], i + 1 + PAIRS)
                        dve.wait_ge(q["y"], i + 1)
                        dve.tensor_tensor(hc[:, pr, :], hs[:, pr, :], psC[:, pr, :], ALU.mult).then_inc(q["hc"], 1)

                    for i in range(2 * PAIRS + 2):
                        if i < 2 * PAIRS:
                            input_(*divmod(i, PAIRS))
                        if 0 <= i - 1 < 2 * PAIRS:
                            scan(*divmod(i - 1, PAIRS))
                        if i - 2 >= 0:
                            output(*divmod(i - 2, PAIRS))

        @block.tensor
        def _(pe):
            with pe.Fori(0, DJ * J2) as g:
                for k in range(2):
                    n = g * 2 + k
                    pe.wait_ge(q["wlo"], n + 2)
                    for pr in range(PAIRS):
                        cols = slice(pr * TOK2, (pr + 1) * TOK2)
                        pe.wait_ge(q["dB"], n * PAIRS + pr + 1)
                        five_passes(pe, psB[:, pr, :], whi[:, k, 0, :, :], wlo[:, k, 0, :, :], slice(0, P), t["xnh"], t["xnl"], cols).then_inc(q["b_mm"], 1)
                        pe.wait_ge(q["hc"], n * PAIRS + pr + 1)
                        five_passes(pe, psC[:, pr, :], whi[:, k, 1, :, :], wlo[:, k, 1, :, :], slice(0, P), t["xnh"], t["xnl"], cols).then_inc(q["c_mm"], 1)


def scan_output_phase(nc, io, t):
    with ExitStack() as ctx:
        def sb(name, shape, dt=F32):
            return ctx.enter_context(nc.sbuf_tensor(name, shape, dt))

        def sem(name):
            return nc.alloc_semaphore("so_" + name)

        oraw = sb("so_oraw", [P, DJ, D])
        ohi, olo = sb("so_ohi", [P, DJ, D], F32R), sb("so_olo", [P, DJ, D], F32R)
        par = sb("so_par", [P, NSPAR])
        ones = sb("so_ones", [P, 1])
        gm = [sb(f"so_g{x}", [P, DJ, TOK2]) for x in range(2)]
        sq = sb("so_sq", [P, DJ, TOK2])
        gh, gl = sb("so_gh", [P, DJ, TOK2], F32R), sb("so_gl", [P, DJ, TOK2], F32R)
        ms, rr, v, w = (sb(f"so_{n}", [P, NT2, 1]) for n in ("ms", "rr", "v", "w"))
        psq = ctx.enter_context(nc.psum_tensor("so_psq", [P, NT2], F32))
        pso = ctx.enter_context(nc.psum_tensor("so_pso", [P, 4, 512], F32))
        q = {n: sem(n) for n in ("o_in", "ohi", "olo", "one", "g", "sq", "hi", "lo", "ss", "ms", "rs", "mm", "res")}
        block = ctx.enter_context(nc.Block())

        @block.sync
        def _(sp):
            sp.dma_start(oraw[:, :, :], io["s_wout"]).then_inc(q["o_in"], 16)
            sp.dma_start(par[:, :], io["s_params"]).then_inc(q["o_in"], 16)

        @block.gpsimd
        def _(pool):
            pool.memset(ones[:, :], 1.0).then_inc(q["one"], 1)

        @block.scalar
        def _(act):
            act.wait_ge(q["o_in"], 32)
            act.activation(ohi[:, :, :], oraw[:, :, :], ACT.Copy).then_inc(q["ohi"], 1)
            for p in range(PAIRS):
                g = gm[p % 2]
                act.wait_ge(q["g"], p + 1)
                if p:
                    act.wait_ge(q["ss"], p)
                act.activation(sq[:, :, :], g[:, :, :], ACT.Square).then_inc(q["sq"], 1)
                if p:
                    act.wait_ge(q["mm"], p)
                for j in range(DJ):
                    act.activation(gh[:, j, :], g[:, j, :], ACT.Copy, scale=par[:, SP_NW + j:SP_NW + j + 1]).then_inc(q["hi"], 1)

        @block.vector
        def _(dve):
            dve.wait_ge(q["ohi"], 1)
            dve.tensor_tensor(olo[:, :, :], oraw[:, :, :], ohi[:, :, :], ALU.subtract).then_inc(q["olo"], 1)
            for p in range(PAIRS):
                g = gm[p % 2]
                if p >= 2:
                    dve.wait_ge(q["sq"], p - 1)
                    dve.wait_ge(q["hi"], DJ * (p - 1))
                cols = slice(p * TOK2, (p + 1) * TOK2)
                dve.scalar_tensor_tensor(g[:, :, :], t["y"][:, :, cols], 0.5, t["zs"][:, :, cols], ALU.mult, ALU.mult).then_inc(q["g"], 1)
                for j in range(DJ):
                    dve.wait_ge(q["hi"], DJ * p + j + 1)
                    dve.scalar_tensor_tensor(gl[:, j, :], g[:, j, :], par[:, SP_NW + j:SP_NW + j + 1], gh[:, j, :], ALU.mult, ALU.subtract).then_inc(q["lo"], 1)
                dve.wait_ge(q["ss"], p + 1)
                dve.tensor_scalar(ms[:, :, :], psq[:, :].unsqueeze(2), 1.0 / DI, None, ALU.mult).then_inc(q["ms"], 1)
                dve.wait_ge(q["ms"], p + 1)
                rsqrt_steps(dve, q["rs"], p * RSQRT_STEPS, ms[:, :, :], rr[:, :, :], v[:, :, :], w[:, :, :], eps=1e-6)
                dve.wait_ge(q["mm"], p + 1)
                for i in range(NT2):
                    r = t["res"][:, NT2 * p + i, :]
                    dve.scalar_tensor_tensor(r, pso[:, i, 0:D], rr[:, i, :], r, ALU.mult, ALU.add).then_inc(q["res"], 1)

        @block.tensor
        def _(pe):
            pe.wait_ge(q["olo"], 1)
            pe.wait_ge(q["one"], 1)
            for p in range(PAIRS):
                pe.wait_ge(q["sq"], p + 1)
                if p:
                    pe.wait_ge(q["ms"], p)
                    pe.wait_ge(q["res"], NT2 * p)
                for i in range(NT2):
                    for j in range(DJ):
                        last = pe.matmul(psq[:, i:i + 1], sq[:, j, i * P:(i + 1) * P], ones[:, :], start=j == 0, stop=j == DJ - 1)
                last.then_inc(q["ss"], 1)
                pe.wait_ge(q["lo"], DJ * (p + 1))
                for i in range(NT2):
                    tk = slice(i * P, (i + 1) * P)
                    for j in range(DJ):
                        pe.matmul(pso[:, i, 0:D], gh[:, j, tk], ohi[:, j, :], start=j == 0, stop=False)
                        pe.matmul(pso[:, i, 0:D], gh[:, j, tk], olo[:, j, :], start=False, stop=False)
                        last = pe.matmul(pso[:, i, 0:D], gl[:, j, tk], ohi[:, j, :], start=False, stop=j == DJ - 1)
                last.then_inc(q["mm"], 1)


def gate_phase(nc, io, t):
    with ExitStack() as ctx:
        def sb(name, shape, dt=F32):
            return ctx.enter_context(nc.sbuf_tensor(name, shape, dt))

        def sem(name):
            return nc.alloc_semaphore("ga_" + name)

        tick = sem("tick")

        E, NB = EXPERTS, B * QB
        x3 = sb("ga_x", [P, NB, 2 * P])
        st, mv = sb("ga_st", [P, NB, 6]), sb("ga_mv", [P, NB, 2])
        rs, v, w = (sb(f"ga_{n}", [P, NB, 1]) for n in ("rs", "v", "w"))
        xT = [sb(f"ga_xT{i}", [P, 2, TOK2]) for i in range(2)]
        graw = sb("ga_graw", [P, 2, E])
        ghi, glo = sb("ga_ghi", [P, 2, E], F32R), sb("ga_glo", [P, 2, E], F32R)
        gb, b2 = sb("ga_gb", [P, E]), sb("ga_b2", [E, D])
        lg, pr, c1, c2, rank = (sb(f"ga_{n}", [P, NB, E]) for n in ("lg", "pr", "c1", "c2", "rank"))
        m = sb("ga_m", [P, NB, 1])
        wT = sb("ga_wT", [E, NB, P])
        psx = ctx.enter_context(nc.psum_tensor("ga_psx", [P, 2, 2, 512], F32))
        psg = ctx.enter_context(nc.psum_tensor("ga_psg", [P, NB, E], F32))
        pst = ctx.enter_context(nc.psum_tensor("ga_pst", [E, 512], F32))
        psb = ctx.enter_context(nc.psum_tensor("ga_psb", [P, 2, 512], F32))
        q = {n: sem(n) for n in ("in", "ghi", "glo", "rank", "st", "ag", "rs", "x", "t_mm", "t_ev", "hi", "lo", "g_mm", "k", "exp",
                                 "wt_mm", "wt_ev", "b_mm", "res")}
        block = ctx.enter_context(nc.Block())

        @block.sync
        def _(sp):
            sp.dma_start(graw[:, :, :], io["g_w"]).then_inc(q["in"], 16)
            sp.dma_start(gb[:, :], io["g_b"].partition_broadcast(P)).then_inc(q["in"], 16)
            sp.dma_start(b2[:, :], io["g_b2"]).then_inc(q["in"], 16)

        @block.gpsimd
        def _(pool):
            for e in range(E):
                pool.memset(rank[:, :, e:e + 1], float(E - e)).then_inc(q["rank"], 1)

        @block.scalar
        def _(act):
            act.wait_ge(q["in"], 48)
            act.activation(ghi[:, :, :], graw[:, :, :], ACT.Copy).then_inc(q["ghi"], 1)
            for p in range(PAIRS):
                x = xT[p % 2]
                act.wait_ge(q["t_mm"], p + 1)
                if p >= 2:
                    act.wait_ge(q["lo"], 2 * (p - 1))
                act.activation(x[:, :, :], psx[:, p % 2, :, :], ACT.Copy).then_inc(q["t_ev"], 1)
                act.wait_ge(q["t_ev"], p + 1)
                act.activation(t["xnh"][:, :, p * TOK2:(p + 1) * TOK2], x[:, :, :], ACT.Copy).then_inc(q["hi"], 1)
            act.wait_ge(q["k"], 3)
            act.activation(pr[:, :, :], lg[:, :, :], ACT.Exp).then_inc(q["exp"], 1)
            for i in range(NB // 4):
                act.wait_ge(q["wt_mm"], i + 1)
                act.activation(wT[:, 4 * i:4 * i + 4, :], pst[:, :].rearrange("e (b n) -> e b n", b=4), ACT.Copy).then_inc(q["wt_ev"], 1)

        @block.vector
        def _(dve):
            dve.wait_ge(q["ghi"], 1)
            dve.tensor_tensor(glo[:, :, :], graw[:, :, :], ghi[:, :, :], ALU.subtract).then_inc(q["glo"], 1)
            layernorm_tokens(dve, tick, t["res"], x3, st, mv, rs[:, :, :], v[:, :, :], w[:, :, :], q["st"], q["ag"], q["rs"], q["x"], 0, NB)
            for p in range(PAIRS):
                x, cols = xT[p % 2], slice(p * TOK2, (p + 1) * TOK2)
                dve.wait_ge(q["hi"], p + 1)
                dve.tensor_tensor(t["xnl"][:, cols], x[:, 0, :], t["xnh"][:, 0, cols], ALU.subtract).then_inc(q["lo"], 1)
                s1 = t["xnh"][P // 2:, 1, cols]
                dve.tensor_tensor(s1, x[P // 2:, 1, :], s1, ALU.subtract).then_inc(q["lo"], 1)
            n = 0

            def step(instruction):
                nonlocal n
                n += 1
                instruction.then_inc(q["k"], 1)
                dve.wait_ge(q["k"], n)

            def over_e(x):
                return x.to_broadcast([P, NB, E])

            dve.wait_ge(q["g_mm"], 1)
            dve.wait_ge(q["in"], 48)
            step(dve.tensor_tensor(lg[:, :, :], psg[:, :, :], gb[:, :].unsqueeze(1).to_broadcast([P, NB, E]), ALU.add))
            step(dve.tensor_reduce(m[:, :, :], lg[:, :, :], AX, ALU.max))
            step(dve.tensor_tensor(lg[:, :, :], lg[:, :, :], over_e(m[:, :, :]), ALU.subtract))
            dve.wait_ge(q["exp"], 1)
            step(dve.tensor_reduce(m[:, :, :], pr[:, :, :], AX, ALU.add))
            step(dve.reciprocal(w[:, :, :], m[:, :, :]))
            step(dve.tensor_tensor(pr[:, :, :], pr[:, :, :], over_e(w[:, :, :]), ALU.mult))
            dve.wait_ge(q["rank"], E)
            for best in range(2):
                step(dve.tensor_reduce(m[:, :, :], pr[:, :, :], AX, ALU.max))
                step(dve.tensor_tensor(c1[:, :, :], pr[:, :, :], over_e(m[:, :, :]), ALU.is_equal))
                step(dve.tensor_tensor(c1[:, :, :], c1[:, :, :], rank[:, :, :], ALU.mult))
                step(dve.tensor_reduce(m[:, :, :], c1[:, :, :], AX, ALU.max))
                step(dve.tensor_tensor(c1[:, :, :], c1[:, :, :], over_e(m[:, :, :]), ALU.is_equal))
                dst = c2 if best == 0 else lg
                step(dve.tensor_tensor(dst[:, :, :], pr[:, :, :], c1[:, :, :], ALU.mult))
                if best == 0:
                    step(dve.scalar_tensor_tensor(c1[:, :, :], c1[:, :, :], 2.0, pr[:, :, :], ALU.mult, ALU.subtract))
                    step(dve.tensor_scalar(pr[:, :, :], c1[:, :, :], -1.0, None, ALU.mult))
                else:
                    step(dve.tensor_tensor(c2[:, :, :], c2[:, :, :], lg[:, :, :], ALU.add))
            step(dve.tensor_reduce(m[:, :, :], c2[:, :, :], AX, ALU.add))
            step(dve.reciprocal(w[:, :, :], m[:, :, :]))
            step(dve.tensor_tensor(t["tokw"][:, :, :], c2[:, :, :], over_e(w[:, :, :]), ALU.mult))
            for i in range(NB):
                dve.wait_ge(q["b_mm"], i + 1)
                r = t["res"][:, i, :]
                dve.tensor_tensor(r, psb[:, i % 2, 0:D], r, ALU.add).then_inc(q["res"], 1)

        @block.tensor
        def _(pe):
            pe.wait_ge(q["x"], NB + 1)
            for p in range(PAIRS):
                if p >= 2:
                    pe.wait_ge(q["t_ev"], p - 1)
                for c in range(2):
                    for i in range(NT2):
                        last = pe.transpose(psx[:, p % 2, c, i * P:(i + 1) * P], x3[:, NT2 * p + i, c * P:(c + 1) * P], t["ident"][:, :])
                last.then_inc(q["t_mm"], 1)
            pe.wait_ge(q["glo"], 1)
            for i in range(NB):
                pe.wait_ge(q["lo"], 2 * (i // NT2) + 2)
                last = five_passes(pe, psg[:, i, :], ghi, glo, slice(0, E), t["xnh"], t["xnl"], slice(i * P, (i + 1) * P), feature_major=False)
            last.then_inc(q["g_mm"], 1)
            pe.wait_ge(q["k"], 24)
            for i in range(NB // 4):
                if i:
                    pe.wait_ge(q["wt_ev"], i)
                for b in range(4):
                    last = pe.matmul(pst[:, b * P:(b + 1) * P], t["tokw"][:, 4 * i + b, :], t["ident"][:, :], start=True, stop=True)
                last.then_inc(q["wt_mm"], 1)
            pe.wait_ge(q["wt_ev"], NB // 4)
            for i in range(NB):
                if i >= 2:
                    pe.wait_ge(q["res"], i - 1)
                pe.matmul(psb[:, i % 2, 0:D], wT[:, i, :], b2[:, :], start=True, stop=True).then_inc(q["b_mm"], 1)


def expert_phase(nc, io, t, out):
    with ExitStack() as ctx:
        def sb(name, shape, dt=F32):
            return ctx.enter_context(nc.sbuf_tensor(name, shape, dt))

        def sem(name):
            return nc.alloc_semaphore("ex_" + name)

        tick = sem("tick")

        W1 = 2 * HID
        NW = W1 + HC * D
        raw = sb("ex_raw", [P, NW])
        whi, wlo = sb("ex_whi", [P, 2, NW], F32R), sb("ex_wlo", [P, 2, NW], F32R)
        b1 = sb("ex_b1", [P, EXPERTS, HC])
        b1e = sb("ex_b1e", [P, 2, HC])
        R = 4
        hr = sb("ex_hr", [P, R, TOK2])
        hh, hl = sb("ex_hh", [P, 2, HC, TOK2], F32R), sb("ex_hl", [P, 2, HC, TOK2], F32R)
        psh = ctx.enter_context(nc.psum_tensor("ex_psh", [P, R, 512], F32))
        psy = ctx.enter_context(nc.psum_tensor("ex_psy", [P, NT2, 512], F32))
        q = {n: sem(n) for n in ("b_in", "b1e", "w_in", "whi", "wlo", "h_mm", "relu", "hi", "lo", "y_mm", "y", "stored")}
        start_at_first(nc, list(q.values()))
        block = ctx.enter_context(nc.Block())
        per = PAIRS * HC

        def w1(w, k):
            return w[:, k, 0:W1].rearrange("p (s n) -> p s n", s=2)

        def w2(w, k, c):
            return w[:, k, W1 + c * D:W1 + (c + 1) * D]

        @block.sync
        def _(sp):
            sp.dma_start(b1[:, :, :], io["e_b1"]).then_inc(q["b_in"], 16)
            sp.dma_start(raw[:, :], io["e_w"][0, :, :]).then_inc(q["w_in"], 16)
            with sp.Fori(0, EXPERTS) as e:
                sp.wait_ge(q["wlo"], e + 1 + FIRST)
                hold(sp, tick)
                sp.dma_start(raw[:, :], io["e_w"][e + 1, :, :]).then_inc(q["w_in"], 16)
            sp.wait_ge(q["y"], EXPERTS * B * QB + FIRST)
            sp.dma_start(out.rearrange("b (k p) d -> p (b k) d", p=P), t["res"][:, :, :]).then_inc(q["stored"], 16)
            sp.wait_ge(q["stored"], 16 + FIRST)

        @block.scalar
        def _(act):
            act.wait_ge(q["b_in"], 16 + FIRST)

            act.wait_ge(q["w_in"], 16 + FIRST)
            act.activation(whi[:, 0, :], raw[:, :], ACT.Copy).then_inc(q["whi"], 1)
            with act.Fori(0, EXPERTS // 2) as e2:
                for k in range(2):
                    e = e2 * 2 + k
                    act.wait_ge(q["relu"], e * per + FIRST)
                    hold(act, tick)
                    act.activation(b1e[:, k, :], b1[:, bass.ds(e, 1), :].rearrange("p a c -> p (a c)"), ACT.Copy).then_inc(q["b1e"], 1)
                    act.wait_ge(q["b1e"], e + 1 + FIRST)
                    for p in range(PAIRS):
                        if p == 1:
                            act.wait_ge(q["w_in"], e * 16 + 32 + FIRST)
                            act.wait_ge(q["y_mm"], e * PAIRS + FIRST)
                            act.activation(whi[:, 1 - k, :], raw[:, :], ACT.Copy).then_inc(q["whi"], 1)
                        for c in range(HC):
                            i = e * per + p * HC + c
                            act.wait_ge(q["h_mm"], i + 1 + FIRST)
                            act.wait_ge(q["lo"], e2 * (2 * per) + max(k * per + p * HC + c + 1 - R, 0) + FIRST)
                            act.activation(hr[:, (p * HC + c) % R, :], psh[:, (p * HC + c) % R, :], ACT.Relu,
                                           bias=b1e[:, k, c:c + 1]).then_inc(q["relu"], 1)

        @block.gpsimd
        def _(pool):
            with pool.Fori(0, EXPERTS // 2) as e2:
                for k in range(2):
                    pool.wait_ge(q["whi"], e2 * 2 + k + 2 + FIRST)
                    pool.tensor_tensor(wlo[:, 1 - k, :], raw[:, :], whi[:, 1 - k, :], ALU.subtract).then_inc(q["wlo"], 1)

        @block.vector
        def _(dve):
            dve.wait_ge(q["whi"], 1 + FIRST)
            dve.tensor_tensor(wlo[:, 0, :], raw[:, :], whi[:, 0, :], ALU.subtract).then_inc(q["wlo"], 1)
            with dve.Fori(0, EXPERTS // 2) as e2:
                for k in range(2):
                    e = e2 * 2 + k

                    def weigh(p):
                        dve.wait_ge(q["y_mm"], e * PAIRS + p + 1 + FIRST)
                        for i in range(NT2):
                            r = t["res"][:, NT2 * p + i, :]
                            dve.scalar_tensor_tensor(r, psy[:, i, 0:D], t["tokw"][:, NT2 * p + i, bass.ds(e, 1)], r, ALU.mult, ALU.add).then_inc(q["y"], 1)

                    for p in range(PAIRS):
                        for c in range(HC):
                            i = e * per + p * HC + c
                            src = hr[:, (p * HC + c) % R, :]
                            if c == 0:
                                n = k * PAIRS + p
                                dve.wait_ge(q["y_mm"], e2 * (2 * PAIRS) + max(n - 1, 0) + FIRST)
                            dve.wait_ge(q["relu"], i + 1 + FIRST)
                            dve.tensor_copy(hh[:, p % 2, c, :], src).then_inc(q["hi"], 1)
                            dve.wait_ge(q["hi"], i + 1 + FIRST)
                            dve.tensor_tensor(hl[:, p % 2, c, :], src, hh[:, p % 2, c, :], ALU.subtract).then_inc(q["lo"], 1)
                        if p:
                            weigh(p - 1)
                    weigh(PAIRS - 1)

        @block.tensor
        def _(pe):
            with pe.Fori(0, EXPERTS // 2) as e2:
                for k in range(2):
                    e = e2 * 2 + k
                    pe.wait_ge(q["wlo"], e + 1 + FIRST)

                    def hidden(p):
                        cols = slice(p * TOK2, (p + 1) * TOK2)
                        for c in range(HC):
                            pe.wait_ge(q["relu"], e2 * (2 * per) + max(k * per + p * HC + c + 1 - R, 0) + FIRST)
                            five_passes(pe, psh[:, (p * HC + c) % R, :], w1(whi, k), w1(wlo, k), slice(c * P, (c + 1) * P),
                                        t["xnh"], t["xnl"], cols).then_inc(q["h_mm"], 1)

                    def output(p):
                        pe.wait_ge(q["lo"], e * per + (p + 1) * HC + FIRST)
                        pe.wait_ge(q["y"], (e * PAIRS + p) * NT2 + FIRST)
                        for i in range(NT2):
                            tk = slice(i * P, (i + 1) * P)
                            for c in range(HC):
                                pe.matmul(psy[:, i, 0:D], hh[:, p % 2, c, tk], w2(whi, k, c), start=c == 0, stop=False)
                                pe.matmul(psy[:, i, 0:D], hh[:, p % 2, c, tk], w2(wlo, k, c), start=False, stop=False)
                                last = pe.matmul(psy[:, i, 0:D], hl[:, p % 2, c, tk], w2(whi, k, c), start=False, stop=c == HC - 1)
                        last.then_inc(q["y_mm"], 1)

                    for p in range(PAIRS):
                        hidden(p)
                        if p:
                            output(p - 1)
                    output(PAIRS - 1)


def host_layout(inp):
    def a(n):
        return np.asarray(inp[n])

    def fold(w):
        return np.stack([w[0:P], np.concatenate([w[P:], w[P:]])], axis=1)

    def fold_b(v):
        return fold(v[:, None])[:, :, 0]

    def by_dim(w):
        c = w.reshape(w.shape[:-1] + (HPC, 2, HD))
        return np.moveaxis(c, -3, -1).reshape(w.shape)

    out = {}
    out["ids"] = np.ascontiguousarray(a("x").reshape(B * QB, P).T)
    out["pos_ids"] = np.ascontiguousarray(a("pos_S").reshape(QB, P).T)
    mask = a("mask_BS_f1_0")
    out["mask_rows"] = mask
    out["mask_cols"] = np.ascontiguousarray(mask.reshape(B * QB, P).T)
    out["tok_emb"], out["pos_emb"] = a("L0_tok_tok_emb"), a("L0_tok_pos_emb")
    ws, ps, rs = [], [], []
    pb = a("L0_tok_c_proj_b")
    out["proj_b0"] = pb[0]
    for l in range(LAYERS):
        w = np.concatenate([by_dim(a("L0_tok_c_attn_w")[l][:, 0:D]), by_dim(a("L0_tok_c_attn_w")[l][:, D:2 * D]),
                            a("L0_tok_c_attn_w")[l][:, 2 * D:], a("L0_tok_c_proj_w")[l], a("L0_tok_c_fc_w")[l]], axis=1)
        m = a("L0_tok_mlp_proj_w")[l].reshape(HC, P, D).transpose(1, 0, 2)
        ws.append(np.concatenate([fold(w).reshape(P, -1), m.reshape(P, -1)], axis=1))
        par = np.zeros((P, NPAR), np.float32)
        bqkv = a("L0_tok_c_attn_b")[l]
        for c in range(2):
            par[0:CUT, PQ + c] = by_dim(bqkv[0:D])[c * CUT:(c + 1) * CUT]
            par[0:CUT, PK + c] = by_dim(bqkv[D:2 * D])[c * CUT:(c + 1) * CUT]
        par[:, PV_:PV_ + 2] = fold_b(bqkv[2 * D:])
        par[:, PL1W:PL1W + 2] = fold_b(a("L0_tok_ln1_w")[l])
        par[:, PL1B:PL1B + 2] = fold_b(a("L0_tok_ln1_b")[l])
        par[:, PL2W:PL2W + 2] = fold_b(a("L0_tok_ln2_w")[l])
        par[:, PL2B:PL2B + 2] = fold_b(a("L0_tok_ln2_b")[l])
        par[:, PFC:] = a("L0_tok_c_fc_b")[l].reshape(HC, P).T
        ps.append(par)
        nxt = pb[l + 1] if l + 1 < LAYERS else np.zeros(D, np.float32)
        rs.append(np.stack([a("L0_tok_ln1_w")[l], a("L0_tok_ln1_b")[l], a("L0_tok_mlp_proj_b")[l],
                            a("L0_tok_ln2_w")[l], a("L0_tok_ln2_b")[l], nxt]))
    out["weights"] = np.stack(ws)
    out["params"] = np.ascontiguousarray(np.stack(ps).transpose(1, 0, 2))
    out["rows"] = np.stack(rs)
    w_in = a("L0_attn_W_in")
    rank = np.zeros((D, P), np.float32)
    rank[:, 0:RANK] = w_in[2 * DI:2 * DI + RANK].T
    rank[:, P // 2:P // 2 + RANK] = w_in[2 * DI:2 * DI + RANK].T
    out["s_w"] = fold(np.concatenate([w_in[0:2 * DI].T, rank], axis=1))
    out["s_wres"] = fold(a("L0_attn_W_res").T)
    out["s_wout"] = a("L0_attn_W_out").T.reshape(DJ, P, D).transpose(1, 0, 2)
    wdt = np.zeros((P, DI), np.float32)
    wdt[0:RANK] = a("L0_attn_W_dt").T
    wdt[P // 2:P // 2 + RANK] = a("L0_attn_W_dt").T
    out["s_wdt"] = wdt

    def chan(v):
        return v.reshape(DJ, P).T

    cw = a("L0_attn_conv_w").reshape(DJ, P, KCONV).transpose(1, 0, 2).reshape(P, DJ * KCONV)
    out["s_params"] = np.concatenate([chan(a("L0_attn_" + n)) for n in ("dt_bias", "conv_b", "Dskip", "norm_w")] + [cw], axis=1)
    out["s_ln"] = np.concatenate([fold_b(a("L0_attn_ln_w")), fold_b(a("L0_attn_ln_b"))], axis=1)
    out["s_alog"] = a("L0_attn_A_log").reshape(DJ, P, NS).transpose(1, 0, 2)
    bc = w_in[2 * DI + RANK:].reshape(2, DJ, P, NS, D)
    bc = bc.transpose(1, 3, 4, 0, 2).reshape(DJ * NS, D, 2, P)
    out["s_wbc"] = np.concatenate([bc[:, 0:P], np.zeros_like(bc[:, 0:P])], axis=2).reshape(DJ * NS, P, 2, 2, P)
    out["s_wbc"][:, :, 0, 0], out["s_wbc"][:, :, 1, 0] = bc[:, 0:P, 0], bc[:, 0:P, 1]
    out["s_wbc"][:, 0:P // 2, :, 1], out["s_wbc"][:, P // 2:, :, 1] = bc[:, P:], bc[:, P:]
    out["s_wbc"] = np.concatenate([out["s_wbc"].reshape(DJ * NS, P, 4 * P), np.zeros((1, P, 4 * P), np.float32)])
    out["g_w"] = fold(a("L0_ffn_gate_w").T)
    out["g_b"], out["g_b2"] = a("L0_ffn_gate_b"), a("L0_ffn_b2")
    out["e_b1"] = a("L0_ffn_b1").reshape(EXPERTS, HC, P).transpose(2, 0, 1)
    out["e_w"] = np.stack([np.concatenate([
        fold(a("L0_ffn_w1")[e].T).reshape(P, -1),
        a("L0_ffn_w2")[e].T.reshape(HC, P, D).transpose(1, 0, 2).reshape(P, -1)], axis=1) for e in range(EXPERTS)])
    out["e_w"] = np.concatenate([out["e_w"], np.zeros_like(out["e_w"][0:1])])
    return {k: np.ascontiguousarray(v) for k, v in out.items()}


def shared(nc, ctx):
    def sb(name, shape, dt=F32):
        return ctx.enter_context(nc.sbuf_tensor(name, shape, dt))

    return {
        "ident": sb("ident", [P, P]),
        "ident_b": sb("ident_b", [P, P], BF16),
        "trib": sb("trib", [P, P], BF16),
        "ext": sb("ext_cols", [P, B * QB]),
        "e10": sb("e10", [P, B * QB]),
        "res": sb("res", [P, B * QB, D]),
        "m1_dram": nc.dram_tensor("m1_dram", (B, P, 3 * P), F32, kind="Internal").ap(),
        "rows_dram": nc.dram_tensor("rows_dram", (LAYERS, 4, D), F32, kind="Internal").ap(),
        "wt_dram": nc.dram_tensor("wt_dram", (B, P, 3 * P), F32, kind="Internal").ap(),
    }


def tower_kernel(nc, io, out):
    with ExitStack() as ctx:
        t = shared(nc, ctx)

        def phase(build, *args):
            with nc.cleanup_on_exit():
                build(nc, io, t, *args)

        with ExitStack() as c1:
            t["hst"] = c1.enter_context(nc.sbuf_tensor("hst", [P, B, 2, S], F32))
            phase(setup_phase, LAYERS)
            phase(tower_phase, LAYERS)
        t["xnh"] = ctx.enter_context(nc.sbuf_tensor("xnh", [P, 2, B * S], F32R))
        t["xnl"] = ctx.enter_context(nc.sbuf_tensor("xnl", [P, B * S], F32R))
        t["tokw"] = ctx.enter_context(nc.sbuf_tensor("tokw", [P, B * QB, EXPERTS], F32))
        with ExitStack() as c2:
            for n in ("dt", "dtu", "zs", "y"):
                t[n] = c2.enter_context(nc.sbuf_tensor("sc_" + n + "_all", [P, DJ, B * S], F32))
            phase(scan_input_phase)
            phase(scan_phase)
            phase(scan_output_phase)
        phase(gate_phase)
        phase(expert_phase, out)


def kernel(**inputs):
    import concourse.bacc as _bacc
    from concourse.bass_utils import run_bass_kernel_spmd as _run

    arrays = host_layout(inputs)
    nc = _bacc.Bacc("TRN2", target_bir_lowering=False, num_devices=1)
    io = {k: nc.dram_tensor("in_" + k, v.shape, mybir.dt.from_np(v.dtype), kind="ExternalInput").ap() for k, v in arrays.items()}
    out = nc.dram_tensor("out_0_dram", (B, S, D), F32, kind="ExternalOutput").ap()
    tower_kernel(nc, io, out)
    r = _run(nc, [{"in_" + k: v for k, v in arrays.items()}], core_ids=[0])
    return r.results[0]["out_0_dram"]
```
